# Optimizing a Trainium2 kernel written in Bass

```python
import numpy as np
import jax
import jax.numpy as jnp

def _softmax(x, axis=-1):
    return jax.nn.softmax(x, axis=axis)
def _gelu(x):
    return jax.nn.gelu(x, approximate=True)
def _silu(x):
    return jax.nn.silu(x)
def _sigmoid(x):
    return jax.nn.sigmoid(x)
def _layernorm(x, axis=-1, eps=1e-5):
    m = jnp.mean(x, axis=axis, keepdims=True)
    v = jnp.var(x, axis=axis, keepdims=True)
    return (x - m) / jnp.sqrt(v + eps)
def _scatter_add(tgt, idx, src, axis=0):
    return tgt.at[idx].add(src)
def _segment_sum(src, seg, n):
    return jax.ops.segment_sum(src, seg, n)

kernel_name = 'mk_conv_seq_d4_conv_nchw512_2d55c5'

def setup_inputs(seed: int = 0):
    np.random.seed(seed)
    _w = jnp.asarray
    def _rec_inputs():
        import jax
        import jax.numpy as jnp
        _gk = jax.random.key(seed)
        x = -0.000929 + 1 * jax.random.normal(jax.random.fold_in(_gk, 1), (2, 512, 32, 32), jnp.float32)
        return x
    x = _rec_inputs()
    def _L0_conv_setup():
        import jax, jax.numpy as jnp
        import numpy as np
        B, C, H, W = (2, 512, 32, 32)
        HEADS = 8
        GROUPS = 8
        DH = 64
        DF = 4
        OFF_SCALE = 4.0
        EPS = 1e-05

        def _bn(t, gamma, beta):
            s = gamma / jnp.sqrt(1.0 + EPS)
            return t * s[None, :, None, None] + beta[None, :, None, None]

        def _gconv1x1(t, w):
            b, c, h, ww = t.shape
            o = jnp.einsum('bgci,goc->bgoi', t.reshape(b, GROUPS, c // GROUPS, h * ww), w)
            return o.reshape(b, GROUPS * w.shape[1], h, ww)

        def _grid_sample(img, grid):
            N, Ci, Hi, Wi = img.shape
            gx = (grid[..., 0] + 1.0) * (Wi / 2.0) - 0.5
            gy = (grid[..., 1] + 1.0) * (Hi / 2.0) - 0.5
            x0 = jnp.floor(gx)
            y0 = jnp.floor(gy)
            wx = gx - x0
            wy = gy - y0

            def gather(im, ix, iy):
                valid = (ix >= 0) & (ix < Wi) & (iy >= 0) & (iy < Hi)
                ixc = jnp.clip(ix, 0, Wi - 1).astype(jnp.int32)
                iyc = jnp.clip(iy, 0, Hi - 1).astype(jnp.int32)
                return im[:, iyc, ixc] * valid[None].astype(im.dtype)

            def sample_one(im, x0, y0, wx, wy):
                v00 = gather(im, x0, y0)
                v01 = gather(im, x0 + 1, y0)
                v10 = gather(im, x0, y0 + 1)
                v11 = gather(im, x0 + 1, y0 + 1)
                wx = wx[None]
                wy = wy[None]
                return v00 * (1 - wx) * (1 - wy) + v01 * wx * (1 - wy) + v10 * (1 - wx) * wy + v11 * wx * wy
            return jax.vmap(sample_one)(img, x0, y0, wx, wy)

        def _forward(x, bn1_g, bn1_b, bn2_g, bn2_b, qw, kw, vw, out_w, out_b, off_dw_w, off_dw_b, off_pw_w, cpb_w1, cpb_b1, cpb_w2, cpb_b2, cpb_w3, cpb_b3, mlp_w1, mlp_b1, mlp_w2, mlp_b2):
            b = x.shape[0]
            xn = _bn(x, bn1_g, bn1_b)
            q = _gconv1x1(xn, qw)
            qg = q.reshape(b * GROUPS, DH, H, W)
            off = jax.lax.conv_general_dilated(qg, off_dw_w, (DF, DF), ((1, 1), (1, 1)), dimension_numbers=('NCHW', 'OIHW', 'NCHW'), feature_group_count=DH)
            off = jax.nn.gelu(off + off_dw_b[None, :, None, None], approximate=False)
            off = jnp.tanh(jnp.einsum('bchw,oc->bohw', off, off_pw_w)) * OFF_SCALE
            Hd, Wd = (off.shape[-2], off.shape[-1])
            gy, gx = jnp.meshgrid(jnp.arange(Hd, dtype=x.dtype), jnp.arange(Wd, dtype=x.dtype), indexing='ij')
            vx = gx[None] + off[:, 0]
            vy = gy[None] + off[:, 1]
            nx = 2.0 * vx / max(Hd - 1, 1) - 1.0
            ny = 2.0 * vy / max(Wd - 1, 1) - 1.0
            vgrid_scaled = jnp.stack((nx, ny), axis=-1)
            kv = _grid_sample(xn.reshape(b * GROUPS, DH, H, W), vgrid_scaled)
            kv = kv.reshape(b, GROUPS * DH, Hd, Wd)
            k = _gconv1x1(kv, kw)
            v = _gconv1x1(kv, vw)
            scale = DH ** (-0.5)
            qh = q.reshape(b, HEADS, DH, H * W).transpose(0, 1, 3, 2) * scale
            kh = k.reshape(b, HEADS, DH, Hd * Wd).transpose(0, 1, 3, 2)
            vh = v.reshape(b, HEADS, DH, Hd * Wd).transpose(0, 1, 3, 2)
            qgy, qgx = jnp.meshgrid(jnp.arange(H, dtype=x.dtype), jnp.arange(W, dtype=x.dtype), indexing='ij')
            grid_q = jnp.stack((2.0 * qgx / max(H - 1, 1) - 1.0, 2.0 * qgy / max(W - 1, 1) - 1.0), axis=-1).reshape(1, H * W, 2)
            grid_kv = vgrid_scaled.reshape(b * GROUPS, Hd * Wd, 2)
            pos = grid_q[:, :, None, :] - grid_kv[:, None, :, :]
            bias = jnp.sign(pos) * jnp.log1p(jnp.abs(pos))
            bias = jax.nn.relu(bias @ cpb_w1 + cpb_b1)
            bias = jax.nn.relu(bias @ cpb_w2 + cpb_b2)
            bias = (bias @ cpb_w3 + cpb_b3).reshape(b, GROUPS, H * W, Hd * Wd)
            sim = jnp.einsum('bhid,bhjd->bhij', qh, kh) + bias
            attn = jax.nn.softmax(sim, axis=-1)
            out = jnp.einsum('bhij,bhjd->bhid', attn, vh)
            out = out.transpose(0, 1, 3, 2).reshape(b, HEADS * DH, H, W)
            out = jnp.einsum('bchw,oc->bohw', out, out_w) + out_b[None, :, None, None]
            x = x + out
            xn2 = _bn(x, bn2_g, bn2_b)
            h1 = jax.nn.gelu(jnp.einsum('bchw,oc->bohw', xn2, mlp_w1) + mlp_b1[None, :, None, None], approximate=False)
            return x + jnp.einsum('bchw,oc->bohw', h1, mlp_w2) + mlp_b2[None, :, None, None]
        ks = jax.random.split(jax.random.key(seed), 16)
        w = lambda k, shape: jax.random.normal(k, shape, dtype=jnp.float32) * 0.02
        return {'x': jax.random.normal(ks[0], (B, C, H, W), dtype=jnp.float32), 'bn1_g': jnp.ones((C,), jnp.float32), 'bn1_b': jnp.zeros((C,), jnp.float32), 'bn2_g': jnp.ones((C,), jnp.float32), 'bn2_b': jnp.zeros((C,), jnp.float32), 'qw': w(ks[1], (GROUPS, DH, C // GROUPS)), 'kw': w(ks[2], (GROUPS, DH, C // GROUPS)), 'vw': w(ks[3], (GROUPS, DH, C // GROUPS)), 'out_w': w(ks[4], (C, HEADS * DH)), 'out_b': jnp.zeros((C,), jnp.float32), 'off_dw_w': w(ks[5], (DH, 1, 6, 6)), 'off_dw_b': jnp.zeros((DH,), jnp.float32), 'off_pw_w': w(ks[6], (2, DH)), 'cpb_w1': w(ks[7], (2, 128)), 'cpb_b1': jnp.zeros((128,), jnp.float32), 'cpb_w2': w(ks[8], (128, 128)), 'cpb_b2': jnp.zeros((128,), jnp.float32), 'cpb_w3': w(ks[9], (128, 1)), 'cpb_b3': jnp.zeros((1,), jnp.float32), 'mlp_w1': w(ks[10], (4 * C, C)), 'mlp_b1': jnp.zeros((4 * C,), jnp.float32), 'mlp_w2': w(ks[11], (C, 4 * C)), 'mlp_b2': jnp.zeros((C,), jnp.float32)}
    _L0_conv_all = _L0_conv_setup()
    _L0_conv_in = {k: v for k, v in _L0_conv_all.items() if k in ('bn1_g', 'bn1_b', 'bn2_g', 'bn2_b', 'qw', 'kw', 'vw', 'out_w', 'out_b', 'off_dw_w', 'off_dw_b', 'off_pw_w', 'cpb_w1', 'cpb_b1', 'cpb_w2', 'cpb_b2', 'cpb_w3', 'cpb_b3', 'mlp_w1', 'mlp_b1', 'mlp_w2', 'mlp_b2', )}
    del _L0_conv_all

    def _L1_conv_setup():
        import jax, jax.numpy as jnp
        import numpy as np
        B, C, H, W = (8, 512, 32, 32)
        HEADS = 8
        EPS = 1e-05

        def conv1x1(X, Wt, b):
            return jnp.einsum('co,bohw->bchw', Wt, X) + b[None, :, None, None]
        key = jax.random.key(seed)
        ks = jax.random.split(key, 9)
        s = 0.02
        f32 = jnp.float32
        return {'X': jax.random.normal(ks[0], (B, C, H, W), f32), 'Wq': jax.random.normal(ks[1], (C, C), f32) * s, 'bq': jnp.zeros((C,), f32), 'Wk': jax.random.normal(ks[2], (C, C), f32) * s, 'bk': jnp.zeros((C,), f32), 'Wv': jax.random.normal(ks[3], (C, C), f32) * s, 'bv': jnp.zeros((C,), f32), 'Wo': jax.random.normal(ks[4], (C, C), f32) * s, 'bo': jnp.zeros((C,), f32), 'gamma': jnp.ones((C,), f32), 'beta': jnp.zeros((C,), f32)}
    _L1_conv_all = _L1_conv_setup()
    _L1_conv_in = {k: v for k, v in _L1_conv_all.items() if k in ('Wq', 'bq', 'Wk', 'bk', 'Wv', 'bv', 'Wo', 'bo', 'gamma', 'beta', )}
    del _L1_conv_all

    def _L2_conv_setup():
        import jax, jax.numpy as jnp
        import numpy as np
        EPS = 1e-05

        def conv1x1(x, w, b):
            return jnp.einsum('bchw,oc->bohw', x, w) + b[None, :, None, None]

        def bn_eval(x, gamma, beta, mean, var):
            inv = gamma / jnp.sqrt(var + EPS)
            return x * inv[None, :, None, None] + (beta - mean * inv)[None, :, None, None]
        key = jax.random.key(seed)
        ks = jax.random.split(key, 20)
        B, C, H, W = (4, 512, 64, 64)
        mid = C // 4
        s_in = 1.0 / np.sqrt(C)
        s_mid = 1.0 / np.sqrt(mid)
        inp = {'x': jax.random.normal(ks[0], (B, C, H, W), jnp.float32), 'wf': jax.random.normal(ks[1], (mid, C), jnp.float32) * s_in, 'bf': jnp.zeros((mid,), jnp.float32), 'gf': jnp.ones((mid,), jnp.float32), 'betaf': jnp.zeros((mid,), jnp.float32), 'mf': jax.random.normal(ks[2], (mid,), jnp.float32) * 0.1, 'vf': jax.random.uniform(ks[3], (mid,), jnp.float32) + 0.5, 'wg': jax.random.normal(ks[4], (mid, C), jnp.float32) * s_in, 'bg': jnp.zeros((mid,), jnp.float32), 'gg': jnp.ones((mid,), jnp.float32), 'betag': jnp.zeros((mid,), jnp.float32), 'mg': jax.random.normal(ks[5], (mid,), jnp.float32) * 0.1, 'vg': jax.random.uniform(ks[6], (mid,), jnp.float32) + 0.5, 'wh': jax.random.normal(ks[7], (mid, C), jnp.float32) * s_in, 'bh': jnp.zeros((mid,), jnp.float32), 'wv': jax.random.normal(ks[8], (C, mid), jnp.float32) * s_mid, 'bv': jnp.zeros((C,), jnp.float32)}
        return inp
    _L2_conv_all = _L2_conv_setup()
    _L2_conv_in = {k: v for k, v in _L2_conv_all.items() if k in ('wf', 'bf', 'gf', 'betaf', 'mf', 'vf', 'wg', 'bg', 'gg', 'betag', 'mg', 'vg', 'wh', 'bh', 'wv', 'bv', )}
    del _L2_conv_all

    def _L3_conv_setup():
        import jax, jax.numpy as jnp
        import numpy as np
        B, C, H, W = (8, 512, 64, 32)
        SE_MID = C // 16
        BN_EPS = 1e-05

        def conv1x1(x, w, b):
            return jnp.einsum('bchw,oc->bohw', x, w) + b[None, :, None, None]
        key = jax.random.key(seed)
        ks = jax.random.split(key, 17)
        s = 0.05
        return {'x': jax.random.normal(ks[0], (B, C, H, W), jnp.float32), 'g_w': jax.random.normal(ks[1], (1, C), jnp.float32) * s, 'g_b': jax.random.normal(ks[2], (1,), jnp.float32) * s, 'theta_w': jax.random.normal(ks[3], (1, C), jnp.float32) * s, 'theta_b': jax.random.normal(ks[4], (1,), jnp.float32) * s, 'phi_w': jax.random.normal(ks[5], (1, C), jnp.float32) * s, 'phi_b': jax.random.normal(ks[6], (1,), jnp.float32) * s, 'W_w': jax.random.normal(ks[7], (C, 1), jnp.float32) * s, 'W_b': jax.random.normal(ks[8], (C,), jnp.float32) * s, 'bn_gamma': jax.random.normal(ks[9], (C,), jnp.float32) * s + 1.0, 'bn_beta': jax.random.normal(ks[10], (C,), jnp.float32) * s, 'bn_mean': jax.random.normal(ks[11], (C,), jnp.float32) * s, 'bn_var': jax.random.uniform(ks[12], (C,), jnp.float32, 0.5, 1.5), 'se1_w': jax.random.normal(ks[13], (SE_MID, C), jnp.float32) * s, 'se1_b': jnp.zeros((SE_MID,), jnp.float32), 'se2_w': jax.random.normal(ks[14], (C, SE_MID), jnp.float32) * s, 'se2_b': jnp.zeros((C,), jnp.float32)}
    _L3_conv_all = _L3_conv_setup()
    _L3_conv_in = {k: v for k, v in _L3_conv_all.items() if k in ('g_w', 'g_b', 'theta_w', 'theta_b', 'phi_w', 'phi_b', 'W_w', 'W_b', 'bn_gamma', 'bn_beta', 'bn_mean', 'bn_var', 'se1_w', 'se1_b', 'se2_w', 'se2_b', )}
    del _L3_conv_all

    return {
        "x": x,
        "L0_conv_bn1_g": _L0_conv_in["bn1_g"],
        "L0_conv_bn1_b": _L0_conv_in["bn1_b"],
        "L0_conv_bn2_g": _L0_conv_in["bn2_g"],
        "L0_conv_bn2_b": _L0_conv_in["bn2_b"],
        "L0_conv_qw": _L0_conv_in["qw"],
        "L0_conv_kw": _L0_conv_in["kw"],
        "L0_conv_vw": _L0_conv_in["vw"],
        "L0_conv_out_w": _L0_conv_in["out_w"],
        "L0_conv_out_b": _L0_conv_in["out_b"],
        "L0_conv_off_dw_w": _L0_conv_in["off_dw_w"],
        "L0_conv_off_dw_b": _L0_conv_in["off_dw_b"],
        "L0_conv_off_pw_w": _L0_conv_in["off_pw_w"],
        "L0_conv_cpb_w1": _L0_conv_in["cpb_w1"],
        "L0_conv_cpb_b1": _L0_conv_in["cpb_b1"],
        "L0_conv_cpb_w2": _L0_conv_in["cpb_w2"],
        "L0_conv_cpb_b2": _L0_conv_in["cpb_b2"],
        "L0_conv_cpb_w3": _L0_conv_in["cpb_w3"],
        "L0_conv_cpb_b3": _L0_conv_in["cpb_b3"],
        "L0_conv_mlp_w1": _L0_conv_in["mlp_w1"],
        "L0_conv_mlp_b1": _L0_conv_in["mlp_b1"],
        "L0_conv_mlp_w2": _L0_conv_in["mlp_w2"],
        "L0_conv_mlp_b2": _L0_conv_in["mlp_b2"],
        "L1_conv_Wq": _L1_conv_in["Wq"],
        "L1_conv_bq": _L1_conv_in["bq"],
        "L1_conv_Wk": _L1_conv_in["Wk"],
        "L1_conv_bk": _L1_conv_in["bk"],
        "L1_conv_Wv": _L1_conv_in["Wv"],
        "L1_conv_bv": _L1_conv_in["bv"],
        "L1_conv_Wo": _L1_conv_in["Wo"],
        "L1_conv_bo": _L1_conv_in["bo"],
        "L1_conv_gamma": _L1_conv_in["gamma"],
        "L1_conv_beta": _L1_conv_in["beta"],
        "L2_conv_wf": _L2_conv_in["wf"],
        "L2_conv_bf": _L2_conv_in["bf"],
        "L2_conv_gf": _L2_conv_in["gf"],
        "L2_conv_betaf": _L2_conv_in["betaf"],
        "L2_conv_mf": _L2_conv_in["mf"],
        "L2_conv_vf": _L2_conv_in["vf"],
        "L2_conv_wg": _L2_conv_in["wg"],
        "L2_conv_bg": _L2_conv_in["bg"],
        "L2_conv_gg": _L2_conv_in["gg"],
        "L2_conv_betag": _L2_conv_in["betag"],
        "L2_conv_mg": _L2_conv_in["mg"],
        "L2_conv_vg": _L2_conv_in["vg"],
        "L2_conv_wh": _L2_conv_in["wh"],
        "L2_conv_bh": _L2_conv_in["bh"],
        "L2_conv_wv": _L2_conv_in["wv"],
        "L2_conv_bv": _L2_conv_in["bv"],
        "L3_conv_g_w": _L3_conv_in["g_w"],
        "L3_conv_g_b": _L3_conv_in["g_b"],
        "L3_conv_theta_w": _L3_conv_in["theta_w"],
        "L3_conv_theta_b": _L3_conv_in["theta_b"],
        "L3_conv_phi_w": _L3_conv_in["phi_w"],
        "L3_conv_phi_b": _L3_conv_in["phi_b"],
        "L3_conv_W_w": _L3_conv_in["W_w"],
        "L3_conv_W_b": _L3_conv_in["W_b"],
        "L3_conv_bn_gamma": _L3_conv_in["bn_gamma"],
        "L3_conv_bn_beta": _L3_conv_in["bn_beta"],
        "L3_conv_bn_mean": _L3_conv_in["bn_mean"],
        "L3_conv_bn_var": _L3_conv_in["bn_var"],
        "L3_conv_se1_w": _L3_conv_in["se1_w"],
        "L3_conv_se1_b": _L3_conv_in["se1_b"],
        "L3_conv_se2_w": _L3_conv_in["se2_w"],
        "L3_conv_se2_b": _L3_conv_in["se2_b"],
    }

def reference(x, L0_conv_bn1_g, L0_conv_bn1_b, L0_conv_bn2_g, L0_conv_bn2_b, L0_conv_qw, L0_conv_kw, L0_conv_vw, L0_conv_out_w, L0_conv_out_b, L0_conv_off_dw_w, L0_conv_off_dw_b, L0_conv_off_pw_w, L0_conv_cpb_w1, L0_conv_cpb_b1, L0_conv_cpb_w2, L0_conv_cpb_b2, L0_conv_cpb_w3, L0_conv_cpb_b3, L0_conv_mlp_w1, L0_conv_mlp_b1, L0_conv_mlp_w2, L0_conv_mlp_b2, L1_conv_Wq, L1_conv_bq, L1_conv_Wk, L1_conv_bk, L1_conv_Wv, L1_conv_bv, L1_conv_Wo, L1_conv_bo, L1_conv_gamma, L1_conv_beta, L2_conv_wf, L2_conv_bf, L2_conv_gf, L2_conv_betaf, L2_conv_mf, L2_conv_vf, L2_conv_wg, L2_conv_bg, L2_conv_gg, L2_conv_betag, L2_conv_mg, L2_conv_vg, L2_conv_wh, L2_conv_bh, L2_conv_wv, L2_conv_bv, L3_conv_g_w, L3_conv_g_b, L3_conv_theta_w, L3_conv_theta_b, L3_conv_phi_w, L3_conv_phi_b, L3_conv_W_w, L3_conv_W_b, L3_conv_bn_gamma, L3_conv_bn_beta, L3_conv_bn_mean, L3_conv_bn_var, L3_conv_se1_w, L3_conv_se1_b, L3_conv_se2_w, L3_conv_se2_b):
    import jax
    import jax.numpy as jnp
    def _L0_conv_ref(x, bn1_g, bn1_b, bn2_g, bn2_b, qw, kw, vw, out_w, out_b, off_dw_w, off_dw_b, off_pw_w, cpb_w1, cpb_b1, cpb_w2, cpb_b2, cpb_w3, cpb_b3, mlp_w1, mlp_b1, mlp_w2, mlp_b2):
        import jax, jax.numpy as jnp
        import numpy as np
        B, C, H, W = (2, 512, 32, 32)
        HEADS = 8
        GROUPS = 8
        DH = 64
        DF = 4
        OFF_SCALE = 4.0
        EPS = 1e-05

        def _bn(t, gamma, beta):
            s = gamma / jnp.sqrt(1.0 + EPS)
            return t * s[None, :, None, None] + beta[None, :, None, None]

        def _gconv1x1(t, w):
            b, c, h, ww = t.shape
            o = jnp.einsum('bgci,goc->bgoi', t.reshape(b, GROUPS, c // GROUPS, h * ww), w)
            return o.reshape(b, GROUPS * w.shape[1], h, ww)

        def _grid_sample(img, grid):
            N, Ci, Hi, Wi = img.shape
            gx = (grid[..., 0] + 1.0) * (Wi / 2.0) - 0.5
            gy = (grid[..., 1] + 1.0) * (Hi / 2.0) - 0.5
            x0 = jnp.floor(gx)
            y0 = jnp.floor(gy)
            wx = gx - x0
            wy = gy - y0

            def gather(im, ix, iy):
                valid = (ix >= 0) & (ix < Wi) & (iy >= 0) & (iy < Hi)
                ixc = jnp.clip(ix, 0, Wi - 1).astype(jnp.int32)
                iyc = jnp.clip(iy, 0, Hi - 1).astype(jnp.int32)
                return im[:, iyc, ixc] * valid[None].astype(im.dtype)

            def sample_one(im, x0, y0, wx, wy):
                v00 = gather(im, x0, y0)
                v01 = gather(im, x0 + 1, y0)
                v10 = gather(im, x0, y0 + 1)
                v11 = gather(im, x0 + 1, y0 + 1)
                wx = wx[None]
                wy = wy[None]
                return v00 * (1 - wx) * (1 - wy) + v01 * wx * (1 - wy) + v10 * (1 - wx) * wy + v11 * wx * wy
            return jax.vmap(sample_one)(img, x0, y0, wx, wy)

        def _forward(x, bn1_g, bn1_b, bn2_g, bn2_b, qw, kw, vw, out_w, out_b, off_dw_w, off_dw_b, off_pw_w, cpb_w1, cpb_b1, cpb_w2, cpb_b2, cpb_w3, cpb_b3, mlp_w1, mlp_b1, mlp_w2, mlp_b2):
            b = x.shape[0]
            xn = _bn(x, bn1_g, bn1_b)
            q = _gconv1x1(xn, qw)
            qg = q.reshape(b * GROUPS, DH, H, W)
            off = jax.lax.conv_general_dilated(qg, off_dw_w, (DF, DF), ((1, 1), (1, 1)), dimension_numbers=('NCHW', 'OIHW', 'NCHW'), feature_group_count=DH)
            off = jax.nn.gelu(off + off_dw_b[None, :, None, None], approximate=False)
            off = jnp.tanh(jnp.einsum('bchw,oc->bohw', off, off_pw_w)) * OFF_SCALE
            Hd, Wd = (off.shape[-2], off.shape[-1])
            gy, gx = jnp.meshgrid(jnp.arange(Hd, dtype=x.dtype), jnp.arange(Wd, dtype=x.dtype), indexing='ij')
            vx = gx[None] + off[:, 0]
            vy = gy[None] + off[:, 1]
            nx = 2.0 * vx / max(Hd - 1, 1) - 1.0
            ny = 2.0 * vy / max(Wd - 1, 1) - 1.0
            vgrid_scaled = jnp.stack((nx, ny), axis=-1)
            kv = _grid_sample(xn.reshape(b * GROUPS, DH, H, W), vgrid_scaled)
            kv = kv.reshape(b, GROUPS * DH, Hd, Wd)
            k = _gconv1x1(kv, kw)
            v = _gconv1x1(kv, vw)
            scale = DH ** (-0.5)
            qh = q.reshape(b, HEADS, DH, H * W).transpose(0, 1, 3, 2) * scale
            kh = k.reshape(b, HEADS, DH, Hd * Wd).transpose(0, 1, 3, 2)
            vh = v.reshape(b, HEADS, DH, Hd * Wd).transpose(0, 1, 3, 2)
            qgy, qgx = jnp.meshgrid(jnp.arange(H, dtype=x.dtype), jnp.arange(W, dtype=x.dtype), indexing='ij')
            grid_q = jnp.stack((2.0 * qgx / max(H - 1, 1) - 1.0, 2.0 * qgy / max(W - 1, 1) - 1.0), axis=-1).reshape(1, H * W, 2)
            grid_kv = vgrid_scaled.reshape(b * GROUPS, Hd * Wd, 2)
            pos = grid_q[:, :, None, :] - grid_kv[:, None, :, :]
            bias = jnp.sign(pos) * jnp.log1p(jnp.abs(pos))
            bias = jax.nn.relu(bias @ cpb_w1 + cpb_b1)
            bias = jax.nn.relu(bias @ cpb_w2 + cpb_b2)
            bias = (bias @ cpb_w3 + cpb_b3).reshape(b, GROUPS, H * W, Hd * Wd)
            sim = jnp.einsum('bhid,bhjd->bhij', qh, kh) + bias
            attn = jax.nn.softmax(sim, axis=-1)
            out = jnp.einsum('bhij,bhjd->bhid', attn, vh)
            out = out.transpose(0, 1, 3, 2).reshape(b, HEADS * DH, H, W)
            out = jnp.einsum('bchw,oc->bohw', out, out_w) + out_b[None, :, None, None]
            x = x + out
            xn2 = _bn(x, bn2_g, bn2_b)
            h1 = jax.nn.gelu(jnp.einsum('bchw,oc->bohw', xn2, mlp_w1) + mlp_b1[None, :, None, None], approximate=False)
            return x + jnp.einsum('bchw,oc->bohw', h1, mlp_w2) + mlp_b2[None, :, None, None]
        return _forward(x, bn1_g, bn1_b, bn2_g, bn2_b, qw, kw, vw, out_w, out_b, off_dw_w, off_dw_b, off_pw_w, cpb_w1, cpb_b1, cpb_w2, cpb_b2, cpb_w3, cpb_b3, mlp_w1, mlp_b1, mlp_w2, mlp_b2)

    def _L1_conv_ref(X, Wq, bq, Wk, bk, Wv, bv, Wo, bo, gamma, beta):
        import jax, jax.numpy as jnp
        import numpy as np
        B, C, H, W = (8, 512, 32, 32)
        HEADS = 8
        EPS = 1e-05

        def conv1x1(X, Wt, b):
            return jnp.einsum('co,bohw->bchw', Wt, X) + b[None, :, None, None]
        b, c, h, w = X.shape
        d = c // HEADS
        n = h * w
        K = conv1x1(X, Wq, bq).reshape(b, HEADS, d, n)
        Q = conv1x1(X, Wk, bk).reshape(b, HEADS, d, n)
        V = conv1x1(X, Wv, bv).reshape(b, HEADS, d, n)
        M = jnp.einsum('bhmn,bhen->bhme', K, V)
        Out = jnp.einsum('bhme,bhmn->bhen', M, Q)
        Out = Out.reshape(b, c, h, w)
        Out = conv1x1(Out, Wo, bo) + X
        mean = Out.mean(axis=(0, 2, 3), keepdims=True)
        var = Out.var(axis=(0, 2, 3), keepdims=True)
        Out = (Out - mean) * jax.lax.rsqrt(var + EPS)
        return Out * gamma[None, :, None, None] + beta[None, :, None, None]

    def _L2_conv_ref(x, wf, bf, gf, betaf, mf, vf, wg, bg, gg, betag, mg, vg, wh, bh, wv, bv):
        import jax, jax.numpy as jnp
        import numpy as np
        EPS = 1e-05

        def conv1x1(x, w, b):
            return jnp.einsum('bchw,oc->bohw', x, w) + b[None, :, None, None]

        def bn_eval(x, gamma, beta, mean, var):
            inv = gamma / jnp.sqrt(var + EPS)
            return x * inv[None, :, None, None] + (beta - mean * inv)[None, :, None, None]
        B, C, H, W = x.shape
        mid = wf.shape[0]
        HW = H * W
        f_x = jax.nn.relu(bn_eval(conv1x1(x, wf, bf), gf, betaf, mf, vf)).reshape(B, mid, HW)
        g_x = jax.nn.relu(bn_eval(conv1x1(x, wg, bg), gg, betag, mg, vg)).reshape(B, mid, HW)
        h_x = conv1x1(x, wh, bh).reshape(B, mid, HW)
        scale = mid ** (-0.5)
        scores = jnp.einsum('bcn,bcm->bnm', f_x, g_x) * scale
        attn = jax.nn.softmax(scores, axis=-1)
        z = jnp.einsum('bnm,bcm->bcn', attn, h_x).reshape(B, mid, H, W)
        z = conv1x1(z, wv, bv)
        return z + x

    def _L3_conv_ref(x, g_w, g_b, theta_w, theta_b, phi_w, phi_b, W_w, W_b, bn_gamma, bn_beta, bn_mean, bn_var, se1_w, se1_b, se2_w, se2_b):
        import jax, jax.numpy as jnp
        import numpy as np
        B, C, H, W = (8, 512, 64, 32)
        SE_MID = C // 16
        BN_EPS = 1e-05

        def conv1x1(x, w, b):
            return jnp.einsum('bchw,oc->bohw', x, w) + b[None, :, None, None]
        b, c, h, w = x.shape
        N = h * w
        x_avg = jnp.mean(x, axis=(2, 3), keepdims=True)
        se_mid = jax.nn.relu(conv1x1(x_avg, se1_w, se1_b))
        W_cw = jax.nn.sigmoid(conv1x1(se_mid, se2_w, se2_b))
        g_x = conv1x1(x, g_w, g_b).reshape(b, N)
        theta_x = conv1x1(x, theta_w, theta_b).reshape(b, N)
        phi_x = conv1x1(x, phi_w, phi_b).reshape(b, N)
        f = theta_x[:, :, None] * phi_x[:, None, :]
        f_div_C = jax.nn.softmax(f, axis=-1)
        y = jnp.einsum('bij,bj->bi', f_div_C, g_x)
        y = y.reshape(b, 1, h, w)
        W_y = conv1x1(y, W_w, W_b)
        inv = bn_gamma / jnp.sqrt(bn_var + BN_EPS)
        W_y = (W_y - bn_mean[None, :, None, None]) * inv[None, :, None, None] + bn_beta[None, :, None, None]
        return W_cw * W_y + x

    def _gn(v, G=32, eps=1e-5):
        B_, C_, H_, W_ = v.shape
        g = v.reshape(B_, G, C_ // G, H_, W_)
        m = jnp.mean(g, axis=(2, 3, 4), keepdims=True)
        s = jnp.var(g, axis=(2, 3, 4), keepdims=True)
        return ((g - m) / jnp.sqrt(s + eps)).reshape(v.shape)

    def _ln_c(v, eps=1e-6):
        m = jnp.mean(v, axis=1, keepdims=True)
        s = jnp.var(v, axis=1, keepdims=True)
        return (v - m) / jnp.sqrt(s + eps)

    def _ln_t(v, eps=1e-5):
        m = jnp.mean(v, axis=-1, keepdims=True)
        s = jnp.var(v, axis=-1, keepdims=True)
        return (v - m) / jnp.sqrt(s + eps)

    def _to_tokens(v):
        B_, C_, H_, W_ = v.shape
        return v.reshape(B_, C_, H_ * W_).transpose(0, 2, 1)
    def _from_tokens(t, like):
        B_, C_, H_, W_ = like.shape
        return t.transpose(0, 2, 1).reshape(B_, C_, H_, W_)

    x = _L0_conv_ref(x, L0_conv_bn1_g, L0_conv_bn1_b, L0_conv_bn2_g, L0_conv_bn2_b, L0_conv_qw, L0_conv_kw, L0_conv_vw, L0_conv_out_w, L0_conv_out_b, L0_conv_off_dw_w, L0_conv_off_dw_b, L0_conv_off_pw_w, L0_conv_cpb_w1, L0_conv_cpb_b1, L0_conv_cpb_w2, L0_conv_cpb_b2, L0_conv_cpb_w3, L0_conv_cpb_b3, L0_conv_mlp_w1, L0_conv_mlp_b1, L0_conv_mlp_w2, L0_conv_mlp_b2)
    x = _L1_conv_ref(x, L1_conv_Wq, L1_conv_bq, L1_conv_Wk, L1_conv_bk, L1_conv_Wv, L1_conv_bv, L1_conv_Wo, L1_conv_bo, L1_conv_gamma, L1_conv_beta)
    x = _L2_conv_ref(x, L2_conv_wf, L2_conv_bf, L2_conv_gf, L2_conv_betaf, L2_conv_mf, L2_conv_vf, L2_conv_wg, L2_conv_bg, L2_conv_gg, L2_conv_betag, L2_conv_mg, L2_conv_vg, L2_conv_wh, L2_conv_bh, L2_conv_wv, L2_conv_bv)
    x = _L3_conv_ref(x, L3_conv_g_w, L3_conv_g_b, L3_conv_theta_w, L3_conv_theta_b, L3_conv_phi_w, L3_conv_phi_b, L3_conv_W_w, L3_conv_W_b, L3_conv_bn_gamma, L3_conv_bn_beta, L3_conv_bn_mean, L3_conv_bn_var, L3_conv_se1_w, L3_conv_se1_b, L3_conv_se2_w, L3_conv_se2_b)
    return x


_drawn_inputs = setup_inputs


def setup_inputs(seed=0):
    import zlib

    import numpy as np

    out = dict(_drawn_inputs(seed))
    spreads = {'L0_conv_bn1_g': (1.0, 0.6),
     'L0_conv_bn1_b': (0.0, 0.325),
     'L0_conv_bn2_g': (1.0, 0.2),
     'L0_conv_bn2_b': (0.0, 0.1),
     'L0_conv_out_b': (0.0, 0.1),
     'L0_conv_off_dw_b': (0.0, 0.8),
     'L0_conv_cpb_b1': (0.0, 2.0),
     'L0_conv_cpb_b2': (0.0, 2.0),
     'L0_conv_mlp_b1': (0.0, 0.1),
     'L0_conv_mlp_b2': (0.0, 0.1),
     'L1_conv_bq': (0.0, 0.1),
     'L1_conv_bk': (0.0, 0.1),
     'L1_conv_bv': (0.0, 0.1),
     'L1_conv_bo': (0.0, 2.0),
     'L1_conv_gamma': (1.0, 0.2),
     'L1_conv_beta': (0.0, 0.1),
     'L2_conv_bf': (0.0, 0.525),
     'L2_conv_gf': (1.0, 0.2),
     'L2_conv_betaf': (0.0, 0.682),
     'L2_conv_bg': (0.0, 0.753),
     'L2_conv_gg': (1.0, 0.2),
     'L2_conv_betag': (0.0, 0.8),
     'L2_conv_bh': (0.0, 0.1),
     'L2_conv_bv': (0.0, 0.1),
     'L3_conv_se1_b': (0.0, 0.8),
     'L3_conv_se2_b': (0.0, 0.8)}
    factors = {'L0_conv_qw': 8.0,
     'L0_conv_kw': 8.0,
     'L0_conv_off_dw_w': 8.0,
     'L0_conv_off_pw_w': 8.0,
     'L0_conv_cpb_w1': 26.372,
     'L0_conv_cpb_w2': 39.632,
     'L0_conv_cpb_w3': 42.374,
     'L2_conv_mf': 5.464,
     'L2_conv_mg': 6.089,
     'L3_conv_g_w': 8.0,
     'L3_conv_theta_w': 8.0,
     'L3_conv_phi_w': 6.467,
     'L3_conv_W_w': 8.0,
     'L3_conv_bn_gamma': 8.0,
     'L3_conv_bn_var': 8.0,
     'L3_conv_se1_w': 8.0,
     'L3_conv_se2_w': 8.0,
     'L3_conv_W_b': 3.747,
     'L3_conv_bn_beta': 8.0,
     'L3_conv_bn_mean': 3.557}
    for name, (base, spread) in spreads.items():
        noise = np.random.default_rng([zlib.crc32(name.encode()), seed]).standard_normal(out[name].shape)
        drawn = base * np.exp(spread * noise) if base else spread * noise
        out[name] = jnp.asarray(drawn.astype(out[name].dtype))
    for name, factor in factors.items():
        out[name] = (out[name] * factor).astype(out[name].dtype)
    return out
```

```python
from contextlib import ExitStack

import numpy as np

import concourse.bass as bass
from concourse import mybir

F32 = mybir.dt.float32
F32R = mybir.dt.float32r
ACT = mybir.ActivationFunctionType
ALU = mybir.AluOpType
AX = mybir.AxisListType

P = 128
B, C, H, W = 2, 512, 32, 32
HW = H * W
CC = C // P
BLK = CC * B
BANK = 512
NT = HW // BANK
PC = HW // P
HEADS, DH = 8, 64
HALF = P // DH
HD = WD = 8
J = HD * WD
KS, DF = 6, 4
TAPS = sorted(range(KS * KS), key=lambda tap: tap != KS + 1)
OFF_SCALE = 4.0
EPS = 1e-5
BG = B * HEADS
FH = 4 * C
FC = FH // P
MID = C // 4
SE = C // 16
BIASF = 128

_WIDTHS = [
    ("bn1_g", CC), ("bn1_b", CC), ("bn2_g", CC), ("bn2_b", CC), ("out_b", CC),
    ("dw_w", KS * KS), ("dw_b", 1), ("pw", 2), ("cpb_b2", 1), ("cpb_b3", 1), ("cpb_w3", 1),
    ("mlp_b1", FC), ("mlp_b2", CC),
    ("bk", CC), ("bo", CC), ("gamma", CC), ("beta", CC),
    ("bf", 1), ("gf", 1), ("betaf", 1), ("mf", 1), ("vf", 1),
    ("bg", 1), ("gg", 1), ("betag", 1), ("mg", 1), ("vg", 1), ("bv2", CC),
    ("gtp_w", CC * 3), ("gtp_b", 1), ("W_w", CC), ("W_b", CC),
    ("bn_gamma", CC), ("bn_beta", CC), ("bn_mean", CC), ("bn_var", CC), ("se1_b", 1), ("se2_b", CC),
]
VCOL, VN = {}, 0
for _n, _w in _WIDTHS:
    VCOL[_n] = (VN, _w)
    VN += _w
_CWIDTHS = [("grid_x", J), ("grid_y", J), ("neg_ix", 1), ("neg_iy", PC), ("grid_q", W),
            ("mask_hi", 1), ("mask_lo", 1), ("ident", P)]
KCOL, KN = {}, 0
for _n, _w in _CWIDTHS:
    KCOL[_n] = (KN, _w)
    KN += _w

ROWS = 10


def flat(ap):
    n = ap.ndim - 1
    names = " ".join("abcdef"[:n])
    return ap.rearrange(f"p {names} -> p ({names})") if n > 1 else ap


class Kit:

    def __init__(self, nc, ctx, dram):
        self.nc, self.ctx, self.dram = nc, ctx, dram

    def sem(self, name):
        return self.ctx.enter_context(self.nc.semaphore(name))

    def v(self, name, i=0, n=1, p0=0, p1=P):
        o, _ = VCOL[name]
        return self.vecs[p0:p1, o + i:o + i + n]

    def k(self, name, i=0, n=None, p0=0, p1=P):
        o, w = KCOL[name]
        return self.consts[p0:p1, o + i:o + i + (w if n is None else n)]


def tensors(nc, ctx):
    def sb(name, shape, dt=F32):
        return ctx.enter_context(nc.sbuf_tensor(name, shape, dt))

    def ps(name, shape):
        return ctx.enter_context(nc.psum_tensor(name, shape, F32))

    return sb, ps


def stage_front(K, sb, ps):
    nc = K.nc
    K.XN = sb("XN", [P, CC, B, HW])
    K.XT = sb("XT", [P, B * PC, C])
    s1 = sb("s1", [P, CC])
    K.QW = QW = sb("QW", [P, CC, P])
    K.KW = KW = sb("KW", [P, CC, P])
    K.VW = VW = sb("VW", [P, CC, DH])
    qps = [ps(f"qps{i}", [P, BANK]) for i in range(2)]
    tps = [ps(f"tps{i}", [P, CC, P]) for i in range(2)]
    small, x_in, zero = K.sem("small_loaded"), [K.sem(f"x_loaded{c}") for c in range(CC)], K.sem("front_zeroed")
    w_in, s1_ready, xn_ready = K.sem("front_weights"), K.sem("s1_ready"), K.sem("xn_ready")
    q_mm, q_out, t_mm, t_out = K.sem("q_mm"), K.sem("q_out"), K.sem("xt_mm"), K.sem("xt_out")
    d = K.dram
    with nc.Block() as block:
        @block.sync
        def _(sp):
            sp.dma_start(K.vecs[:], d["vecs"]).then_inc(small, 16)
            sp.dma_start(K.consts[:], d["consts"]).then_inc(small, 16)
            for c in range(CC):
                for b in range(B):
                    sp.dma_start(K.X[:, c, b], d["x"][b, c * P:(c + 1) * P, :]).then_inc(x_in[c], 16)
            sp.wait_ge(zero, 2)
            for h in range(HALF):
                half = slice(h * DH, (h + 1) * DH)
                sp.dma_start(QW[half, :, half], d["qwT"][half]).then_inc(w_in, 16)
                sp.dma_start(KW[half, :, half], d["kwT"][half]).then_inc(w_in, 16)
            sp.dma_start(VW[:], d["vwT"]).then_inc(w_in, 16)
            sp.wait_ge(w_in, 80)

        @block.gpsimd
        def _(pool):
            nc.gpsimd.memset(QW[:], 0.0).then_inc(zero, 1)
            nc.gpsimd.memset(KW[:], 0.0).then_inc(zero, 1)
            nc.gpsimd.memset(K.KBD[:], 0.0).then_inc(zero, 1)
            nc.gpsimd.memset(K.VBD[:], 0.0).then_inc(zero, 1)
            pool.wait_ge(zero, 4)

        @block.scalar
        def _(act):
            act.wait_ge(s1_ready, 1)
            for c in range(CC):
                act.wait_ge(x_in[c], 16 * B)
                nc.scalar.activation(flat(K.XN[:, c]), flat(K.X[:, c]), ACT.Identity,
                                     bias=K.v("bn1_b", c), scale=s1[:, c:c + 1]).then_inc(xn_ready, 1)
            for i in range(BLK * NT):
                blk, t = divmod(i, NT)
                act.wait_ge(q_mm, i + 1)
                nc.scalar.activation(K.Q[:, blk, t * BANK:(t + 1) * BANK], qps[i % 2][:], ACT.Copy).then_inc(q_out, 1)

        @block.tensor
        def _(pe):
            pe.wait_ge(w_in, 80)
            pe.wait_ge(small, 32)
            for i in range(BLK * NT):
                blk, t = divmod(i, NT)
                c, b = divmod(blk, B)
                pe.wait_ge(xn_ready, c + 1)
                if i >= 2:
                    pe.wait_ge(q_out, i - 1)
                nc.tensor.matmul(qps[i % 2][:], QW[:, c], K.XN[:, c, b, t * BANK:(t + 1) * BANK],
                                 start=True, stop=True).then_inc(q_mm, 1)
            for i in range(B * PC):
                b, ch = divmod(i, PC)
                if i >= 2:
                    pe.wait_ge(t_out, i - 1)
                for c in range(CC):
                    last = nc.tensor.transpose(tps[i % 2][:, c], K.XN[:, c, b, ch * P:(ch + 1) * P], K.k("ident"))
                last.then_inc(t_mm, 1)

        @block.vector
        def _(dve):
            dve.wait_ge(small, 32)
            nc.vector.tensor_scalar(s1[:], K.v("bn1_g", 0, CC), float(1.0 / np.sqrt(1.0 + EPS)), None,
                                    ALU.mult).then_inc(s1_ready, 1)
            for i in range(B * PC):
                dve.wait_ge(t_mm, i + 1)
                nc.vector.tensor_copy(K.XT[:, i], flat(tps[i % 2][:])).then_inc(t_out, 1)


def stage_offsets(K, sb, ps):
    nc = K.nc
    diag = [sb(f"dw_diag{i}", [P, P]) for i in range(4)]
    pwr = sb("pw_rep", [P, 2, P])
    gel = sb("dw_gelu", [P, BLK * J])
    NX = sb("NX", [P, 2, HALF * BLK, J])
    tmp = sb("off_tmp", [P, 2, HALF * BLK, J])
    GXY = K.GXY
    ops, acc = ps("off_ps", [P, 2, HALF, BANK]), ps("dw_ps", [P, BLK, HD, WD])
    taps = K.sem("conv_taps")
    conv, gelu_done, pw_mm, tanh_done, crd = (K.sem("conv_step"), K.sem("gelu_done"), K.sem("pw_mm"),
                                              K.sem("tanh_done"), K.sem("coord_step"))
    nx_dram = K.sem("nx_stored")
    nt_in = K.nt_in = K.sem("nt_loaded")
    dn = nc.dram_tensor("nx_scratch", (2, HALF, BLK, J), F32).ap()
    with nc.Block() as block:
        @block.vector
        def _(dve):
            nc.vector.tensor_copy(pwr[:], K.v("pw", 0, 2).unsqueeze(2).to_broadcast([P, 2, P])).then_inc(conv, 1)
            for n in range(KS * KS):
                if n >= 4:
                    dve.wait_ge(taps, n - 3)
                nc.vector.tensor_scalar(diag[n % 4][:], K.k("ident"), K.v("dw_w", TAPS[n]), None, ALU.mult).then_inc(conv, 1)
            dve.wait_ge(tanh_done, 1)
            for axis, grid in enumerate(("grid_x", "grid_y")):
                nc.vector.scalar_tensor_tensor(tmp[:, axis], NX[:, axis], OFF_SCALE,
                                               K.k(grid).unsqueeze(1).to_broadcast([P, HALF * BLK, J]),
                                               ALU.mult, ALU.add).then_inc(crd, 1)
            dve.wait_ge(crd, 2)
            nc.vector.tensor_scalar(GXY[:], tmp[:], 2.0, 1.0 / (HD - 1), ALU.mult, ALU.mult).then_inc(crd, 1)
            dve.wait_ge(crd, 3)
            nc.vector.tensor_scalar(NX[:], GXY[:], -1.0, None, ALU.add).then_inc(crd, 1)
            dve.wait_ge(crd, 4)
            nc.vector.tensor_scalar(tmp[:], NX[:], 1.0, W / 2.0, ALU.add, ALU.mult).then_inc(crd, 1)
            dve.wait_ge(crd, 5)
            nc.vector.tensor_scalar(GXY[:], tmp[:], -0.5, None, ALU.add).then_inc(crd, 1)
            dve.wait_ge(crd, 6)

        @block.scalar
        def _(act):
            act.wait_ge(taps, KS * KS)
            nc.scalar.activation(gel[:], flat(acc[:]), ACT.Gelu, bias=K.v("dw_b")).then_inc(gelu_done, 1)
            act.wait_ge(pw_mm, 1)
            nc.scalar.activation(NX[:].rearrange("p a (h k) j -> p a h (k j)", h=HALF), ops[:], ACT.Tanh).then_inc(tanh_done, 1)

        @block.tensor
        def _(pe):
            q = K.Q[:].rearrange("p k (y x) -> p k y x", x=W)
            for n, tap in enumerate(TAPS):
                (y0, y1), (x0, x1) = ((int(k == 0), HD - int(k == KS - 1)) for k in divmod(tap, KS))
                ky, kx = divmod(tap, KS)
                iy, ix = DF * y0 + ky - 1, DF * x0 + kx - 1
                pe.wait_ge(conv, n + 2)
                last = nc.tensor.matmul(acc[:, :, y0:y1, x0:x1], diag[n % 4][:],
                                        q[:, :, iy:iy + DF * (y1 - y0 - 1) + 1:DF, ix:ix + DF * (x1 - x0 - 1) + 1:DF],
                                        start=(n == 0), stop=(n == KS * KS - 1))
                last.then_inc(taps, 1)
            pe.wait_ge(gelu_done, 1)
            for axis in range(2):
                for h in range(HALF):
                    half = slice(h * DH, (h + 1) * DH)
                    last = nc.tensor.matmul(ops[:, axis, h], pwr[half, axis], gel[half, :], start=True, stop=True)
            last.then_inc(pw_mm, 1)

        @block.sync
        def _(sp):
            sp.wait_ge(crd, 4)
            sp.dma_start(dn.rearrange("a h k j -> (a h k j)").unsqueeze(0), NX[0:1].rearrange("p a k j -> p (a k j)")).then_inc(nx_dram, 16)
            sp.wait_ge(nx_dram, 16)
            for axis in range(2):
                for h in range(HALF):
                    sp.dma_start(K.nt[axis * BG + h:axis * BG + BG:HALF, :], dn[axis, h]).then_inc(nt_in, 16)
            sp.wait_ge(nt_in, 64)


def stage_tables(K, sb, ps):
    nc = K.nc
    n_ax = 2 * BG
    th = sb("tab_hi", [n_ax, W, J], F32R)
    tl = sb("tab_lo", [n_ax, W, J], F32R)
    wt = K.XN[:].rearrange("p c b n -> p (c b n)").rearrange("p (s n) -> p s n", s=PC)
    SAMP = HALF * BLK * J
    pos, lg, sg = (wt[0:n_ax, 2 * i:2 * i + 2].rearrange("p s n -> p (s n)").rearrange("p (y j) -> p y j", j=J) for i in range(3))
    tx = sb("tent_x", [P, SAMP])
    ty = [sb(f"tent_y{i}", [P, SAMP]) for i in range(2)]
    kv = sb("kv", [P, BLK, J])
    w1raw, w1h, w1l, w1t = (sb("w1raw", [ROWS, BIASF]), sb("w1h", [ROWS, BIASF], F32R),
                            sb("w1l", [ROWS, BIASF], F32R), sb("w1t", [ROWS, BIASF]))
    w2raw = sb("w2raw", [P, BIASF])
    kvps, kps, vps = ps("kv_ps", [P, BLK, J]), ps("k_ps", [P, BLK, J]), ps("v_ps", [P, BLK, J])
    tab, axd, absd, tyd, wtd = (K.sem("tab_step"), K.sem("act_pos"), K.sem("act_dist"), K.sem("act_tent"), K.sem("w_tent"))
    kv_mm, kv_out, k_mm, v_mm, kb_out = (K.sem("kv_mm"), K.sem("kv_out"), K.sem("k_mm"), K.sem("v_mm"), K.sem("kvbd_out"))
    cw_in, cw, tab_out = K.sem("cpb_w_loaded"), K.sem("cpb_w_step"), K.sem("tab_stored")
    d = K.dram
    with nc.Block() as block:
        @block.sync
        def _(sp):
            sp.dma_start(w1raw[:], d["cpb_w1r"]).then_inc(cw_in, 16)
            sp.dma_start(w2raw[:], d["cpb_w2"]).then_inc(cw_in, 16)
            sp.wait_ge(tab, 6)
            for part, t in enumerate((th, tl)):
                sp.dma_start(K.dx[:, part], t[0:BG].bitcast(F32)).then_inc(tab_out, 16)
                sp.dma_start(K.dy[:, part].rearrange("(g c) y j -> g c (y j)", g=BG),
                             t[BG:n_ax].bitcast(F32).rearrange("g (c y) j -> g c (y j)", y=2)).then_inc(tab_out, 16)
            sp.wait_ge(tab_out, 64)

        @block.vector
        def _(dve):
            nc.vector.tensor_tensor(pos, K.k("grid_q", p1=n_ax).unsqueeze(2).to_broadcast([n_ax, W, J]),
                                    K.nt[:].unsqueeze(1).to_broadcast([n_ax, W, J]), ALU.subtract).then_inc(tab, 1)
            dve.wait_ge(tab, 1)
            nc.vector.tensor_scalar(sg, pos, 0.0, 2.0, ALU.is_ge, ALU.mult).then_inc(tab, 1)
            dve.wait_ge(axd, 2)
            dve.wait_ge(tab, 2)
            nc.vector.scalar_tensor_tensor(pos, sg, -1.0, lg, ALU.add, ALU.mult).then_inc(tab, 1)
            dve.wait_ge(tab, 3)
            nc.vector.tensor_copy(th[:], pos).then_inc(tab, 1)
            dve.wait_ge(tab, 4)
            nc.vector.tensor_tensor(tl[:], pos, th[:].bitcast(F32), ALU.subtract).then_inc(tab, 1)
            dve.wait_ge(tab, 5)
            for s in range(PC):
                dve.wait_ge(tyd, s + 2)
                ins = nc.vector.tensor_tensor(wt[:, s], ty[s % 2][:], tx[:], ALU.mult)
                ins.then_inc(wtd, 1)
                if s == 0:
                    nc.vector.tensor_copy(K.W3[:], K.v("cpb_w3").to_broadcast([P, 32])).then_inc(tab, 1)
            dve.wait_ge(cw_in, 32)
            nc.vector.tensor_copy(w1h[:], w1raw[:]).then_inc(cw, 1)
            nc.vector.tensor_copy(K.W2H[:], w2raw[:]).then_inc(cw, 1)
            dve.wait_ge(cw, 2)
            nc.vector.tensor_tensor(w1l[:], w1raw[:], w1h[:].bitcast(F32), ALU.subtract).then_inc(cw, 1)
            nc.vector.tensor_tensor(K.W2L[:], w2raw[:], K.W2H[:].bitcast(F32), ALU.subtract).then_inc(cw, 1)
            dve.wait_ge(cw, 4)
            nc.vector.tensor_scalar(w1t[:], w1l[:].bitcast(F32), K.k("mask_lo", p1=ROWS), None, ALU.mult).then_inc(cw, 1)
            dve.wait_ge(cw, 5)
            for par in range(2):
                nc.vector.scalar_tensor_tensor(K.W1R[32 * par:32 * par + ROWS], w1h[:].bitcast(F32), K.k("mask_hi", p1=ROWS), w1t[:],
                                               ALU.mult, ALU.add).then_inc(cw, 1)
            dve.wait_ge(kv_mm, 1)
            nc.vector.tensor_copy(kv[:], kvps[:]).then_inc(kv_out, 1)
            dve.wait_ge(k_mm, 1)
            for h in range(HALF):
                half = slice(h * DH, (h + 1) * DH)
                nc.vector.tensor_scalar(K.KBD[half, :, half], kps[half], float(DH) ** -0.5, None, ALU.mult).then_inc(kb_out, 1)
            dve.wait_ge(v_mm, 1)
            for h in range(HALF):
                half = slice(h * DH, (h + 1) * DH)
                nc.vector.tensor_copy(K.VBD[half, :, half], vps[half]).then_inc(kb_out, 1)
            dve.wait_ge(kb_out, 4)
            dve.wait_ge(cw, 7)

        @block.scalar
        def _(act):
            act.wait_ge(tab, 1)
            nc.scalar.activation(lg, pos, ACT.Abs).then_inc(axd, 1)
            act.wait_ge(axd, 1)
            nc.scalar.activation(lg, lg, ACT.Ln, bias=1.0).then_inc(axd, 1)
            gx, gy = (K.GXY[:, a].rearrange("p k j -> p (k j)") for a in range(2))
            for s in range(-1, PC):
                if s >= 1:
                    act.wait_ge(wtd, s - 1)
                to = tx[:] if s < 0 else ty[s % 2][:]
                nc.scalar.activation(to, gx if s < 0 else gy, ACT.Abs,
                                     bias=K.k("neg_ix") if s < 0 else K.k("neg_iy", s, 1)).then_inc(absd, 1)
                act.wait_ge(absd, s + 2)
                nc.scalar.activation(to, to, ACT.Relu,
                                     bias=1.0, scale=-1.0).then_inc(tyd, 1)

        @block.tensor
        def _(pe):
            pe.wait_ge(wtd, PC)
            for blk in range(BLK):
                c, b = divmod(blk, B)
                for h in range(HALF):
                    for s in range(PC):
                        ch0 = c * P + h * DH
                        smp = (h * BLK + blk) * J
                        last = nc.tensor.matmul(kvps[h * DH:(h + 1) * DH, blk], K.XT[:, b * PC + s, ch0:ch0 + DH],
                                                wt[:, s, smp:smp + J], start=(s == 0), stop=(s == PC - 1))
            last.then_inc(kv_mm, 1)
            pe.wait_ge(kv_out, 1)
            for c in range(CC):
                last = nc.tensor.matmul(flat(kps[:, B * c:B * c + B]), K.KW[:, c], flat(kv[:, B * c:B * c + B]), start=True, stop=True)
            last.then_inc(k_mm, 1)
            for blk in range(BLK):
                for h in range(HALF):
                    half = slice(h * DH, (h + 1) * DH)
                    last = nc.tensor.matmul(vps[half, blk], kv[half, blk], K.VW[half, blk // B], start=True, stop=True)
            last.then_inc(v_mm, 1)


def stage_bias(K, sb, ps):
    nc = K.nc
    TILE = 1024
    QROW = W * J
    CHUNK = 2 * QROW
    N = BG * HW * J // (2 * CHUNK)
    S_all = sb("S", [32 + ROWS, 2, W, J], F32R)
    S = [S_all[32 * i:32 * i + ROWS] for i in range(2)]
    hh = [sb(f"h1_hi{i}", [P, TILE], F32R) for i in range(2)]
    hl = [sb(f"h1_lo{i}", [P, TILE], F32R) for i in range(2)]
    h2 = [sb(f"h2_{i}", [P, QROW]) for i in range(2)]
    br = [sb(f"bias_rows{i}", [P, 2, BANK]) for i in range(2)]
    p1 = [ps(f"l1_ps{i}", [P, TILE]) for i in range(2)]
    p2 = [ps(f"l2_ps{i}", [P, BANK]) for i in range(3)]
    p3 = ps("l3_ps", [P, BANK])
    ones = K.sem("s_ones")
    s_in, rows_out = [K.sem(f"s_loaded{i}") for i in range(2)], [K.sem(f"rows_stored{i}") for i in range(2)]
    l1, hi_done, lo_done, l2 = K.sem("l1_mm"), K.sem("hi_done"), K.sem("lo_done"), K.sem("l2_mm")
    relu_a, relu_b, l3, copied = K.sem("relu_a"), K.sem("relu_b"), K.sem("l3_mm"), K.sem("rows_copied")
    with nc.Block() as block:
        @block.vector
        def _(dve):
            nc.vector.memset(S_all[:].bitcast(F32), 1.0).then_inc(ones, 1)
            dve.wait_ge(ones, 1)
    LOADS = 6 * 16
    with nc.Block() as block:
        @block.sync
        def _(sp):
            def load(it, bg, k):
                for dup in range(2):
                    sp.dma_start(S[k][2 * dup:2 * dup + 2].bitcast(F32).rearrange("r q a j -> r q (a j)"),
                                 K.dx[bass.ds(bg, 1)].squeeze(0).rearrange("r a j -> r (a j)").unsqueeze(1)
                                 .to_broadcast([2, 2, QROW])).then_inc(s_in[k], 16)
                    for q in range(2):
                        sp.dma_start(S[k][4 + 2 * dup:6 + 2 * dup, q].bitcast(F32),
                                     K.dy[bass.ds(it * 2 + k, 1), :, q].squeeze(0).unsqueeze(1)
                                     .to_broadcast([2, W, J])).then_inc(s_in[k], 16)
            load(0, 0, 0)
            load(0, 0, 1)
            with sp.Fori(1, N) as it:
                for k in range(2):
                    sp.wait_ge(l1, it * 8 + 4 * k - 4)
                    load(it, it // 8, k)

        @block.tensor
        def _(pe):
            def layer_one(u):
                k, q, part = (u // 4) % 2, (u // 2) % 2, u % 2
                row = S[k][:, q].rearrange("r a j -> r (a j)")
                for a in range(2):
                    at = TILE * part + BANK * a
                    last = nc.tensor.matmul(p1[u % 2][:, BANK * a:BANK * (a + 1)], K.W1R[32 * k:32 * k + ROWS], row[:, at:at + BANK],
                                            start=True, stop=True)
                last.then_inc(l1, 1)

            def layer_three(par):
                for g in range(4):
                    last = nc.tensor.matmul(p3[32 * g:32 * g + 32, :], K.W3[:], h2[par][:, BANK * g:BANK * (g + 1)],
                                            start=True, stop=True, tile_position=(0, 32 * g))
                last.then_inc(l3, 1)

            pe.wait_ge(s_in[0], LOADS)
            layer_one(0)
            layer_one(1)

            def body(it, first, last):
                for u in range(8):
                    t = it * 8 + u
                    pe.wait_ge(hi_done, t + 1)
                    out = (p2[u % 2], p2[2])
                    for a in range(2):
                        if a == 0 and not (first and u < 2):
                            pe.wait_ge(relu_a, t - 1)
                        if a == 1 and not (first and u == 0):
                            pe.wait_ge(relu_b, t)
                        h = hh[u % 2][:, BANK * a:BANK * (a + 1)]
                        nc.tensor.matmul(out[a][:], K.W2H[:], h, start=True, stop=False)
                        nc.tensor.matmul(out[a][:], K.W2L[:], h, start=False, stop=False)
                        if a == 0:
                            pe.wait_ge(lo_done, t + 1)
                        nc.tensor.matmul(out[a][:], K.W2H[:], hl[u % 2][:, BANK * a:BANK * (a + 1)],
                                         start=False, stop=True).then_inc(l2, 1)
                    if not (last and u >= 6):
                        if u == 2:
                            pe.wait_ge(s_in[1], (it + 1) * LOADS)
                        if u == 6:
                            pe.wait_ge(s_in[0], (it + 2) * LOADS)
                        layer_one((u + 2) % 8)
                    if u % 2 == 0 and not (first and u == 0):
                        pe.wait_ge(relu_a, t)
                        pe.wait_ge(relu_b, t)
                        if not (first and u == 2):
                            pe.wait_ge(copied, it * 4 + u // 2 - 1)
                        layer_three((u // 2 - 1) % 2)

            body(0, True, False)
            with pe.Fori(1, N - 1) as it:
                body(it, False, False)
            body(N - 1, False, True)
            pe.wait_ge(relu_a, N * 8)
            pe.wait_ge(relu_b, N * 8)
            pe.wait_ge(copied, N * 4 - 1)
            layer_three(1)

        @block.scalar
        def _(act):
            def high(it, u):
                act.wait_ge(l1, it * 8 + u + 1)
                nc.scalar.activation(hh[u % 2][:], p1[u % 2][:], ACT.Relu).then_inc(hi_done, 1)

            def copy_rows(it, row, first):
                act.wait_ge(l3, it * 4 + row + 1)
                k = row // 2
                if row % 2 == 0 and not first:
                    act.wait_ge(rows_out[k], it * 16)
                nc.scalar.activation(br[k][:, row % 2, :], p3[:], ACT.Identity, bias=K.v("cpb_b3")).then_inc(copied, 1)

            high(0, 0)
            high(0, 1)

            def body(it, first, last):
                for u in range(8):
                    t = it * 8 + u
                    act.wait_ge(l2, t * 2 + 2)
                    if not first or u >= 4:
                        act.wait_ge(l3, it * 4 + u // 2 - 1)
                    at = (u % 2) * TILE + BANK
                    nc.scalar.activation(h2[(u // 2) % 2][:, at:at + BANK], p2[2][:], ACT.Relu,
                                         bias=K.v("cpb_b2")).then_inc(relu_b, 1)
                    if not (last and u >= 6):
                        high(it if u < 6 else it + 1, (u + 2) % 8)
                    if u % 2 == 0 and not (first and u == 0):
                        if u == 0:
                            copy_rows(it - 1, 3, False)
                        else:
                            copy_rows(it, u // 2 - 1, first)

            body(0, True, False)
            with act.Fori(1, N - 1) as it:
                body(it, False, False)
            body(N - 1, False, True)
            copy_rows(N - 1, 3, False)

        @block.vector
        def _(dve):
            def low(it, u):
                dve.wait_ge(hi_done, it * 8 + u + 1)
                nc.vector.scalar_tensor_tensor(hl[u % 2][:], p1[u % 2][:], 0.0, hh[u % 2][:].bitcast(F32),
                                               ALU.max, ALU.subtract).then_inc(lo_done, 1)

            low(0, 0)
            low(0, 1)

            def body(it, first, last):
                for u in range(8):
                    t = it * 8 + u
                    dve.wait_ge(l2, t * 2 + 1)
                    if not first or u >= 4:
                        dve.wait_ge(l3, it * 4 + u // 2 - 1)
                    at = (u % 2) * TILE
                    nc.vector.tensor_scalar(h2[(u // 2) % 2][:, at:at + BANK], p2[u % 2][:], K.v("cpb_b2"), 0.0,
                                            ALU.add, ALU.max).then_inc(relu_a, 1)
                    if not (last and u >= 6):
                        low(it if u < 6 else it + 1, (u + 2) % 8)

            body(0, True, False)
            with dve.Fori(1, N - 1) as it:
                body(it, False, False)
            body(N - 1, False, True)

        @block.gpsimd
        def _(pool):
            with pool.Fori(0, N) as it:
                for k in range(2):
                    pool.wait_ge(copied, it * 4 + 2 * k + 2)
                    pool.dma_start(K.db[bass.ds(it * 2 + k, 1)].squeeze(0).rearrange("q g n -> g q n"),
                                   br[k][0:P:32]).then_inc(rows_out[k], 16)
            for k in range(2):
                pool.wait_ge(rows_out[k], 16 * N)


def stage_attention(K, sb, ps):
    nc = K.nc
    AO = K.AH[:].rearrange("p (k n) -> p k n", k=BLK)
    CH = PC * HALF * J
    bi = [sb(f"bias_in{i}", [P, HALF, PC, J]) for i in range(2)]
    sc = [sb(f"scores{i}", [P, PC, HALF, J]) for i in range(2)]
    pr = sb("probs", [P, PC, HALF, J])
    at = sb("probsT", [P, HW])
    mx, sm, rs = sb("smax", [P, PC * HALF]), sb("ssum", [P, PC * HALF]), sb("srec", [P, PC * HALF])
    sps = [ps(f"score_ps{i}", [P, PC, P]) for i in range(2)]
    tps, ops = ps("probsT_ps", [P, HW]), ps("att_ps", [P, HW])
    b_in, s_mm, st, ex = [K.sem(f"bias_in{i}") for i in range(2)], K.sem("score_mm"), K.sem("soft_step"), K.sem("soft_exp")
    t_mm, t_out, o_mm, o_out = K.sem("probsT_mm"), K.sem("probsT_out"), K.sem("att_mm"), K.sem("att_out")
    STEPS = 6
    with nc.Block() as block:
        @block.sync
        def _(sp):
            for g in range(BLK):
                if g >= 2:
                    sp.wait_ge(st, STEPS * (g - 2) + 1)
                for h in range(HALF):
                    sp.dma_start(bi[g % 2][:, h], K.db_bg[HALF * g + h].rearrange("(s p) j -> p s j", p=P)).then_inc(b_in[g % 2], 16)

        @block.tensor
        def _(pe):
            def scores(g):
                if g >= 2:
                    pe.wait_ge(st, STEPS * (g - 2) + 1)
                for s in range(PC):
                    last = nc.tensor.matmul(sps[g % 2][:, s], K.Q[:, g, s * P:(s + 1) * P], K.KBD[:, g], start=True, stop=True)
                last.then_inc(s_mm, 1)

            def values(g):
                pe.wait_ge(st, STEPS * g + STEPS)
                if g >= 1:
                    pe.wait_ge(t_out, g)
                for s in range(PC):
                    last = nc.tensor.transpose(tps[:, s * P:(s + 1) * P], pr[:, s].rearrange("p h j -> p (h j)"), K.k("ident"))
                last.then_inc(t_mm, 1)
                pe.wait_ge(t_out, g + 1)
                if g >= 1:
                    pe.wait_ge(o_out, g)
                for t in range(NT):
                    last = nc.tensor.matmul(ops[:, t * BANK:(t + 1) * BANK], K.VBD[:, g], at[:, t * BANK:(t + 1) * BANK],
                                            start=True, stop=True)
                last.then_inc(o_mm, 1)

            scores(0)
            for g in range(BLK):
                if g + 1 < BLK:
                    scores(g + 1)
                values(g)

        @block.vector
        def _(dve):
            for g in range(BLK):
                n = STEPS * g
                s3 = sc[g % 2][:].rearrange("p s h j -> p (s h) j")
                dve.wait_ge(s_mm, g + 1)
                dve.wait_ge(b_in[g % 2], 16 * HALF * (g // 2 + 1))
                nc.vector.tensor_tensor(sc[g % 2][:], sps[g % 2][:].rearrange("p s (h j) -> p s h j", h=HALF),
                                        bi[g % 2][:].rearrange("p h s j -> p s h j"), ALU.add).then_inc(st, 1)
                dve.wait_ge(st, n + 1)
                nc.vector.tensor_reduce(mx[:], s3, AX.X, ALU.max).then_inc(st, 1)
                dve.wait_ge(st, n + 2)
                nc.vector.tensor_tensor(s3, s3, mx[:].unsqueeze(2).to_broadcast([P, PC * HALF, J]), ALU.subtract).then_inc(st, 1)
                dve.wait_ge(ex, g + 1)
                nc.vector.tensor_reduce(sm[:], s3, AX.X, ALU.add).then_inc(st, 1)
                dve.wait_ge(st, n + 4)
                nc.vector.reciprocal(rs[:], sm[:]).then_inc(st, 1)
                dve.wait_ge(st, n + 5)
                if g >= 1:
                    dve.wait_ge(t_mm, g)
                nc.vector.tensor_tensor(pr[:].rearrange("p s h j -> p (s h) j"), s3,
                                        rs[:].unsqueeze(2).to_broadcast([P, PC * HALF, J]), ALU.mult).then_inc(st, 1)

        @block.scalar
        def _(act):
            def out(g):
                act.wait_ge(t_mm, g + 1)
                if g >= 1:
                    act.wait_ge(o_mm, g)
                nc.scalar.activation(at[:], tps[:], ACT.Copy).then_inc(t_out, 1)
                act.wait_ge(o_mm, g + 1)
                nc.scalar.activation(AO[:, g], ops[:], ACT.Copy).then_inc(o_out, 1)

            for g in range(BLK):
                act.wait_ge(st, STEPS * g + 3)
                nc.scalar.activation(flat(sc[g % 2][:]), flat(sc[g % 2][:]), ACT.Exp).then_inc(ex, 1)
                if g >= 1:
                    out(g - 1)
            out(BLK - 1)


def stage_out_proj(K, sb, ps):
    nc = K.nc
    AO = K.AH[:].rearrange("p (c b n) -> p c b n", c=CC, b=B)
    OW = flat(K.Q[:])[:, 0:CC * C].rearrange("p (c o) -> p c o", c=CC)
    s2 = sb("s2", [P, CC])
    pp = [ps(f"proj_ps{i}", [P, BANK]) for i in range(4)]
    w_in, mm, out, s2d = K.sem("out_w_loaded"), K.sem("proj_mm"), K.sem("proj_out"), K.sem("s2_ready")
    with nc.Block() as block:
        @block.sync
        def _(sp):
            sp.dma_start(OW, K.dram["out_wT"]).then_inc(w_in, 16)

        @block.tensor
        def _(pe):
            pe.wait_ge(w_in, 16)
            for i in range(B * NT * CC):
                bt, o = divmod(i, CC)
                b, t = divmod(bt, NT)
                if i >= 4:
                    pe.wait_ge(out, i - 3)
                for c in range(CC):
                    last = nc.tensor.matmul(pp[i % 4][:], OW[:, c, o * P:(o + 1) * P], AO[:, c, b, t * BANK:(t + 1) * BANK],
                                            start=(c == 0), stop=(c == CC - 1))
                last.then_inc(mm, 1)

        @block.vector
        def _(dve):
            nc.vector.tensor_scalar(s2[:], K.v("bn2_g", 0, CC), float(1.0 / np.sqrt(1.0 + EPS)), None,
                                    ALU.mult).then_inc(s2d, 1)
            for i in range(B * NT * CC):
                bt, o = divmod(i, CC)
                b, t = divmod(bt, NT)
                x = K.X[:, o, b, t * BANK:(t + 1) * BANK]
                dve.wait_ge(mm, i + 1)
                nc.vector.scalar_tensor_tensor(x, pp[i % 4][:], K.v("out_b", o), x, ALU.add, ALU.add).then_inc(out, 1)

        @block.scalar
        def _(act):
            act.wait_ge(s2d, 1)
            for i in range(B * NT * CC):
                bt, o = divmod(i, CC)
                b, t = divmod(bt, NT)
                act.wait_ge(out, i + 1)
                nc.scalar.activation(K.XN2[:, o, b, t * BANK:(t + 1) * BANK], K.X[:, o, b, t * BANK:(t + 1) * BANK],
                                     ACT.Identity, bias=K.v("bn2_b", o), scale=s2[:, o:o + 1])


def stage_mlp(K, sb, ps):
    nc = K.nc
    HID = K.AH[:].rearrange("p (f n) -> p f n", f=FC)
    pa = [ps(f"mlp_ps{i}", [P, BANK]) for i in range(3)]
    pb = [ps(f"mlp_out_ps{i}", [P, BANK]) for i in range(2)]
    m1, ge, m2, out = K.sem("mlp1_mm"), K.sem("mlp_gelu"), K.sem("mlp2_mm"), K.sem("mlp_out")
    with nc.Block() as block:
        @block.tensor
        def _(pe):
            pe.wait_ge(K.mlp_in, 32)
            for bt in range(B * NT):
                b, t = divmod(bt, NT)
                for f in range(FC):
                    n = bt * FC + f
                    if n >= 3:
                        pe.wait_ge(ge, n - 2)
                    for c in range(CC):
                        last = nc.tensor.matmul(pa[n % 3][:], K.W1M[:, c, f * P:(f + 1) * P], K.XN2[:, c, b, t * BANK:(t + 1) * BANK],
                                                start=(c == 0), stop=(c == CC - 1))
                    last.then_inc(m1, 1)
                for o in range(CC):
                    n = bt * CC + o
                    if n >= 2:
                        pe.wait_ge(out, n - 1)
                    for f in range(FC):
                        pe.wait_ge(ge, bt * FC + f + 1)
                        last = nc.tensor.matmul(pb[n % 2][:], K.W2M[:, f, o * P:(o + 1) * P], HID[:, f], start=(f == 0), stop=(f == FC - 1))
                    last.then_inc(m2, 1)

        @block.scalar
        def _(act):
            for bt in range(B * NT):
                for f in range(FC):
                    n = bt * FC + f
                    act.wait_ge(m1, n + 1)
                    if bt:
                        act.wait_ge(m2, bt * CC)
                    nc.scalar.activation(HID[:, f], pa[n % 3][:], ACT.Gelu, bias=K.v("mlp_b1", f)).then_inc(ge, 1)

        @block.vector
        def _(dve):
            for bt in range(B * NT):
                b, t = divmod(bt, NT)
                for o in range(CC):
                    x = K.X[:, o, b, t * BANK:(t + 1) * BANK]
                    dve.wait_ge(m2, bt * CC + o + 1)
                    nc.vector.scalar_tensor_tensor(x, pb[(bt * CC + o) % 2][:], K.v("mlp_b2", o), x, ALU.add, ALU.add).then_inc(out, 1)


def stage_linear(K, sb, ps):
    nc = K.nc
    d = K.dram
    wq, wv, wk, wo = (sb(n, [P, CC, C]) for n in ("l1_wq", "l1_wv", "l1_wk", "l1_wo"))
    bqr, bvr = sb("bq_rep", [P, C]), sb("bv_rep", [P, C])
    kt, vt = sb("kt", [P, PC, C]), sb("vt", [P, PC, C])
    mt, aT, tt = sb("mt", [P, CC, P]), sb("aT", [P, CC, C]), sb("tT", [P, CC, C])
    bb = sb("lin_bias", [P, CC])
    Y = sb("lin_y", [P, CC, B, HW])
    st = sb("bn_st", [P, CC, B * NT, 6])
    mv, inv, sh = sb("bn_mv", [P, CC, 2]), sb("bn_inv", [P, CC]), sb("bn_sh", [P, CC])
    kps, vps = [ps(f"kt_ps{i}", [P, BANK]) for i in range(2)], [ps(f"vt_ps{i}", [P, BANK]) for i in range(2)]
    mps, bps = ps("m_ps", [P, CC, P]), ps("b_ps", [P, CC])
    yps = [ps(f"y_ps{i}", [P, BANK]) for i in range(2)]
    w_in, zero = K.sem("l1_w_loaded"), K.sem("mt_zeroed")
    kv_mm, k_out, v_out, m_mm, m_out = K.sem("ktvt_mm"), K.sem("kt_out"), K.sem("vt_out"), K.sem("m_mm"), K.sem("m_out")
    g_mm, g_out, b_mm, b_out = K.sem("fold_mm"), K.sem("fold_out"), K.sem("foldb_mm"), K.sem("foldb_out")
    y_mm, y_out, s_step, sq, nrm = K.sem("lin_mm"), K.sem("lin_out"), K.sem("bn_step"), K.sem("bn_sqrt"), K.sem("bn_done")
    with nc.Block() as block:
        @block.sync
        def _(sp):
            for t, n in ((wq, "WqT"), (wv, "WvT"), (wk, "Wk"), (wo, "WoT")):
                sp.dma_start(t[:], d[n]).then_inc(w_in, 16)
            sp.dma_start(bqr[:], d["bq"].partition_broadcast(P)).then_inc(w_in, 16)
            sp.dma_start(bvr[:], d["bv"].partition_broadcast(P)).then_inc(w_in, 16)

        @block.gpsimd
        def _(pool):
            nc.gpsimd.memset(mt[:], 0.0).then_inc(zero, 1)

        @block.tensor
        def _(pe):
            pe.wait_ge(w_in, 96)
            for b in range(B):
                for s in range(PC):
                    n = b * PC + s
                    if n >= 2:
                        pe.wait_ge(k_out, n - 1)
                        pe.wait_ge(v_out, n - 1)
                    for w, t in ((wq, kps), (wv, vps)):
                        for c in range(CC):
                            last = nc.tensor.matmul(t[n % 2][:], K.X[:, c, b, s * P:(s + 1) * P], w[:, c], start=(c == 0), stop=(c == CC - 1))
                    last.then_inc(kv_mm, 1)
                pe.wait_ge(k_out, PC * (b + 1))
                pe.wait_ge(v_out, PC * (b + 1))
                if b:
                    pe.wait_ge(m_out, 2 * b)
                for c in range(CC):
                    for s in range(PC):
                        last = nc.tensor.matmul(mps[:, c], vt[:, s, c * P:(c + 1) * P], kt[:, s, c * P:(c + 1) * P],
                                                start=(s == 0), stop=(s == PC - 1))
                last.then_inc(m_mm, 1)
                pe.wait_ge(m_out, 2 * b + 2)
                for i in range(2 * CC):
                    n = b * 2 * CC + i
                    if n >= 2:
                        pe.wait_ge(g_out, n - 1)
                    if i == CC:
                        pe.wait_ge(g_out, n)
                    if i < CC:
                        last = nc.tensor.matmul(yps[n % 2][:], mt[:, i], wo[:, i], start=True, stop=True)
                    else:
                        for c in range(CC):
                            last = nc.tensor.matmul(yps[n % 2][:], wk[:, c, (i - CC) * P:(i - CC + 1) * P], aT[:, c],
                                                    start=(c == 0), stop=(c == CC - 1))
                    last.then_inc(g_mm, 1)
                if b:
                    pe.wait_ge(b_out, b)
                for o in range(CC):
                    for c in range(CC):
                        last = nc.tensor.matmul(bps[:, o:o + 1], aT[:, c, o * P:(o + 1) * P], K.v("bk", c), start=(c == 0), stop=(c == CC - 1))
                last.then_inc(b_mm, 1)
                pe.wait_ge(g_out, (b + 1) * 2 * CC)
                for i in range(NT * CC):
                    t, o = divmod(i, CC)
                    n = b * NT * CC + i
                    if n >= 2:
                        pe.wait_ge(y_out, n - 1)
                    for c in range(CC):
                        last = nc.tensor.matmul(yps[n % 2][:], tt[:, c, o * P:(o + 1) * P], K.X[:, c, b, t * BANK:(t + 1) * BANK],
                                                start=(c == 0), stop=(c == CC - 1))
                    last.then_inc(y_mm, 1)

        @block.vector
        def _(dve):
            dve.wait_ge(w_in, 96)
            dve.wait_ge(zero, 1)
            for b in range(B):
                for s in range(PC):
                    n = b * PC + s
                    dve.wait_ge(kv_mm, n + 1)
                    if b and s == 0:
                        dve.wait_ge(m_mm, b)
                    nc.vector.tensor_tensor(kt[:, s], kps[n % 2][:], bqr[:], ALU.add).then_inc(k_out, 1)
                    nc.vector.tensor_tensor(vt[:, s], vps[n % 2][:], bvr[:], ALU.add).then_inc(v_out, 1)
                dve.wait_ge(m_mm, b + 1)
                if b:
                    dve.wait_ge(g_mm, b * 2 * CC)
                for h in range(HALF):
                    half = slice(h * DH, (h + 1) * DH)
                    nc.vector.tensor_copy(mt[half, :, half], mps[half, :, half]).then_inc(m_out, 1)
                dve.wait_ge(b_mm, b + 1)
                if b:
                    dve.wait_ge(y_out, NT * CC * b)
                nc.vector.tensor_tensor(bb[:], bps[:], K.v("bo", 0, CC), ALU.add).then_inc(b_out, 1)
                dve.wait_ge(b_out, b + 1)
                for i in range(NT * CC):
                    t, o = divmod(i, CC)
                    n = b * NT * CC + i
                    dve.wait_ge(y_mm, n + 1)
                    nc.vector.scalar_tensor_tensor(Y[:, o, b, t * BANK:(t + 1) * BANK], yps[n % 2][:], bb[:, o:o + 1],
                                                   K.X[:, o, b, t * BANK:(t + 1) * BANK], ALU.add, ALU.add).then_inc(y_out, 1)
            n = 0
            for o in range(CC):
                for b in range(B):
                    for t in range(NT):
                        dve.wait_ge(y_out, b * NT * CC + t * CC + o + 1)
                        nc.vector.bn_stats(st[:, o, b * NT + t], Y[:, o, b, t * BANK:(t + 1) * BANK]).then_inc(s_step, 1)
                        n += 1
            dve.wait_ge(s_step, n)
            for o in range(CC):
                nc.vector.bn_aggr(mv[:, o], flat(st[:, o])).then_inc(s_step, 1)
                n += 1
            dve.wait_ge(sq, 1)
            nc.vector.reciprocal(sh[:], inv[:]).then_inc(s_step, 1)
            dve.wait_ge(s_step, n + 1)
            nc.vector.tensor_tensor(inv[:], sh[:], K.v("gamma", 0, CC), ALU.mult).then_inc(s_step, 1)
            dve.wait_ge(s_step, n + 2)
            nc.vector.tensor_tensor(sh[:], mv[:, :, 0], inv[:], ALU.mult).then_inc(s_step, 1)
            dve.wait_ge(s_step, n + 3)
            nc.vector.tensor_tensor(sh[:], K.v("beta", 0, CC), sh[:], ALU.subtract).then_inc(s_step, 1)
            dve.wait_ge(s_step, n + 4)
            for o in range(CC // 2):
                nc.vector.tensor_scalar(flat(K.X[:, o]), flat(Y[:, o]), inv[:, o:o + 1], sh[:, o:o + 1], ALU.mult, ALU.add).then_inc(nrm, 1)

        @block.scalar
        def _(act):
            for b in range(B):
                for i in range(2 * CC):
                    n = b * 2 * CC + i
                    act.wait_ge(g_mm, n + 1)
                    if b and i == 0:
                        act.wait_ge(y_mm, NT * CC * b)
                    dst = aT[:, i] if i < CC else tt[:, i - CC]
                    nc.scalar.activation(dst, yps[n % 2][:], ACT.Copy).then_inc(g_out, 1)
            N_ST = CC * B * NT + CC
            act.wait_ge(s_step, N_ST)
            act.wait_ge(K.eps_ready, 1)
            nc.scalar.activation(inv[:], mv[:, :, 1], ACT.Sqrt, bias=K.eps[:]).then_inc(sq, 1)
            act.wait_ge(s_step, N_ST + 4)
            for o in range(CC // 2, CC):
                nc.scalar.activation(flat(K.X[:, o]), flat(Y[:, o]), ACT.Identity, bias=sh[:, o:o + 1], scale=inv[:, o:o + 1])


def stage_nonlocal(K, sb, ps):
    nc = K.nc
    d = K.dram
    wf, wg, wh = (sb(n, [P, CC, MID]) for n in ("wf", "wg", "wh"))
    wv = sb("wv", [P, C])
    bhr = sb("bh_rep", [P, MID])
    fg = [sb("f", [P, B, HW]), sb("g", [P, B, HW])]
    hT = sb("hT", [P, B * PC, MID])
    ex = [sb(f"e{i}", [P, HW]) for i in range(2)]
    eT = sb("eT", [P, PC, HW])
    z = sb("z", [P, HW])
    sc, bi = sb("fg_sc", [P, 2]), sb("fg_bi", [P, 2])
    nm, sm, rs = sb("nmax", [P, B * PC]), sb("esum", [P, B * PC]), sb("erec", [P, B * PC])
    sps = [ps(f"fg_ps{i}", [P, HW]) for i in range(2)]
    tps = ps("eT_ps", [P, HW])
    zps = [ps(f"z_ps{i}", [P, BANK]) for i in range(2)]
    SC = float(MID) ** -0.5
    w_in, cf, cs = K.sem("l2_w_loaded"), K.sem("fg_coef"), K.sem("fg_sqrt")
    fg_mm, fg_out, h_mm, h_out = K.sem("fg_mm"), K.sem("fg_out"), K.sem("h_mm"), K.sem("h_out")
    s_mm, mxd, exd, sts, t_mm, t_out = K.sem("nl_score"), K.sem("nl_max"), K.sem("nl_exp"), K.sem("nl_step"), K.sem("nl_tr"), K.sem("nl_tr_out")
    z_mm, z_out, o_mm, o_out = K.sem("z_mm"), K.sem("z_out"), K.sem("nlo_mm"), K.sem("nlo_out")
    NF = 2 * B
    with nc.Block() as block:
        @block.sync
        def _(sp):
            for t, n in ((wf, "wfT"), (wg, "wgT"), (wh, "whT")):
                sp.dma_start(t[:], d[n]).then_inc(w_in, 16)
            sp.dma_start(wv[:], d["wvT"]).then_inc(w_in, 16)
            sp.dma_start(bhr[:], d["bh"].partition_broadcast(P)).then_inc(w_in, 16)

        @block.tensor
        def _(pe):
            pe.wait_ge(w_in, 80)
            for i in range(NF):
                b, k = divmod(i, 2)
                if i >= 2:
                    pe.wait_ge(fg_out, i - 1)
                for t in range(NT):
                    for c in range(CC):
                        last = nc.tensor.matmul(sps[i % 2][:, t * BANK:(t + 1) * BANK], (wf, wg)[k][:, c],
                                                K.X[:, c, b, t * BANK:(t + 1) * BANK], start=(c == 0), stop=(c == CC - 1))
                last.then_inc(fg_mm, 1)
            for i in range(B * PC // 4):
                if i >= 2:
                    pe.wait_ge(h_out, i - 1)
                for r in range(4):
                    b, s = divmod(4 * i + r, PC)
                    for c in range(CC):
                        last = nc.tensor.matmul(zps[i % 2][:, r * MID:(r + 1) * MID], K.X[:, c, b, s * P:(s + 1) * P], wh[:, c],
                                                start=(c == 0), stop=(c == CC - 1))
                last.then_inc(h_mm, 1)
            pe.wait_ge(fg_out, NF)
            pe.wait_ge(h_out, B * PC // 4)

            def scores(n):
                b, s = divmod(n, PC)
                if n >= 2:
                    pe.wait_ge(exd, n - 1)
                for t in range(NT):
                    last = nc.tensor.matmul(sps[n % 2][:, t * BANK:(t + 1) * BANK], fg[0][:, b, s * P:(s + 1) * P],
                                            fg[1][:, b, t * BANK:(t + 1) * BANK], start=True, stop=True)
                last.then_inc(s_mm, 1)

            def turn(n):
                pe.wait_ge(sts, 2 * n + 2)
                if n >= 1:
                    pe.wait_ge(t_out, n)
                for m in range(PC):
                    last = nc.tensor.transpose(tps[:, m * P:(m + 1) * P], ex[n % 2][:, m * P:(m + 1) * P], K.k("ident"))
                last.then_inc(t_mm, 1)

            scores(0)
            for b in range(B):
                for s in range(PC):
                    n = b * PC + s
                    if n + 1 < B * PC:
                        scores(n + 1)
                    turn(n)
                pe.wait_ge(t_out, PC * (b + 1))
                for t in range(NT):
                    n = b * NT + t
                    if n >= 2:
                        pe.wait_ge(z_out, n - 1)
                    if n:
                        pe.wait_ge(o_out, n * CC)
                    for m in range(PC):
                        last = nc.tensor.matmul(zps[0][:], hT[:, b * PC + m], eT[:, m, t * BANK:(t + 1) * BANK],
                                                start=(m == 0), stop=(m == PC - 1))
                    last.then_inc(z_mm, 1)
                    pe.wait_ge(z_out, n + 1)
                    for o in range(CC):
                        k = n * CC + o
                        if k >= 2:
                            pe.wait_ge(o_out, k - 1)
                        nc.tensor.matmul(zps[1 - o % 2][:], wv[:, o * P:(o + 1) * P], z[:, t * BANK:(t + 1) * BANK],
                                         start=True, stop=True).then_inc(o_mm, 1)

        @block.vector
        def _(dve):
            dve.wait_ge(cs, 1)
            n = 0
            nc.vector.reciprocal(bi[:], sc[:]).then_inc(cf, 1)
            dve.wait_ge(cf, 1)
            for k, (g, cb, be, me) in enumerate((("gf", "bf", "betaf", "mf"), ("gg", "bg", "betag", "mg"))):
                n = 1 + 4 * k
                col = slice(k, k + 1)
                nc.vector.tensor_tensor(sc[:, col], bi[:, col], K.v(g), ALU.mult).then_inc(cf, 1)
                dve.wait_ge(cf, n + 1)
                nc.vector.tensor_tensor(bi[:, col], K.v(cb), K.v(me), ALU.subtract).then_inc(cf, 1)
                dve.wait_ge(cf, n + 2)
                nc.vector.tensor_tensor(bi[:, col], bi[:, col], sc[:, col], ALU.mult).then_inc(cf, 1)
                dve.wait_ge(cf, n + 3)
                nc.vector.tensor_tensor(bi[:, col], bi[:, col], K.v(be), ALU.add).then_inc(cf, 1)
                dve.wait_ge(cf, n + 4)
            dve.wait_ge(w_in, 80)
            for i in range(B * PC // 4):
                dve.wait_ge(h_mm, i + 1)
                nc.vector.tensor_tensor(hT[:, 4 * i:4 * i + 4], zps[i % 2][:].rearrange("p (r m) -> p r m", r=4),
                                        bhr[:].unsqueeze(1).to_broadcast([P, 4, MID]), ALU.add).then_inc(h_out, 1)

            def peak(n):
                dve.wait_ge(s_mm, n + 1)
                nc.vector.tensor_reduce(rs[:, n:n + 1], sps[n % 2][:], AX.X, ALU.max).then_inc(mxd, 1)
                dve.wait_ge(mxd, 2 * n + 1)
                nc.vector.tensor_scalar(nm[:, n:n + 1], rs[:, n:n + 1], -SC, None, ALU.mult).then_inc(mxd, 1)

            def norm(n):
                dve.wait_ge(exd, n + 1)
                nc.vector.reciprocal(rs[:, n:n + 1], sm[:, n:n + 1]).then_inc(sts, 1)
                dve.wait_ge(sts, 2 * n + 1)
                nc.vector.tensor_scalar(ex[n % 2][:], ex[n % 2][:], rs[:, n:n + 1], None, ALU.mult).then_inc(sts, 1)

            def project(n):
                b, t = divmod(n, NT)
                for o in range(CC):
                    x = K.X[:, o, b, t * BANK:(t + 1) * BANK]
                    dve.wait_ge(o_mm, n * CC + o + 1)
                    nc.vector.scalar_tensor_tensor(x, zps[1 - o % 2][:], K.v("bv2", o), x, ALU.add, ALU.add).then_inc(o_out, 1)

            peak(0)
            for n in range(B * PC):
                if n + 1 < B * PC:
                    peak(n + 1)
                norm(n)
                if n % PC == PC - 1:
                    for t in range(NT):
                        project((n // PC) * NT + t)

        @block.scalar
        def _(act):
            act.wait_ge(K.eps_ready, 1)
            nc.scalar.activation(sc[:, 1:2], K.v("vg"), ACT.Sqrt, bias=K.eps[:])
            nc.scalar.activation(sc[:, 0:1], K.v("vf"), ACT.Sqrt, bias=K.eps[:]).then_inc(cs, 1)
            act.wait_ge(cf, 9)
            for i in range(NF):
                b, k = divmod(i, 2)
                act.wait_ge(fg_mm, i + 1)
                nc.scalar.activation(fg[k][:, b], sps[i % 2][:], ACT.Relu, bias=bi[:, k:k + 1], scale=sc[:, k:k + 1]).then_inc(fg_out, 1)

            def exps(n):
                act.wait_ge(mxd, 2 * n + 2)
                if n >= 2:
                    act.wait_ge(t_mm, n - 1)
                nc.scalar.activation(ex[n % 2][:], sps[n % 2][:], ACT.Exp, bias=nm[:, n:n + 1], scale=SC,
                                     accum_out=sm[:, n:n + 1]).then_inc(exd, 1)

            exps(0)
            for n in range(B * PC):
                b, s = divmod(n, PC)
                if n + 1 < B * PC:
                    exps(n + 1)
                act.wait_ge(t_mm, n + 1)
                if b and s == 0:
                    act.wait_ge(z_mm, NT * b)
                nc.scalar.activation(eT[:, :, s * P:(s + 1) * P], tps[:].rearrange("p (m n) -> p m n", m=PC), ACT.Copy).then_inc(t_out, 1)
                if s == PC - 1:
                    for t in range(NT):
                        k = b * NT + t
                        act.wait_ge(z_mm, k + 1)
                        nc.scalar.activation(z[:, t * BANK:(t + 1) * BANK], zps[0][:], ACT.Copy).then_inc(z_out, 1)


def stage_rank_one(K, sb, ps):
    nc = K.nc
    d = K.dram
    se1, se2 = sb("se1", [P, CC, SE]), sb("se2", [SE, C])
    rows = sb("gtp_rows", [3, B, HW])
    rep = sb("gp_rep", [P, 2, B, HW])
    th = sb("theta", [P, B, PC])
    av, mid, gate = sb("avg", [P, CC, B]), sb("se_mid", [SE, B]), sb("gate", [P, CC, B])
    inv, t1, ga, gd = sb("bn3_inv", [P, CC]), sb("bn3_t", [P, CC]), sb("ga", [P, CC, B]), sb("gd", [P, CC, B])
    pm = sb("phi_ext", [P, 2, B])
    m1, m2 = sb("m1", [P, B, PC]), sb("m2", [P, B, PC])
    e = [sb(f"r1_e{i}", [P, HW]) for i in range(2)]
    den, num, y = sb("r1_den", [P, B * PC]), sb("r1_num", [P, B * PC]), sb("r1_y", [P, B * PC])
    ones, dg = sb("ones", [P, P]), [sb(f"dg{i}", [P, P]) for i in range(2)]
    out = [sb(f"out{i}", [P, HW]) for i in range(2)]
    gps = [ps(f"gtp_ps{i}", [3, BANK]) for i in range(2)]
    aps = ps("se_ps", [P, CC, B])
    mps = ps("se1_ps", [SE, B])
    yps = ps("yrep_ps", [P, B, HW])
    w_in, av_d, g_mm, g_out, gd_out, r_in = (K.sem("l3_w_loaded"), K.sem("avg_done"), K.sem("gtp_mm"), K.sem("gtp_out"),
                                             K.sem("gtp_stored"), K.sem("rep_loaded"))
    se, sx, st, ex = K.sem("se_mm"), K.sem("se_act"), K.sem("r1_step"), K.sem("r1_exp")
    nd, ydg, y_mm, af, o_st, o_out = K.sem("r1_sum"), K.sem("r1_diag"), K.sem("r1_mm"), K.sem("r1_affine"), K.sem("out_stored"), K.sem("out_sum")
    dg_dram = nc.dram_tensor("gtp_scratch", (3, B, HW), F32).ap()
    with nc.Block() as block:
        @block.sync
        def _(sp):
            sp.dma_start(se1[:], d["se1_wT"]).then_inc(w_in, 16)
            sp.dma_start(se2[:], d["se2_wT"]).then_inc(w_in, 16)
            sp.wait_ge(g_out, B * NT)
            sp.dma_start(dg_dram, rows[:]).then_inc(gd_out, 16)
            sp.wait_ge(gd_out, 16)
            sp.dma_start(rep[:, 1], dg_dram[2].partition_broadcast(P)).then_inc(r_in, 16)
            for b in range(B):
                sp.dma_start(th[:, b], dg_dram[1, b].rearrange("(p s) -> p s", p=P)).then_inc(r_in, 16)
            sp.dma_start(rep[:, 0], dg_dram[0].partition_broadcast(P)).then_inc(r_in, 16)
            for n in range(CC * B):
                c, b = divmod(n, B)
                sp.wait_ge(o_out, n + 1)
                sp.dma_start(d["out"][b, c * P:(c + 1) * P, :], out[n % 2][:]).then_inc(o_st, 16)
                sp.wait_ge(o_st, 16 * (n + 1))

        @block.gpsimd
        def _(pool):
            nc.gpsimd.memset(ones[:], 1.0).then_inc(ydg, 1)

        @block.tensor
        def _(pe):
            for n in range(B * NT):
                b, t = divmod(n, NT)
                if n >= 2:
                    pe.wait_ge(g_out, n - 1)
                for c in range(CC):
                    last = nc.tensor.matmul(gps[n % 2][:], K.v("gtp_w", 3 * c, 3), K.X[:, c, b, t * BANK:(t + 1) * BANK],
                                            start=(c == 0), stop=(c == CC - 1))
                last.then_inc(g_mm, 1)
            pe.wait_ge(w_in, 32)
            pe.wait_ge(av_d, 1)
            for c in range(CC):
                last = nc.tensor.matmul(mps[:], se1[:, c], av[:, c], start=(c == 0), stop=(c == CC - 1))
            last.then_inc(se, 1)
            pe.wait_ge(sx, 1)
            for c in range(CC):
                last = nc.tensor.matmul(aps[:, c], se2[:, c * P:(c + 1) * P], mid[:], start=True, stop=True)
            last.then_inc(se, 1)
            for n in range(B * PC):
                b, s = divmod(n, PC)
                pe.wait_ge(ydg, n + 2)
                nc.tensor.matmul(yps[:, b, s * P:(s + 1) * P], ones[:], dg[n % 2][:], start=True, stop=True).then_inc(y_mm, 1)

        @block.vector
        def _(dve):
            nc.vector.tensor_reduce(av[:], K.X[:], AX.X, ALU.add).then_inc(st, 1)
            dve.wait_ge(st, 1)
            nc.vector.tensor_scalar(av[:], av[:], 1.0 / HW, None, ALU.mult).then_inc(av_d, 1)
            dve.wait_ge(r_in, 64)
            nc.vector.tensor_reduce(pm[:, 0], rep[:, 1], AX.X, ALU.max).then_inc(st, 1)
            nc.vector.tensor_reduce(pm[:, 1], rep[:, 1], AX.X, ALU.min).then_inc(st, 1)
            dve.wait_ge(st, 3)
            nc.vector.tensor_tensor(m1[:], th[:], pm[:, 0].unsqueeze(2).to_broadcast([P, B, PC]), ALU.mult).then_inc(st, 1)
            nc.vector.tensor_tensor(m2[:], th[:], pm[:, 1].unsqueeze(2).to_broadcast([P, B, PC]), ALU.mult).then_inc(st, 1)
            dve.wait_ge(st, 5)
            nc.vector.tensor_tensor(m1[:], m1[:], m2[:], ALU.max).then_inc(st, 1)
            dve.wait_ge(st, 6)
            nc.vector.tensor_scalar(m2[:], m1[:], -1.0, None, ALU.mult).then_inc(st, 1)
            for n in range(B * PC):
                dve.wait_ge(ex, n + 1)
                nc.vector.tensor_tensor_reduce(e[n % 2][:], e[n % 2][:], rep[:, 0, n // PC], 1.0, 0.0, ALU.mult, ALU.add,
                                               num[:, n:n + 1]).then_inc(nd, 1)
            dve.wait_ge(nd, B * PC)
            nc.vector.reciprocal(y[:], den[:]).then_inc(st, 1)
            dve.wait_ge(st, 8)
            nc.vector.tensor_tensor(y[:], y[:], num[:], ALU.mult).then_inc(st, 1)
            dve.wait_ge(st, 9)
            dve.wait_ge(ydg, 1)
            for n in range(B * PC):
                if n >= 2:
                    dve.wait_ge(y_mm, n - 1)
                nc.vector.tensor_scalar(dg[n % 2][:], K.k("ident"), y[:, n:n + 1], None, ALU.mult).then_inc(ydg, 1)
            dve.wait_ge(sx, 3)
            nc.vector.reciprocal(t1[:], inv[:]).then_inc(st, 1)
            dve.wait_ge(st, 10)
            nc.vector.tensor_tensor(inv[:], t1[:], K.v("bn_gamma", 0, CC), ALU.mult).then_inc(st, 1)
            dve.wait_ge(st, 11)
            nc.vector.tensor_tensor(t1[:], K.v("W_b", 0, CC), K.v("bn_mean", 0, CC), ALU.subtract).then_inc(st, 1)
            dve.wait_ge(st, 12)
            nc.vector.tensor_tensor(t1[:], t1[:], inv[:], ALU.mult).then_inc(st, 1)
            dve.wait_ge(st, 13)
            nc.vector.tensor_tensor(t1[:], t1[:], K.v("bn_beta", 0, CC), ALU.add).then_inc(st, 1)
            nc.vector.tensor_tensor(inv[:], inv[:], K.v("W_w", 0, CC), ALU.mult).then_inc(st, 1)
            dve.wait_ge(st, 15)
            nc.vector.tensor_tensor(ga[:], gate[:], inv[:].unsqueeze(2).to_broadcast([P, CC, B]), ALU.mult).then_inc(st, 1)
            nc.vector.tensor_tensor(gd[:], gate[:], t1[:].unsqueeze(2).to_broadcast([P, CC, B]), ALU.mult).then_inc(st, 1)
            for n in range(CC * B):
                c, b = divmod(n, B)
                dve.wait_ge(af, n + 1)
                nc.vector.tensor_tensor(out[n % 2][:], out[n % 2][:], K.X[:, c, b], ALU.add).then_inc(o_out, 1)

        @block.scalar
        def _(act):
            for n in range(B * NT):
                b, t = divmod(n, NT)
                act.wait_ge(g_mm, n + 1)
                nc.scalar.activation(rows[:, b, t * BANK:(t + 1) * BANK], gps[n % 2][:], ACT.Identity,
                                     bias=K.v("gtp_b", p1=3)).then_inc(g_out, 1)
            act.wait_ge(se, 1)
            nc.scalar.activation(mid[:], mps[:], ACT.Relu, bias=K.v("se1_b", p1=SE)).then_inc(sx, 1)
            act.wait_ge(se, 2)
            for c in range(CC):
                last = nc.scalar.activation(gate[:, c], aps[:, c], ACT.Sigmoid, bias=K.v("se2_b", c))
            last.then_inc(sx, 1)
            nc.scalar.activation(inv[:], K.v("bn_var", 0, CC), ACT.Sqrt, bias=K.eps[:]).then_inc(sx, 1)
            act.wait_ge(st, 7)
            for n in range(B * PC):
                b, s = divmod(n, PC)
                if n >= 2:
                    act.wait_ge(nd, n - 1)
                nc.scalar.activation(e[n % 2][:], rep[:, 1, b], ACT.Exp, bias=m2[:, b, s:s + 1], scale=th[:, b, s:s + 1],
                                     accum_out=den[:, n:n + 1]).then_inc(ex, 1)
            act.wait_ge(y_mm, B * PC)
            act.wait_ge(st, 17)
            for n in range(CC * B):
                c, b = divmod(n, B)
                if n >= 2:
                    act.wait_ge(o_st, 16 * (n - 1))
                nc.scalar.activation(out[n % 2][:].rearrange("p (i s) -> p i s", i=P), yps[:, b].rearrange("p (s i) -> p i s", i=P),
                                     ACT.Identity, bias=gd[:, c, b:b + 1], scale=ga[:, c, b:b + 1]).then_inc(af, 1)


def build(nc, dram):
    with ExitStack() as ctx:
        K = Kit(nc, ctx, dram)
        sb, _ = tensors(nc, ctx)
        K.vecs, K.consts = sb("vecs", [P, VN]), sb("consts_sb", [P, KN])
        K.eps = sb("eps", [P, 1])
        K.X = sb("X", [P, CC, B, HW])
        K.W1R = sb("W1R", [32 + ROWS, BIASF], F32R)
        K.W2H, K.W2L = sb("W2H", [P, BIASF], F32R), sb("W2L", [P, BIASF], F32R)
        K.W3 = sb("W3", [P, 32])
        K.dx = nc.dram_tensor("x_table", (BG, 2, W, J), F32).ap()
        K.dy = nc.dram_tensor("y_table", (BG * H // 2, 2, 2, J), F32).ap()
        K.db = nc.dram_tensor("bias_scratch", (BG * H // 2, 2, 4, BANK), F32).ap()
        K.db_bg = K.db.rearrange("c q g n -> (c q g n)").rearrange("(g i j) -> g i j", g=BG, j=J)
        K.eps_ready = K.sem("eps_ready")
        with nc.Block() as block:
            @block.vector
            def _(dve):
                nc.vector.memset(K.eps[:], EPS).then_inc(K.eps_ready, 1)
        with ExitStack() as l0:
            sb0, _ = tensors(nc, l0)
            K.Q = sb0("Q", [P, BLK, HW])
            K.KBD, K.VBD = sb0("KBD", [P, BLK, P]), sb0("VBD", [P, BLK, P])
            with ExitStack() as front:
                with ExitStack() as s:
                    sbf, _ = tensors(nc, front)
                    stage_front(K, sbf, tensors(nc, s)[1])
                K.GXY, K.nt = sbf("GXY", [P, 2, HALF * BLK, J]), sbf("nt", [2 * BG, J])
                with ExitStack() as s:
                    sbo, pso = tensors(nc, s)
                    stage_offsets(K, sbo, pso)
                with ExitStack() as s:
                    stage_tables(K, *tensors(nc, s))
            with ExitStack() as s:
                sb1, _ = tensors(nc, s)
                K.W1M, K.W2M = sb1("W1M", [P, CC, FH]), sb1("W2M", [P, FC, C])
                K.mlp_in = K.sem("mlp_w_loaded")
                with nc.Block() as block:
                    @block.scalar
                    def _(act):
                        act.dma_start(K.W1M[:], dram["mlp_w1T"]).then_inc(K.mlp_in, 16)
                        act.dma_start(K.W2M[:], dram["mlp_w2T"]).then_inc(K.mlp_in, 16)
                with ExitStack() as s2:
                    stage_bias(K, *tensors(nc, s2))
                K.AH = sb1("AH", [P, FC * BANK])
                with ExitStack() as s2:
                    stage_attention(K, *tensors(nc, s2))
                K.XN2 = sb1("XN2", [P, CC, B, HW])
                with ExitStack() as s2:
                    stage_out_proj(K, *tensors(nc, s2))
                with ExitStack() as s2:
                    stage_mlp(K, *tensors(nc, s2))
        with ExitStack() as s:
            stage_linear(K, *tensors(nc, s))
        with ExitStack() as s:
            stage_nonlocal(K, *tensors(nc, s))
        with ExitStack() as s:
            stage_rank_one(K, *tensors(nc, s))


def constants():
    j, p = np.arange(J), np.arange(P)
    k = np.zeros((P, KN), np.float32)

    def put(name, a):
        o, w = KCOL[name]
        k[:, o:o + w] = a

    put("grid_x", (j % WD)[None])
    put("grid_y", (j // WD)[None])
    put("neg_ix", -(p % W)[:, None])
    put("neg_iy", -(np.arange(PC)[None] * (P // W) + (p // W)[:, None]))
    put("grid_q", (np.float32(2.0) * np.arange(W, dtype=np.float32) / np.float32(W - 1) - np.float32(1.0))[None])
    put("mask_hi", np.isin(p, (0, 1, 4, 5, 8)).astype(np.float32)[:, None])
    put("mask_lo", np.isin(p, (2, 3, 6, 7, 9)).astype(np.float32)[:, None])
    put("ident", np.eye(P, dtype=np.float32))
    return k


def lay_out(a):
    def chunks(v):
        return v.reshape(-1, P).T

    def pad(v):
        return np.concatenate([v, np.zeros(P - v.shape[0], v.dtype)])[:, None]

    def in_rows(w):
        return np.ascontiguousarray(w.T.reshape(-1, P, w.shape[0]).transpose(1, 0, 2))

    def rep(v, n=P):
        return np.broadcast_to(v.reshape(1, 1), (n, 1))

    L0, L1, L2, L3 = ({k[8:]: v for k, v in a.items() if k.startswith(f"L{i}_conv_")} for i in range(4))
    vec = {
        "bn1_g": chunks(L0["bn1_g"]), "bn1_b": chunks(L0["bn1_b"]), "bn2_g": chunks(L0["bn2_g"]), "bn2_b": chunks(L0["bn2_b"]),
        "out_b": chunks(L0["out_b"]), "dw_w": np.concatenate([L0["off_dw_w"].reshape(DH, -1)] * HALF),
        "dw_b": np.concatenate([L0["off_dw_b"]] * HALF)[:, None], "pw": np.concatenate([L0["off_pw_w"].T] * HALF),
        "cpb_b2": L0["cpb_b2"][:, None], "cpb_b3": rep(L0["cpb_b3"]), "cpb_w3": L0["cpb_w3"],
        "mlp_b1": chunks(L0["mlp_b1"]), "mlp_b2": chunks(L0["mlp_b2"]),
        "bk": chunks(L1["bk"]), "bo": chunks(L1["bo"]), "gamma": chunks(L1["gamma"]), "beta": chunks(L1["beta"]),
        "bv2": chunks(L2["bv"]),
        "gtp_w": np.stack([L3["g_w"][0], L3["theta_w"][0], L3["phi_w"][0]], 1).reshape(CC, P, 3).transpose(1, 0, 2).reshape(P, 3 * CC),
        "gtp_b": pad(np.concatenate([L3["g_b"], L3["theta_b"], L3["phi_b"]])),
        "W_w": chunks(L3["W_w"].reshape(-1)), "W_b": chunks(L3["W_b"]),
        "bn_gamma": chunks(L3["bn_gamma"]), "bn_beta": chunks(L3["bn_beta"]), "bn_mean": chunks(L3["bn_mean"]),
        "bn_var": chunks(L3["bn_var"]), "se1_b": pad(L3["se1_b"]), "se2_b": chunks(L3["se2_b"]),
    }
    for n in ("bf", "gf", "betaf", "mf", "vf", "bg", "gg", "betag", "mg", "vg"):
        vec[n] = L2[n][:, None]

    def per_group(w):
        return np.ascontiguousarray(w.reshape(CC, HALF, DH, DH).transpose(1, 3, 0, 2).reshape(P, CC, DH))

    w1, b1 = L0["cpb_w1"], L0["cpb_b1"]
    return {
        "x": a["x"].reshape(B, C, HW),
        "vecs": np.concatenate([vec[n] for n, _ in _WIDTHS], 1), "consts": constants(),
        "qwT": per_group(L0["qw"]), "kwT": per_group(L0["kw"]), "vwT": per_group(L0["vw"]),
        "cpb_w1r": np.stack([w1[0]] * 4 + [w1[1]] * 4 + [b1] * 2), "cpb_w2": L0["cpb_w2"],
        "out_wT": in_rows(L0["out_w"]), "mlp_w1T": in_rows(L0["mlp_w1"]), "mlp_w2T": in_rows(L0["mlp_w2"]),
        "WqT": in_rows(L1["Wq"]), "WvT": in_rows(L1["Wv"]), "Wk": in_rows(L1["Wk"].T), "WoT": in_rows(L1["Wo"]),
        "bq": L1["bq"], "bv": L1["bv"],
        "wfT": in_rows(L2["wf"]), "wgT": in_rows(L2["wg"]), "whT": in_rows(L2["wh"]), "wvT": np.ascontiguousarray(L2["wv"].T),
        "bh": L2["bh"], "se1_wT": in_rows(L3["se1_w"]), "se2_wT": np.ascontiguousarray(L3["se2_w"].T),
    }


def kernel(**inputs):
    import concourse.bacc as bacc
    from concourse.bass_utils import run_bass_kernel_spmd

    arrays = {n: np.ascontiguousarray(v) for n, v in lay_out({k: np.asarray(v) for k, v in inputs.items()}).items()}
    nc = bacc.Bacc("TRN2", target_bir_lowering=False, num_devices=1)
    dram = {n: nc.dram_tensor(f"in_{n}", v.shape, mybir.dt.from_np(v.dtype), kind="ExternalInput").ap() for n, v in arrays.items()}
    dram["out"] = nc.dram_tensor("out", (B, C, HW), F32, kind="ExternalOutput").ap()
    build(nc, dram)
    result = run_bass_kernel_spmd(nc, [{f"in_{n}": v for n, v in arrays.items()}], core_ids=[0])
    return result.results[0]["out"].reshape(B, C, H, W)
```

```python
from contextlib import ExitStack

import numpy as np

import concourse.bass as bass
from concourse import mybir

F32 = mybir.dt.float32
F32R = mybir.dt.float32r
ACT = mybir.ActivationFunctionType
ALU = mybir.AluOpType
AX = mybir.AxisListType

P = 128
B, C, H, W = 2, 512, 32, 32
HW = H * W
CC = C // P
BLK = CC * B
BANK = 512
NT = HW // BANK
PC = HW // P
HEADS, DH = 8, 64
HALF = P // DH
HD = WD = 8
J = HD * WD
KS, DF = 6, 4
TAPS = sorted(range(KS * KS), key=lambda tap: tap != KS + 1)
OFF_SCALE = 4.0
EPS = 1e-5
BG = B * HEADS
FH = 4 * C
FC = FH // P
MID = C // 4
SE = C // 16
BIASF = 128

_WIDTHS = [
    ("bn1_g", CC), ("bn1_b", CC), ("bn2_g", CC), ("bn2_b", CC), ("out_b", CC),
    ("dw_w", KS * KS), ("dw_b", 1), ("pw", 2), ("cpb_b2", 1), ("cpb_b3", 1), ("cpb_w3", 1),
    ("mlp_b1", FC), ("mlp_b2", CC),
    ("bk", CC), ("bo", CC), ("gamma", CC), ("beta", CC),
    ("bf", 1), ("gf", 1), ("betaf", 1), ("mf", 1), ("vf", 1),
    ("bg", 1), ("gg", 1), ("betag", 1), ("mg", 1), ("vg", 1), ("bv2", CC),
    ("gtp_w", CC * 3), ("gtp_b", 1), ("W_w", CC), ("W_b", CC),
    ("bn_gamma", CC), ("bn_beta", CC), ("bn_mean", CC), ("bn_var", CC), ("se1_b", 1), ("se2_b", CC),
]
VCOL, VN = {}, 0
for _n, _w in _WIDTHS:
    VCOL[_n] = (VN, _w)
    VN += _w
_CWIDTHS = [("grid_x", J), ("grid_y", J), ("neg_ix", 1), ("neg_iy", PC), ("grid_q", W),
            ("mask_hi", 1), ("mask_lo", 1), ("ident", P)]
KCOL, KN = {}, 0
for _n, _w in _CWIDTHS:
    KCOL[_n] = (KN, _w)
    KN += _w

ROWS = 10


def flat(ap):
    n = ap.ndim - 1
    names = " ".join("abcdef"[:n])
    return ap.rearrange(f"p {names} -> p ({names})") if n > 1 else ap


def carver(*tensors):
    free = [[flat(t[:]), 0] for t in tensors]

    def room(shape):
        n = int(np.prod(shape[1:]))
        area = next(a for a in free if a[1] + n <= a[0].shape[-1])
        ap = area[0][0:shape[0], area[1]:area[1] + n]
        area[1] += n
        names = "abcdef"[:len(shape) - 1]
        if len(names) > 1:
            ap = ap.rearrange(f"p ({' '.join(names)}) -> p {' '.join(names)}", **dict(zip(names, shape[1:])))
        return ap

    return room


def place(nc, sb, name, shape, rounded_shape=None):
    at = -(-nc.sbuf_base // 32) * 32
    t = sb(name, shape)
    return t, nc.alloc_sbuf_tensor_at(f"{name}_r", rounded_shape or shape, F32R, offset=at)


def split_norm(K, n, tmp, hi_done, lo_done):
    nc, (b, t) = K.nc, divmod(n, NT)

    def high(c):
        nc.scalar.activation(K.xn2[n % 2][0][:, c], K.X[:, c, b, t * BANK:(t + 1) * BANK],
                             ACT.Identity, bias=K.v("bn2_b", c), scale=K.s2[:, c:c + 1]).then_inc(hi_done, 1)

    def low(c, dve, step):
        if n or c:
            dve.wait_ge(lo_done, n * CC + c)
        nc.vector.tensor_scalar(tmp[:], K.X[:, c, b, t * BANK:(t + 1) * BANK], K.s2[:, c:c + 1], K.v("bn2_b", c),
                                ALU.mult, ALU.add).then_inc(step, 1)
        dve.wait_ge(step, n * CC + c + 1)
        dve.wait_ge(hi_done, n * CC + c + 1)
        nc.vector.tensor_tensor(K.xn2[n % 2][1][:, c], tmp[:], K.xn2[n % 2][0][:, c].bitcast(F32), ALU.subtract).then_inc(lo_done, 1)

    return high, low


class Kit:

    def __init__(self, nc, ctx, dram):
        self.nc, self.ctx, self.dram = nc, ctx, dram

    def sem(self, name):
        return self.ctx.enter_context(self.nc.semaphore(name))

    def v(self, name, i=0, n=1, p0=0, p1=P):
        o, _ = VCOL[name]
        return self.vecs[p0:p1, o + i:o + i + n]

    def k(self, name, i=0, n=None, p0=0, p1=P):
        o, w = KCOL[name]
        return self.consts[p0:p1, o + i:o + i + (w if n is None else n)]


def tensors(nc, ctx):
    def sb(name, shape, dt=F32):
        return ctx.enter_context(nc.sbuf_tensor(name, shape, dt))

    def ps(name, shape):
        return ctx.enter_context(nc.psum_tensor(name, shape, F32))

    return sb, ps


def stage_front(K, sb, ps):
    nc = K.nc
    K.XN = sb("XN", [P, CC, B, HW])
    K.XT = sb("XT", [P, B * PC, C])
    s1 = sb("s1", [P, CC])
    K.QW = QW = sb("QW", [P, CC, P])
    K.KW = KW = sb("KW", [P, CC, P])
    K.VW = VW = sb("VW", [P, CC, DH])
    qps = [ps(f"qps{i}", [P, BANK]) for i in range(2)]
    tps = [ps(f"tps{i}", [P, CC, P]) for i in range(2)]
    small, x_in, zero = K.sem("small_loaded"), [K.sem(f"x_loaded{c}") for c in range(CC)], K.sem("front_zeroed")
    w_in, s1_ready, xn_ready = K.sem("front_weights"), K.sem("s1_ready"), K.sem("xn_ready")
    q_mm, q_out, t_mm, t_out = K.sem("q_mm"), K.sem("q_out"), K.sem("xt_mm"), K.sem("xt_out")
    d = K.dram
    with nc.Block() as block:
        @block.sync
        def _(sp):
            sp.dma_start(K.vecs[:], d["vecs"]).then_inc(small, 16)
            sp.dma_start(K.consts[:], d["consts"]).then_inc(small, 16)
            for c in range(CC):
                for b in range(B):
                    sp.dma_start(K.X[:, c, b], d["x"][b, c * P:(c + 1) * P, :]).then_inc(x_in[c], 16)
            sp.wait_ge(zero, 2)
            for h in range(HALF):
                half = slice(h * DH, (h + 1) * DH)
                sp.dma_start(QW[half, :, half], d["qwT"][half]).then_inc(w_in, 16)
                sp.dma_start(KW[half, :, half], d["kwT"][half]).then_inc(w_in, 16)
            sp.dma_start(VW[:], d["vwT"]).then_inc(w_in, 16)
            sp.wait_ge(w_in, 80)

        @block.gpsimd
        def _(pool):
            nc.gpsimd.memset(QW[:], 0.0).then_inc(zero, 1)
            nc.gpsimd.memset(KW[:], 0.0).then_inc(zero, 1)
            nc.gpsimd.memset(K.KBD[:], 0.0).then_inc(zero, 1)
            nc.gpsimd.memset(K.VBD[:], 0.0).then_inc(zero, 1)
            pool.wait_ge(zero, 4)

        @block.scalar
        def _(act):
            act.wait_ge(s1_ready, 1)
            for c in range(CC):
                act.wait_ge(x_in[c], 16 * B)
                nc.scalar.activation(flat(K.XN[:, c]), flat(K.X[:, c]), ACT.Identity,
                                     bias=K.v("bn1_b", c), scale=s1[:, c:c + 1]).then_inc(xn_ready, 1)
            for i in range(BLK * NT):
                blk, t = divmod(i, NT)
                act.wait_ge(q_mm, i + 1)
                nc.scalar.activation(K.Q[:, blk, t * BANK:(t + 1) * BANK], qps[i % 2][:], ACT.Copy).then_inc(q_out, 1)

        @block.tensor
        def _(pe):
            pe.wait_ge(w_in, 80)
            pe.wait_ge(small, 32)
            for i in range(BLK * NT):
                blk, t = divmod(i, NT)
                c, b = divmod(blk, B)
                pe.wait_ge(xn_ready, c + 1)
                if i >= 2:
                    pe.wait_ge(q_out, i - 1)
                nc.tensor.matmul(qps[i % 2][:], QW[:, c], K.XN[:, c, b, t * BANK:(t + 1) * BANK],
                                 start=True, stop=True).then_inc(q_mm, 1)
            for i in range(B * PC):
                b, ch = divmod(i, PC)
                if i >= 2:
                    pe.wait_ge(t_out, i - 1)
                for c in range(CC):
                    last = nc.tensor.transpose(tps[i % 2][:, c], K.XN[:, c, b, ch * P:(ch + 1) * P], K.k("ident"))
                last.then_inc(t_mm, 1)

        @block.vector
        def _(dve):
            dve.wait_ge(small, 32)
            nc.vector.tensor_scalar(s1[:], K.v("bn1_g", 0, CC), float(1.0 / np.sqrt(1.0 + EPS)), None,
                                    ALU.mult).then_inc(s1_ready, 1)
            for i in range(B * PC):
                dve.wait_ge(t_mm, i + 1)
                nc.vector.tensor_copy(K.XT[:, i], flat(tps[i % 2][:])).then_inc(t_out, 1)


def stage_offsets(K, sb, ps):
    nc = K.nc
    diag = [sb(f"dw_diag{i}", [P, P]) for i in range(4)]
    pwr = sb("pw_rep", [P, 2, P])
    gel = sb("dw_gelu", [P, BLK * J])
    NX = sb("NX", [P, 2, HALF * BLK, J])
    tmp = sb("off_tmp", [P, 2, HALF * BLK, J])
    GXY = K.GXY
    ops, acc = ps("off_ps", [P, 2, HALF, BANK]), ps("dw_ps", [P, BLK, HD, WD])
    taps = K.sem("conv_taps")
    conv, gelu_done, pw_mm, tanh_done, crd = (K.sem("conv_step"), K.sem("gelu_done"), K.sem("pw_mm"),
                                              K.sem("tanh_done"), K.sem("coord_step"))
    nx_dram = K.sem("nx_stored")
    nt_in = K.nt_in = K.sem("nt_loaded")
    dn = nc.dram_tensor("nx_scratch", (2, HALF, BLK, J), F32).ap()
    with nc.Block() as block:
        @block.vector
        def _(dve):
            nc.vector.tensor_copy(pwr[:], K.v("pw", 0, 2).unsqueeze(2).to_broadcast([P, 2, P])).then_inc(conv, 1)
            for n in range(KS * KS):
                if n >= 4:
                    dve.wait_ge(taps, n - 3)
                nc.vector.tensor_scalar(diag[n % 4][:], K.k("ident"), K.v("dw_w", TAPS[n]), None, ALU.mult).then_inc(conv, 1)
            dve.wait_ge(tanh_done, 1)
            for axis, grid in enumerate(("grid_x", "grid_y")):
                nc.vector.scalar_tensor_tensor(tmp[:, axis], NX[:, axis], OFF_SCALE,
                                               K.k(grid).unsqueeze(1).to_broadcast([P, HALF * BLK, J]),
                                               ALU.mult, ALU.add).then_inc(crd, 1)
            dve.wait_ge(crd, 2)
            nc.vector.tensor_scalar(GXY[:], tmp[:], 2.0, 1.0 / (HD - 1), ALU.mult, ALU.mult).then_inc(crd, 1)
            dve.wait_ge(crd, 3)
            nc.vector.tensor_scalar(NX[:], GXY[:], -1.0, None, ALU.add).then_inc(crd, 1)
            dve.wait_ge(crd, 4)
            nc.vector.tensor_scalar(tmp[:], NX[:], 1.0, W / 2.0, ALU.add, ALU.mult).then_inc(crd, 1)
            dve.wait_ge(crd, 5)
            nc.vector.tensor_scalar(GXY[:], tmp[:], -0.5, None, ALU.add).then_inc(crd, 1)
            dve.wait_ge(crd, 6)

        @block.scalar
        def _(act):
            act.wait_ge(taps, KS * KS)
            nc.scalar.activation(gel[:], flat(acc[:]), ACT.Gelu, bias=K.v("dw_b")).then_inc(gelu_done, 1)
            act.wait_ge(pw_mm, 1)
            nc.scalar.activation(NX[:].rearrange("p a (h k) j -> p a h (k j)", h=HALF), ops[:], ACT.Tanh).then_inc(tanh_done, 1)

        @block.tensor
        def _(pe):
            q = K.Q[:].rearrange("p k (y x) -> p k y x", x=W)
            for n, tap in enumerate(TAPS):
                (y0, y1), (x0, x1) = ((int(k == 0), HD - int(k == KS - 1)) for k in divmod(tap, KS))
                ky, kx = divmod(tap, KS)
                iy, ix = DF * y0 + ky - 1, DF * x0 + kx - 1
                pe.wait_ge(conv, n + 2)
                last = nc.tensor.matmul(acc[:, :, y0:y1, x0:x1], diag[n % 4][:],
                                        q[:, :, iy:iy + DF * (y1 - y0 - 1) + 1:DF, ix:ix + DF * (x1 - x0 - 1) + 1:DF],
                                        start=(n == 0), stop=(n == KS * KS - 1))
                last.then_inc(taps, 1)
            pe.wait_ge(gelu_done, 1)
            for axis in range(2):
                for h in range(HALF):
                    half = slice(h * DH, (h + 1) * DH)
                    last = nc.tensor.matmul(ops[:, axis, h], pwr[half, axis], gel[half, :], start=True, stop=True)
            last.then_inc(pw_mm, 1)

        @block.sync
        def _(sp):
            sp.wait_ge(crd, 4)
            sp.dma_start(dn.rearrange("a h k j -> (a h k j)").unsqueeze(0), NX[0:1].rearrange("p a k j -> p (a k j)")).then_inc(nx_dram, 16)
            sp.wait_ge(nx_dram, 16)
            for axis in range(2):
                for h in range(HALF):
                    sp.dma_start(K.nt[axis * BG + h:axis * BG + BG:HALF, :], dn[axis, h]).then_inc(nt_in, 16)
            sp.wait_ge(nt_in, 64)


def stage_tables(K, sb, ps):
    nc = K.nc
    n_ax = 2 * BG
    th = sb("tab_hi", [n_ax, W, J], F32R)
    tl = sb("tab_lo", [n_ax, W, J], F32R)
    wt = K.XN[:].rearrange("p c b n -> p (c b n)").rearrange("p (s n) -> p s n", s=PC)
    SAMP = HALF * BLK * J
    pos, lg, sg = (wt[0:n_ax, 2 * i:2 * i + 2].rearrange("p s n -> p (s n)").rearrange("p (y j) -> p y j", j=J) for i in range(3))
    tx = sb("tent_x", [P, SAMP])
    ty = [sb(f"tent_y{i}", [P, SAMP]) for i in range(2)]
    kv = sb("kv", [P, BLK, J])
    w1raw, w1h, w1l, w1t = (sb("w1raw", [ROWS, BIASF]), sb("w1h", [ROWS, BIASF], F32R),
                            sb("w1l", [ROWS, BIASF], F32R), sb("w1t", [ROWS, BIASF]))
    w2raw = sb("w2raw", [P, BIASF])
    kvps, kps, vps = ps("kv_ps", [P, BLK, J]), ps("k_ps", [P, BLK, J]), ps("v_ps", [P, BLK, J])
    tab, axd, absd, tyd, wtd = (K.sem("tab_step"), K.sem("act_pos"), K.sem("act_dist"), K.sem("act_tent"), K.sem("w_tent"))
    kv_mm, kv_out, k_mm, v_mm, kb_out = (K.sem("kv_mm"), K.sem("kv_out"), K.sem("k_mm"), K.sem("v_mm"), K.sem("kvbd_out"))
    cw_in, cw, tab_out = K.sem("cpb_w_loaded"), K.sem("cpb_w_step"), K.sem("tab_stored")
    d = K.dram
    with nc.Block() as block:
        @block.sync
        def _(sp):
            sp.dma_start(w1raw[:], d["cpb_w1r"]).then_inc(cw_in, 16)
            sp.dma_start(w2raw[:], d["cpb_w2"]).then_inc(cw_in, 16)
            sp.wait_ge(tab, 6)
            for part, t in enumerate((th, tl)):
                sp.dma_start(K.dx[:, part], t[0:BG].bitcast(F32)).then_inc(tab_out, 16)
                sp.dma_start(K.dy[:, part].rearrange("(g c) y j -> g c (y j)", g=BG),
                             t[BG:n_ax].bitcast(F32).rearrange("g (c y) j -> g c (y j)", y=2)).then_inc(tab_out, 16)
            sp.wait_ge(tab_out, 64)

        @block.vector
        def _(dve):
            nc.vector.tensor_tensor(pos, K.k("grid_q", p1=n_ax).unsqueeze(2).to_broadcast([n_ax, W, J]),
                                    K.nt[:].unsqueeze(1).to_broadcast([n_ax, W, J]), ALU.subtract).then_inc(tab, 1)
            dve.wait_ge(tab, 1)
            nc.vector.tensor_scalar(sg, pos, 0.0, 2.0, ALU.is_ge, ALU.mult).then_inc(tab, 1)
            dve.wait_ge(axd, 2)
            dve.wait_ge(tab, 2)
            nc.vector.scalar_tensor_tensor(pos, sg, -1.0, lg, ALU.add, ALU.mult).then_inc(tab, 1)
            dve.wait_ge(tab, 3)
            nc.vector.tensor_copy(th[:], pos).then_inc(tab, 1)
            dve.wait_ge(tab, 4)
            nc.vector.tensor_tensor(tl[:], pos, th[:].bitcast(F32), ALU.subtract).then_inc(tab, 1)
            dve.wait_ge(tab, 5)
            for s in range(PC):
                dve.wait_ge(tyd, s + 2)
                ins = nc.vector.tensor_tensor(wt[:, s], ty[s % 2][:], tx[:], ALU.mult)
                ins.then_inc(wtd, 1)
                if s == 0:
                    nc.vector.tensor_copy(K.W3[:], K.v("cpb_w3").to_broadcast([P, 32])).then_inc(tab, 1)
            dve.wait_ge(cw_in, 32)
            nc.vector.tensor_copy(w1h[:], w1raw[:]).then_inc(cw, 1)
            nc.vector.tensor_copy(K.W2H[:], w2raw[:]).then_inc(cw, 1)
            dve.wait_ge(cw, 2)
            nc.vector.tensor_tensor(w1l[:], w1raw[:], w1h[:].bitcast(F32), ALU.subtract).then_inc(cw, 1)
            nc.vector.tensor_tensor(K.W2L[:], w2raw[:], K.W2H[:].bitcast(F32), ALU.subtract).then_inc(cw, 1)
            dve.wait_ge(cw, 4)
            nc.vector.tensor_scalar(w1t[:], w1l[:].bitcast(F32), K.k("mask_lo", p1=ROWS), None, ALU.mult).then_inc(cw, 1)
            dve.wait_ge(cw, 5)
            for par in range(2):
                nc.vector.scalar_tensor_tensor(K.W1R[32 * par:32 * par + ROWS], w1h[:].bitcast(F32), K.k("mask_hi", p1=ROWS), w1t[:],
                                               ALU.mult, ALU.add).then_inc(cw, 1)
            dve.wait_ge(kv_mm, 1)
            nc.vector.tensor_copy(kv[:], kvps[:]).then_inc(kv_out, 1)
            dve.wait_ge(k_mm, 1)
            for h in range(HALF):
                half = slice(h * DH, (h + 1) * DH)
                nc.vector.tensor_scalar(K.KBD[half, :, half], kps[half], float(DH) ** -0.5, None, ALU.mult).then_inc(kb_out, 1)
            dve.wait_ge(v_mm, 1)
            for h in range(HALF):
                half = slice(h * DH, (h + 1) * DH)
                nc.vector.tensor_copy(K.VBD[half, :, half], vps[half]).then_inc(kb_out, 1)
            dve.wait_ge(kb_out, 4)
            dve.wait_ge(cw, 7)

        @block.scalar
        def _(act):
            act.wait_ge(tab, 1)
            nc.scalar.activation(lg, pos, ACT.Abs).then_inc(axd, 1)
            act.wait_ge(axd, 1)
            nc.scalar.activation(lg, lg, ACT.Ln, bias=1.0).then_inc(axd, 1)
            gx, gy = (K.GXY[:, a].rearrange("p k j -> p (k j)") for a in range(2))
            for s in range(-1, PC):
                if s >= 1:
                    act.wait_ge(wtd, s - 1)
                to = tx[:] if s < 0 else ty[s % 2][:]
                nc.scalar.activation(to, gx if s < 0 else gy, ACT.Abs,
                                     bias=K.k("neg_ix") if s < 0 else K.k("neg_iy", s, 1)).then_inc(absd, 1)
                act.wait_ge(absd, s + 2)
                nc.scalar.activation(to, to, ACT.Relu,
                                     bias=1.0, scale=-1.0).then_inc(tyd, 1)

        @block.tensor
        def _(pe):
            pe.wait_ge(wtd, PC)
            for blk in range(BLK):
                c, b = divmod(blk, B)
                for h in range(HALF):
                    for s in range(PC):
                        ch0 = c * P + h * DH
                        smp = (h * BLK + blk) * J
                        last = nc.tensor.matmul(kvps[h * DH:(h + 1) * DH, blk], K.XT[:, b * PC + s, ch0:ch0 + DH],
                                                wt[:, s, smp:smp + J], start=(s == 0), stop=(s == PC - 1))
            last.then_inc(kv_mm, 1)
            pe.wait_ge(kv_out, 1)
            for c in range(CC):
                last = nc.tensor.matmul(flat(kps[:, B * c:B * c + B]), K.KW[:, c], flat(kv[:, B * c:B * c + B]), start=True, stop=True)
            last.then_inc(k_mm, 1)
            for blk in range(BLK):
                for h in range(HALF):
                    half = slice(h * DH, (h + 1) * DH)
                    last = nc.tensor.matmul(vps[half, blk], kv[half, blk], K.VW[half, blk // B], start=True, stop=True)
            last.then_inc(v_mm, 1)


def stage_bias(K, sb, ps):
    nc = K.nc
    TILE = 1024
    QROW = W * J
    CHUNK = 2 * QROW
    N = BG * HW * J // (2 * CHUNK)
    S_all = sb("S", [32 + ROWS, 2, W, J], F32R)
    S = [S_all[32 * i:32 * i + ROWS] for i in range(2)]
    hh = [sb(f"h1_hi{i}", [P, TILE], F32R) for i in range(2)]
    hl = [sb(f"h1_lo{i}", [P, TILE], F32R) for i in range(2)]
    h2 = [sb(f"h2_{i}", [P, QROW]) for i in range(2)]
    br = [sb(f"bias_rows{i}", [P, 2, BANK]) for i in range(2)]
    p1 = [ps(f"l1_ps{i}", [P, TILE]) for i in range(2)]
    p2 = [ps(f"l2_ps{i}", [P, BANK]) for i in range(3)]
    p3 = ps("l3_ps", [P, BANK])
    ones = K.sem("s_ones")
    s_in, rows_out = [K.sem(f"s_loaded{i}") for i in range(2)], [K.sem(f"rows_stored{i}") for i in range(2)]
    l1, hi_done, lo_done, l2 = K.sem("l1_mm"), K.sem("hi_done"), K.sem("lo_done"), K.sem("l2_mm")
    relu_a, relu_b, l3, copied = K.sem("relu_a"), K.sem("relu_b"), K.sem("l3_mm"), K.sem("rows_copied")
    with nc.Block() as block:
        @block.vector
        def _(dve):
            nc.vector.memset(S_all[:].bitcast(F32), 1.0).then_inc(ones, 1)
            dve.wait_ge(ones, 1)
    LOADS = 6 * 16
    with nc.Block() as block:
        @block.sync
        def _(sp):
            def load(it, bg, k):
                for dup in range(2):
                    sp.dma_start(S[k][2 * dup:2 * dup + 2].bitcast(F32).rearrange("r q a j -> r q (a j)"),
                                 K.dx[bass.ds(bg, 1)].squeeze(0).rearrange("r a j -> r (a j)").unsqueeze(1)
                                 .to_broadcast([2, 2, QROW])).then_inc(s_in[k], 16)
                    for q in range(2):
                        sp.dma_start(S[k][4 + 2 * dup:6 + 2 * dup, q].bitcast(F32),
                                     K.dy[bass.ds(it * 2 + k, 1), :, q].squeeze(0).unsqueeze(1)
                                     .to_broadcast([2, W, J])).then_inc(s_in[k], 16)
            load(0, 0, 0)
            load(0, 0, 1)
            with sp.Fori(1, N) as it:
                for k in range(2):
                    sp.wait_ge(l1, it * 8 + 4 * k - 4)
                    load(it, it // 8, k)

        @block.tensor
        def _(pe):
            def layer_one(u):
                k, q, part = (u // 4) % 2, (u // 2) % 2, u % 2
                row = S[k][:, q].rearrange("r a j -> r (a j)")
                for a in range(2):
                    at = TILE * part + BANK * a
                    last = nc.tensor.matmul(p1[u % 2][:, BANK * a:BANK * (a + 1)], K.W1R[32 * k:32 * k + ROWS], row[:, at:at + BANK],
                                            start=True, stop=True)
                last.then_inc(l1, 1)

            def layer_three(par):
                for g in range(4):
                    last = nc.tensor.matmul(p3[32 * g:32 * g + 32, :], K.W3[:], h2[par][:, BANK * g:BANK * (g + 1)],
                                            start=True, stop=True, tile_position=(0, 32 * g))
                last.then_inc(l3, 1)

            pe.wait_ge(s_in[0], LOADS)
            layer_one(0)
            layer_one(1)

            def body(it, first, last):
                for u in range(8):
                    t = it * 8 + u
                    pe.wait_ge(hi_done, t + 1)
                    out = (p2[u % 2], p2[2])
                    for a in range(2):
                        if a == 0 and not (first and u < 2):
                            pe.wait_ge(relu_a, t - 1)
                        if a == 1 and not (first and u == 0):
                            pe.wait_ge(relu_b, t)
                        h = hh[u % 2][:, BANK * a:BANK * (a + 1)]
                        nc.tensor.matmul(out[a][:], K.W2H[:], h, start=True, stop=False)
                        nc.tensor.matmul(out[a][:], K.W2L[:], h, start=False, stop=False)
                        if a == 0:
                            pe.wait_ge(lo_done, t + 1)
                        nc.tensor.matmul(out[a][:], K.W2H[:], hl[u % 2][:, BANK * a:BANK * (a + 1)],
                                         start=False, stop=True).then_inc(l2, 1)
                    if not (last and u >= 6):
                        if u == 2:
                            pe.wait_ge(s_in[1], (it + 1) * LOADS)
                        if u == 6:
                            pe.wait_ge(s_in[0], (it + 2) * LOADS)
                        layer_one((u + 2) % 8)
                    if u % 2 == 0 and not (first and u == 0):
                        pe.wait_ge(relu_a, t)
                        pe.wait_ge(relu_b, t)
                        if not (first and u == 2):
                            pe.wait_ge(copied, it * 4 + u // 2 - 1)
                        layer_three((u // 2 - 1) % 2)

            body(0, True, False)
            with pe.Fori(1, N - 1) as it:
                body(it, False, False)
            body(N - 1, False, True)
            pe.wait_ge(relu_a, N * 8)
            pe.wait_ge(relu_b, N * 8)
            pe.wait_ge(copied, N * 4 - 1)
            layer_three(1)

        @block.scalar
        def _(act):
            def high(it, u):
                act.wait_ge(l1, it * 8 + u + 1)
                nc.scalar.activation(hh[u % 2][:], p1[u % 2][:], ACT.Relu).then_inc(hi_done, 1)

            def copy_rows(it, row, first):
                act.wait_ge(l3, it * 4 + row + 1)
                k = row // 2
                if row % 2 == 0 and not first:
                    act.wait_ge(rows_out[k], it * 16)
                nc.scalar.activation(br[k][:, row % 2, :], p3[:], ACT.Identity, bias=K.v("cpb_b3")).then_inc(copied, 1)

            high(0, 0)
            high(0, 1)

            def body(it, first, last):
                for u in range(8):
                    t = it * 8 + u
                    act.wait_ge(l2, t * 2 + 2)
                    if not first or u >= 4:
                        act.wait_ge(l3, it * 4 + u // 2 - 1)
                    at = (u % 2) * TILE + BANK
                    nc.scalar.activation(h2[(u // 2) % 2][:, at:at + BANK], p2[2][:], ACT.Relu,
                                         bias=K.v("cpb_b2")).then_inc(relu_b, 1)
                    if not (last and u >= 6):
                        high(it if u < 6 else it + 1, (u + 2) % 8)
                    if u % 2 == 0 and not (first and u == 0):
                        if u == 0:
                            copy_rows(it - 1, 3, False)
                        else:
                            copy_rows(it, u // 2 - 1, first)

            body(0, True, False)
            with act.Fori(1, N - 1) as it:
                body(it, False, False)
            body(N - 1, False, True)
            copy_rows(N - 1, 3, False)

        @block.vector
        def _(dve):
            def low(it, u):
                dve.wait_ge(hi_done, it * 8 + u + 1)
                nc.vector.scalar_tensor_tensor(hl[u % 2][:], p1[u % 2][:], 0.0, hh[u % 2][:].bitcast(F32),
                                               ALU.max, ALU.subtract).then_inc(lo_done, 1)

            low(0, 0)
            low(0, 1)

            def body(it, first, last):
                for u in range(8):
                    t = it * 8 + u
                    dve.wait_ge(l2, t * 2 + 1)
                    if not first or u >= 4:
                        dve.wait_ge(l3, it * 4 + u // 2 - 1)
                    at = (u % 2) * TILE
                    nc.vector.tensor_scalar(h2[(u // 2) % 2][:, at:at + BANK], p2[u % 2][:], K.v("cpb_b2"), 0.0,
                                            ALU.add, ALU.max).then_inc(relu_a, 1)
                    if not (last and u >= 6):
                        low(it if u < 6 else it + 1, (u + 2) % 8)

            body(0, True, False)
            with dve.Fori(1, N - 1) as it:
                body(it, False, False)
            body(N - 1, False, True)

        @block.gpsimd
        def _(pool):
            with pool.Fori(0, N) as it:
                for k in range(2):
                    pool.wait_ge(copied, it * 4 + 2 * k + 2)
                    pool.dma_start(K.db[bass.ds(it * 2 + k, 1)].squeeze(0).rearrange("q g n -> g q n"),
                                   br[k][0:P:32]).then_inc(rows_out[k], 16)
            for k in range(2):
                pool.wait_ge(rows_out[k], 16 * N)


def stage_attention(K, sb, ps):
    nc = K.nc
    room = carver(K.HA)
    bi = [room([P, HALF, PC, J]) for _ in range(2)]
    sc = [room([P, PC, HALF, J]) for _ in range(3)]
    at = room([P, HW])
    pr = [room([P, PC, HALF, J]) for _ in range(2)]
    OW = K.OW = carver(K.XNB)([P, CC, C])
    mx, sm, rs = sb("smax", [P, PC * HALF]), sb("ssum", [P, PC * HALF]), sb("srec", [P, PC * HALF])
    sps = [ps(f"score_ps{i}", [P, PC, P]) for i in range(2)]
    tps, ops = ps("probsT_ps", [P, HW]), ps("att_ps", [P, HW])
    b_in, s_mm, ex = [K.sem(f"bias_in{i}") for i in range(2)], K.sem("score_mm"), K.sem("soft_exp")
    added, peaked, shifted, summed, recip, scaled = (K.sem("bias_added"), K.sem("soft_max"), K.sem("soft_shift"),
                                                     K.sem("soft_sum"), K.sem("soft_recip"), K.sem("soft_scaled"))
    t_mm, t_out, o_mm, o_out = K.sem("probsT_mm"), K.sem("probsT_out"), K.sem("att_mm"), K.sem("att_out")
    ow_in = K.ow_in = K.sem("out_w_loaded")

    def rows(t):
        return t[:].rearrange("p s h j -> p (s h) j")

    def wide(t):
        return t[:].unsqueeze(2).to_broadcast([P, PC * HALF, J])

    with nc.Block() as block:
        @block.sync
        def _(sp):
            for g in range(BLK):
                if g >= 2:
                    sp.wait_ge(added, g - 1)
                for h in range(HALF):
                    sp.dma_start(bi[g % 2][:, h], K.db_bg[HALF * g + h].rearrange("(s p) j -> p s j", p=P)).then_inc(b_in[g % 2], 16)
            sp.dma_start(OW, K.dram["out_wT"]).then_inc(ow_in, 16)

        @block.tensor
        def _(pe):
            for k in range(BLK + 3):
                if k < BLK:
                    if k >= 2:
                        pe.wait_ge(added, k - 1)
                    for s in range(PC):
                        last = nc.tensor.matmul(sps[k % 2][:, s], K.Q[:, k, s * P:(s + 1) * P], K.KBD[:, k], start=True, stop=True)
                    last.then_inc(s_mm, 1)
                if k >= 3:
                    g = k - 3
                    pe.wait_ge(t_out, g + 1)
                    if g >= 1:
                        pe.wait_ge(o_out, g)
                    for t in range(NT):
                        last = nc.tensor.matmul(ops[:, t * BANK:(t + 1) * BANK], K.VBD[:, g], at[:, t * BANK:(t + 1) * BANK],
                                                start=True, stop=True)
                    last.then_inc(o_mm, 1)
                if 2 <= k < BLK + 2:
                    g = k - 2
                    pe.wait_ge(scaled, g + 1)
                    if g >= 1:
                        pe.wait_ge(t_out, g)
                    for s in range(PC):
                        last = nc.tensor.transpose(tps[:, s * P:(s + 1) * P], pr[g % 2][:, s].rearrange("p h j -> p (h j)"), K.k("ident"))
                    last.then_inc(t_mm, 1)

        @block.vector
        def _(dve):
            for k in range(BLK + 1):
                if k < BLK:
                    dve.wait_ge(s_mm, k + 1)
                    dve.wait_ge(b_in[k % 2], 16 * HALF * (k // 2 + 1))
                    if k >= 3:
                        dve.wait_ge(scaled, k - 2)
                    nc.vector.tensor_tensor(sc[k % 3], sps[k % 2][:].rearrange("p s (h j) -> p s h j", h=HALF),
                                            bi[k % 2].rearrange("p h s j -> p s h j"), ALU.add).then_inc(added, 1)
                    dve.wait_ge(added, k + 1)
                    if k:
                        dve.wait_ge(shifted, k)
                    nc.vector.tensor_reduce(mx[:], rows(sc[k % 3]), AX.X, ALU.max).then_inc(peaked, 1)
                if k:
                    g = k - 1
                    dve.wait_ge(ex, g + 1)
                    nc.vector.tensor_reduce(sm[:], rows(sc[g % 3]), AX.X, ALU.add).then_inc(summed, 1)
                    dve.wait_ge(summed, g + 1)
                    nc.vector.reciprocal(rs[:], sm[:]).then_inc(recip, 1)
                    dve.wait_ge(recip, g + 1)
                    if g >= 2:
                        dve.wait_ge(t_mm, g - 1)
                    nc.vector.tensor_tensor(rows(pr[g % 2]), rows(sc[g % 3]), wide(rs), ALU.mult).then_inc(scaled, 1)

        @block.gpsimd
        def _(pool):
            for g in range(BLK):
                pool.wait_ge(peaked, g + 1)
                nc.gpsimd.tensor_tensor(rows(sc[g % 3]), rows(sc[g % 3]), wide(mx), ALU.subtract).then_inc(shifted, 1)

        @block.scalar
        def _(act):
            for k in range(1, BLK + 4):
                if k >= 4:
                    act.wait_ge(o_mm, k - 3)
                    nc.scalar.activation(K.Q[:, k - 4], ops[:], ACT.Copy).then_inc(o_out, 1)
                if k <= BLK:
                    act.wait_ge(shifted, k)
                    e = flat(sc[(k - 1) % 3][:])
                    nc.scalar.activation(e, e, ACT.Exp).then_inc(ex, 1)
                if 3 <= k < BLK + 3:
                    act.wait_ge(t_mm, k - 2)
                    if k >= 4:
                        act.wait_ge(o_mm, k - 3)
                    nc.scalar.activation(at, tps[:], ACT.Copy).then_inc(t_out, 1)


def stage_out_proj(K, sb, ps):
    nc = K.nc
    AO = K.Q[:].rearrange("p (c b) n -> p c b n", b=B)
    OW = K.OW
    pp = [ps(f"proj_ps{i}", [P, BANK]) for i in range(4)]
    mm, out, s2d, wh_done, wl_done = K.sem("proj_mm"), K.sem("proj_out"), K.sem("s2_ready"), K.sem("w_hi_done"), K.sem("w_lo_done")
    K.xh_done, K.xl_done, K.x_step = K.sem("xn2_hi_done"), K.sem("xn2_lo_done"), K.sem("xn2_step")
    x_high, x_low = split_norm(K, 0, ps("norm_ps", [P, BANK]), K.xh_done, K.xl_done)
    with nc.Block() as block:
        @block.tensor
        def _(pe):
            pe.wait_ge(K.ow_in, 16)
            for i in range(B * NT * CC):
                bt, o = divmod(i, CC)
                b, t = divmod(bt, NT)
                if i >= 4:
                    pe.wait_ge(out, i - 3)
                for c in range(CC):
                    last = nc.tensor.matmul(pp[i % 4][:], OW[:, c, o * P:(o + 1) * P], AO[:, c, b, t * BANK:(t + 1) * BANK],
                                            start=(c == 0), stop=(c == CC - 1))
                last.then_inc(mm, 1)

        @block.vector
        def _(dve):
            nc.vector.tensor_scalar(K.s2[:], K.v("bn2_g", 0, CC), float(1.0 / np.sqrt(1.0 + EPS)), None,
                                    ALU.mult).then_inc(s2d, 1)
            dve.wait_ge(s2d, 1)
            for i in range(B * NT * CC):
                bt, o = divmod(i, CC)
                b, t = divmod(bt, NT)
                x = K.X[:, o, b, t * BANK:(t + 1) * BANK]
                dve.wait_ge(mm, i + 1)
                nc.vector.scalar_tensor_tensor(x, pp[i % 4][:], K.v("out_b", o), x, ALU.add, ALU.add).then_inc(out, 1)
                if bt == 1:
                    x_low(o, dve, K.x_step)
                if i % 2:
                    f = i // 2
                    dve.wait_ge(wh_done, f + 1)
                    nc.vector.tensor_tensor(flat(K.w_lo[:, f]), flat(K.WR[:, f]), flat(K.w_hi[:, f]).bitcast(F32),
                                            ALU.subtract).then_inc(wl_done, 1)

        @block.scalar
        def _(act):
            act.wait_ge(K.mlp_in, 16)
            act.wait_ge(s2d, 1)
            for f in range(FC // 2):
                nc.scalar.activation(flat(K.w_hi[:, f]), flat(K.WR[:, f]), ACT.Copy).then_inc(wh_done, 1)
                if f >= CC:
                    act.wait_ge(out, f - CC + 1)
                    x_high(f - CC)


def stage_mlp(K, sb, ps):
    nc = K.nc
    parts = [(K.w_hi[:, f] if f < FC // 2 else K.w_hi2[:, f - FC // 2], K.w_lo[:, f]) for f in range(FC)]
    hid = [(s[:, 0], s[:, 1]) for s in K.hid]
    SLOTS = len(hid)
    pa = [ps(f"mlp_ps{i}", [P, BANK]) for i in range(3)]
    pb = [ps(f"mlp_out_ps{i}", [P, BANK]) for i in range(CC)]
    tmp = ps("norm_ps2", [P, BANK])
    m1, ge, lo_done, m2, out, w_step = (K.sem("mlp1_mm"), K.sem("mlp_gelu"), K.sem("hidden_lo"), K.sem("mlp2_mm"),
                                        K.sem("mlp_out"), K.sem("w_split"))
    PAIRS = ((0, 0), (1, 0), (0, 1))
    N = B * NT * FC
    NORM = range(4, 4 + CC)
    room = carver(K.HA)
    K.lin_w = [room([P, CC, C]) for _ in range(4)]
    K.lin_b = [flat(K.XNA[:])[:, i * C:(i + 1) * C] for i in range(2)]
    K.lin_in = K.sem("l1_w_loaded")
    with nc.Block() as block:
        @block.sync
        def _(sp):
            sp.wait_ge(m2, N - FC // 2)
            for t, n in zip(K.lin_w, ("WqT", "WvT", "Wk", "WoT")):
                sp.dma_start(t, K.dram[n]).then_inc(K.lin_in, 16)
            for t, n in zip(K.lin_b, ("bq", "bv")):
                sp.dma_start(t, K.dram[n].partition_broadcast(P)).then_inc(K.lin_in, 16)

        @block.gpsimd
        def _(pool):
            for f in range(FC // 2, FC):
                hi, lo = (flat(w) for w in parts[f])
                nc.gpsimd.tensor_copy(hi, flat(K.WR[:, f])).then_inc(w_step, 1)
                pool.wait_ge(w_step, 2 * (f - FC // 2) + 1)
                nc.gpsimd.tensor_tensor(lo, flat(K.WR[:, f]), hi.bitcast(F32), ALU.subtract).then_inc(w_step, 1)

        @block.tensor
        def _(pe):
            def hidden(n):
                bt, f = divmod(n, FC)
                if f == 0 and bt:
                    pe.wait_ge(K.xl_done, CC * (bt + 1))
                if bt == 0 and f >= FC // 2:
                    pe.wait_ge(w_step, 2 * (f - FC // 2) + 2)
                if n >= 3:
                    pe.wait_ge(lo_done, n - 2)
                for c in range(CC):
                    for i, (w, x) in enumerate(PAIRS):
                        last = nc.tensor.matmul(pa[n % 3][:], parts[f][w][:, 0, c * P:(c + 1) * P],
                                                K.xn2[bt % 2][x][:, c],
                                                start=(c == 0 and i == 0), stop=(c == CC - 1 and i == 2))
                last.then_inc(m1, 1)

            def gather(n):
                bt, f = divmod(n, FC)
                pe.wait_ge(lo_done, n + 1)
                for o in range(CC):
                    if f == 0 and bt:
                        pe.wait_ge(out, (bt - 1) * CC + o + 1)
                    for i, (w, x) in enumerate(PAIRS):
                        last = nc.tensor.matmul(pb[o][:], parts[f][w][:, 1, o * P:(o + 1) * P],
                                                hid[n % SLOTS][x],
                                                start=(f == 0 and i == 0), stop=(f == FC - 1 and i == 2))
                last.then_inc(m2, 1)

            hidden(0)
            for n in range(N):
                if n + 1 < N:
                    hidden(n + 1)
                gather(n)

        @block.scalar
        def _(act):
            for n in range(N):
                bt, f = divmod(n, FC)
                act.wait_ge(m1, n + 1)
                if n >= SLOTS:
                    act.wait_ge(m2, n - SLOTS + 1)
                nc.scalar.activation(hid[n % SLOTS][0], pa[n % 3][:], ACT.Gelu, bias=K.v("mlp_b1", f))
                nc.scalar.activation(pa[n % 3][:], pa[n % 3][:], ACT.Gelu, bias=K.v("mlp_b1", f)).then_inc(ge, 1)
                if f in NORM and bt + 1 < B * NT:
                    split_norm(K, bt + 1, tmp, K.xh_done, K.xl_done)[0](f - NORM[0])

        @block.vector
        def _(dve):
            def add(bt):
                b, t = divmod(bt, NT)
                dve.wait_ge(m2, (bt + 1) * FC)
                for o in range(CC):
                    x = K.X[:, o, b, t * BANK:(t + 1) * BANK]
                    nc.vector.scalar_tensor_tensor(x, pb[o][:], K.v("mlp_b2", o), x, ALU.add, ALU.add).then_inc(out, 1)

            for n in range(N):
                bt, f = divmod(n, FC)
                hi, lo = hid[n % SLOTS]
                dve.wait_ge(ge, n + 1)
                nc.vector.tensor_tensor(lo, pa[n % 3][:], hi.bitcast(F32), ALU.subtract).then_inc(lo_done, 1)
                if f == 0 and bt:
                    add(bt - 1)
                if f in NORM and bt + 1 < B * NT:
                    split_norm(K, bt + 1, tmp, K.xh_done, K.xl_done)[1](f - NORM[0], dve, K.x_step)
            add(B * NT - 1)


def stage_linear(K, sb, ps):
    nc = K.nc
    d = K.dram
    wq, wv, wk, wo = K.lin_w
    bqr, bvr = K.lin_b
    room = carver(K.WR)
    kt, vt = room([P, PC, C]), room([P, PC, C])
    mt, aT, tt = room([P, CC, P]), room([P, CC, C]), room([P, CC, C])
    bb = sb("lin_bias", [P, CC])
    Y = carver(K.Q)([P, CC, B, HW])
    st = sb("bn_st", [P, CC, B * NT, 6])
    mv, inv, sh = sb("bn_mv", [P, CC, 2]), sb("bn_inv", [P, CC]), sb("bn_sh", [P, CC])
    kps, vps = [ps(f"kt_ps{i}", [P, BANK]) for i in range(2)], [ps(f"vt_ps{i}", [P, BANK]) for i in range(2)]
    mps, bps = ps("m_ps", [P, CC, P]), ps("b_ps", [P, CC])
    yps = [ps(f"y_ps{i}", [P, BANK]) for i in range(2)]
    w_in, zero = K.lin_in, K.sem("mt_zeroed")
    kv_mm, k_out, v_out, m_mm, m_out = K.sem("ktvt_mm"), K.sem("kt_out"), K.sem("vt_out"), K.sem("m_mm"), K.sem("m_out")
    g_mm, g_out, b_mm, b_out = K.sem("fold_mm"), K.sem("fold_out"), K.sem("foldb_mm"), K.sem("foldb_out")
    y_mm, y_out, s_step, sq, nrm = K.sem("lin_mm"), K.sem("lin_out"), K.sem("bn_step"), K.sem("bn_sqrt"), K.sem("bn_done")
    with nc.Block() as block:
        @block.sync
        def _(sp):
            for t, n in zip(K.fgh_w, ("wfT", "wgT", "whT")):
                sp.dma_start(t, d[n]).then_inc(K.nl_in, 16)
            sp.dma_start(K.nl_wv, d["wvT"]).then_inc(K.nl_in, 16)
            sp.dma_start(K.bhr[:], d["bh"].partition_broadcast(P)).then_inc(K.nl_in, 16)
            sp.dma_start(K.se1[:], d["se1_wT"]).then_inc(K.se_in, 16)
            sp.dma_start(K.se2[:], d["se2_wT"]).then_inc(K.se_in, 16)

        @block.gpsimd
        def _(pool):
            nc.gpsimd.memset(mt, 0.0).then_inc(zero, 1)

        @block.tensor
        def _(pe):
            pe.wait_ge(w_in, 96)
            for b in range(B):
                for s in range(PC):
                    n = b * PC + s
                    if n >= 2:
                        pe.wait_ge(k_out, n - 1)
                        pe.wait_ge(v_out, n - 1)
                    for w, t in ((wq, kps), (wv, vps)):
                        for c in range(CC):
                            last = nc.tensor.matmul(t[n % 2][:], K.X[:, c, b, s * P:(s + 1) * P], w[:, c], start=(c == 0), stop=(c == CC - 1))
                    last.then_inc(kv_mm, 1)
                pe.wait_ge(k_out, PC * (b + 1))
                pe.wait_ge(v_out, PC * (b + 1))
                if b:
                    pe.wait_ge(m_out, 2 * b)
                for c in range(CC):
                    for s in range(PC):
                        last = nc.tensor.matmul(mps[:, c], vt[:, s, c * P:(c + 1) * P], kt[:, s, c * P:(c + 1) * P],
                                                start=(s == 0), stop=(s == PC - 1))
                last.then_inc(m_mm, 1)
                pe.wait_ge(m_out, 2 * b + 2)
                for i in range(2 * CC):
                    n = b * 2 * CC + i
                    if n >= 2:
                        pe.wait_ge(g_out, n - 1)
                    if i == CC:
                        pe.wait_ge(g_out, n)
                    if i < CC:
                        last = nc.tensor.matmul(yps[n % 2][:], mt[:, i], wo[:, i], start=True, stop=True)
                    else:
                        for c in range(CC):
                            last = nc.tensor.matmul(yps[n % 2][:], wk[:, c, (i - CC) * P:(i - CC + 1) * P], aT[:, c],
                                                    start=(c == 0), stop=(c == CC - 1))
                    last.then_inc(g_mm, 1)
                if b:
                    pe.wait_ge(b_out, b)
                for o in range(CC):
                    for c in range(CC):
                        last = nc.tensor.matmul(bps[:, o:o + 1], aT[:, c, o * P:(o + 1) * P], K.v("bk", c), start=(c == 0), stop=(c == CC - 1))
                last.then_inc(b_mm, 1)
                pe.wait_ge(g_out, (b + 1) * 2 * CC)
                for i in range(NT * CC):
                    t, o = divmod(i, CC)
                    n = b * NT * CC + i
                    if n >= 2:
                        pe.wait_ge(y_out, n - 1)
                    for c in range(CC):
                        last = nc.tensor.matmul(yps[n % 2][:], tt[:, c, o * P:(o + 1) * P], K.X[:, c, b, t * BANK:(t + 1) * BANK],
                                                start=(c == 0), stop=(c == CC - 1))
                    last.then_inc(y_mm, 1)

        @block.vector
        def _(dve):
            dve.wait_ge(w_in, 96)
            dve.wait_ge(zero, 1)
            for b in range(B):
                for s in range(PC):
                    n = b * PC + s
                    dve.wait_ge(kv_mm, n + 1)
                    if b and s == 0:
                        dve.wait_ge(m_mm, b)
                    nc.vector.tensor_tensor(kt[:, s], kps[n % 2][:], bqr, ALU.add).then_inc(k_out, 1)
                    nc.vector.tensor_tensor(vt[:, s], vps[n % 2][:], bvr, ALU.add).then_inc(v_out, 1)
                dve.wait_ge(m_mm, b + 1)
                if b:
                    dve.wait_ge(g_mm, b * 2 * CC)
                for h in range(HALF):
                    half = slice(h * DH, (h + 1) * DH)
                    nc.vector.tensor_copy(mt[half, :, half], mps[half, :, half]).then_inc(m_out, 1)
                dve.wait_ge(b_mm, b + 1)
                if b:
                    dve.wait_ge(y_out, NT * CC * b)
                nc.vector.tensor_tensor(bb[:], bps[:], K.v("bo", 0, CC), ALU.add).then_inc(b_out, 1)
                dve.wait_ge(b_out, b + 1)
                for i in range(NT * CC):
                    t, o = divmod(i, CC)
                    n = b * NT * CC + i
                    dve.wait_ge(y_mm, n + 1)
                    nc.vector.scalar_tensor_tensor(Y[:, o, b, t * BANK:(t + 1) * BANK], yps[n % 2][:], bb[:, o:o + 1],
                                                   K.X[:, o, b, t * BANK:(t + 1) * BANK], ALU.add, ALU.add).then_inc(y_out, 1)
            n = 0
            for o in range(CC):
                for b in range(B):
                    for t in range(NT):
                        dve.wait_ge(y_out, b * NT * CC + t * CC + o + 1)
                        nc.vector.bn_stats(st[:, o, b * NT + t], Y[:, o, b, t * BANK:(t + 1) * BANK]).then_inc(s_step, 1)
                        n += 1
            dve.wait_ge(s_step, n)
            for o in range(CC):
                nc.vector.bn_aggr(mv[:, o], flat(st[:, o])).then_inc(s_step, 1)
                n += 1
            dve.wait_ge(sq, 1)
            nc.vector.reciprocal(sh[:], inv[:]).then_inc(s_step, 1)
            dve.wait_ge(s_step, n + 1)
            nc.vector.tensor_tensor(inv[:], sh[:], K.v("gamma", 0, CC), ALU.mult).then_inc(s_step, 1)
            dve.wait_ge(s_step, n + 2)
            nc.vector.tensor_tensor(sh[:], mv[:, :, 0], inv[:], ALU.mult).then_inc(s_step, 1)
            dve.wait_ge(s_step, n + 3)
            nc.vector.tensor_tensor(sh[:], K.v("beta", 0, CC), sh[:], ALU.subtract).then_inc(s_step, 1)
            dve.wait_ge(s_step, n + 4)
            for o in range(CC // 2):
                nc.vector.tensor_scalar(flat(K.X[:, o]), flat(Y[:, o]), inv[:, o:o + 1], sh[:, o:o + 1], ALU.mult, ALU.add).then_inc(nrm, 1)

        @block.scalar
        def _(act):
            for b in range(B):
                for i in range(2 * CC):
                    n = b * 2 * CC + i
                    act.wait_ge(g_mm, n + 1)
                    if b and i == 0:
                        act.wait_ge(y_mm, NT * CC * b)
                    dst = aT[:, i] if i < CC else tt[:, i - CC]
                    nc.scalar.activation(dst, yps[n % 2][:], ACT.Copy).then_inc(g_out, 1)
            N_ST = CC * B * NT + CC
            act.wait_ge(s_step, N_ST)
            act.wait_ge(K.eps_ready, 1)
            nc.scalar.activation(inv[:], mv[:, :, 1], ACT.Sqrt, bias=K.eps[:]).then_inc(sq, 1)
            act.wait_ge(s_step, N_ST + 4)
            for o in range(CC // 2, CC):
                nc.scalar.activation(flat(K.X[:, o]), flat(Y[:, o]), ACT.Identity, bias=sh[:, o:o + 1], scale=inv[:, o:o + 1])


def stage_nonlocal(K, sb, ps):
    nc = K.nc
    wf, wg, wh = K.fgh_w
    wv, bhr = K.nl_wv, K.bhr
    room = carver(K.WR)
    fg = [room([P, B, HW]), room([P, B, HW])]
    hT = room([P, B * PC, MID])
    ex = [room([P, HW]) for _ in range(3)]
    z = room([P, HW])
    eT = carver(K.Q)([P, PC, HW])
    sc, bi = sb("fg_sc", [P, 2]), sb("fg_bi", [P, 2])
    nm, sm, rs = sb("nmax", [P, B * PC]), sb("esum", [P, B * PC]), sb("erec", [P, B * PC])
    sps = [ps(f"fg_ps{i}", [P, HW]) for i in range(2)]
    tps = ps("eT_ps", [P, HW])
    zps = [ps(f"z_ps{i}", [P, BANK]) for i in range(2)]
    SC = float(MID) ** -0.5
    w_in, cf, cs = K.nl_in, K.sem("fg_coef"), K.sem("fg_sqrt")
    fg_mm, fg_out, h_mm, h_out = K.sem("fg_mm"), K.sem("fg_out"), K.sem("h_mm"), K.sem("h_out")
    s_mm, mxd, exd, sts, t_mm, t_out = K.sem("nl_score"), K.sem("nl_max"), K.sem("nl_exp"), K.sem("nl_step"), K.sem("nl_tr"), K.sem("nl_tr_out")
    z_mm, z_out, o_mm, o_out = K.sem("z_mm"), K.sem("z_out"), K.sem("nlo_mm"), K.sem("nlo_out")
    NF = 2 * B
    TAIL = {PC * (b + 1) + 1: b for b in range(B)}
    STEPS = B * PC + 2
    with nc.Block() as block:
        @block.tensor
        def _(pe):
            pe.wait_ge(w_in, 80)
            for i in range(NF):
                b, k = divmod(i, 2)
                if i >= 2:
                    pe.wait_ge(fg_out, i - 1)
                for t in range(NT):
                    for c in range(CC):
                        last = nc.tensor.matmul(sps[i % 2][:, t * BANK:(t + 1) * BANK], (wf, wg)[k][:, c],
                                                K.X[:, c, b, t * BANK:(t + 1) * BANK], start=(c == 0), stop=(c == CC - 1))
                last.then_inc(fg_mm, 1)
            for i in range(B * PC // 4):
                if i >= 2:
                    pe.wait_ge(h_out, i - 1)
                for r in range(4):
                    b, s = divmod(4 * i + r, PC)
                    for c in range(CC):
                        last = nc.tensor.matmul(zps[i % 2][:, r * MID:(r + 1) * MID], K.X[:, c, b, s * P:(s + 1) * P], wh[:, c],
                                                start=(c == 0), stop=(c == CC - 1))
                last.then_inc(h_mm, 1)
            pe.wait_ge(fg_out, NF)
            pe.wait_ge(h_out, B * PC // 4)

            def scores(n):
                b, s = divmod(n, PC)
                if n >= 2:
                    pe.wait_ge(exd, n - 1)
                for t in range(NT):
                    last = nc.tensor.matmul(sps[n % 2][:, t * BANK:(t + 1) * BANK], fg[0][:, b, s * P:(s + 1) * P],
                                            fg[1][:, b, t * BANK:(t + 1) * BANK], start=True, stop=True)
                last.then_inc(s_mm, 1)

            def turn(n):
                pe.wait_ge(sts, 2 * n + 2)
                if n >= 1:
                    pe.wait_ge(t_out, n)
                for m in range(PC):
                    last = nc.tensor.transpose(tps[:, m * P:(m + 1) * P], ex[n % 3][:, m * P:(m + 1) * P], K.k("ident"))
                last.then_inc(t_mm, 1)

            def weigh(b):
                pe.wait_ge(t_out, PC * (b + 1))
                for t in range(NT):
                    if b:
                        pe.wait_ge(o_out, b * NT * CC - NT + t + 1)
                    for m in range(PC):
                        last = nc.tensor.matmul(zps[t][:], hT[:, b * PC + m], eT[:, m, t * BANK:(t + 1) * BANK],
                                                start=(m == 0), stop=(m == PC - 1))
                    last.then_inc(z_mm, 1)
                for i in range(NT * CC):
                    t, o = divmod(i, CC)
                    k = b * NT * CC + i
                    pe.wait_ge(z_out, b * NT + max(t, i % 2) + 1)
                    if i >= 2:
                        pe.wait_ge(o_out, k - 1)
                    nc.tensor.matmul(zps[i % 2][:], wv[:, o * P:(o + 1) * P], z[:, t * BANK:(t + 1) * BANK],
                                     start=True, stop=True).then_inc(o_mm, 1)

            for k in range(STEPS):
                if k < B * PC:
                    scores(k)
                if k >= 2:
                    turn(k - 2)
                if k in TAIL:
                    weigh(TAIL[k])

        @block.vector
        def _(dve):
            dve.wait_ge(cs, 1)
            n = 0
            nc.vector.reciprocal(bi[:], sc[:]).then_inc(cf, 1)
            dve.wait_ge(cf, 1)
            for k, (g, cb, be, me) in enumerate((("gf", "bf", "betaf", "mf"), ("gg", "bg", "betag", "mg"))):
                n = 1 + 4 * k
                col = slice(k, k + 1)
                nc.vector.tensor_tensor(sc[:, col], bi[:, col], K.v(g), ALU.mult).then_inc(cf, 1)
                dve.wait_ge(cf, n + 1)
                nc.vector.tensor_tensor(bi[:, col], K.v(cb), K.v(me), ALU.subtract).then_inc(cf, 1)
                dve.wait_ge(cf, n + 2)
                nc.vector.tensor_tensor(bi[:, col], bi[:, col], sc[:, col], ALU.mult).then_inc(cf, 1)
                dve.wait_ge(cf, n + 3)
                nc.vector.tensor_tensor(bi[:, col], bi[:, col], K.v(be), ALU.add).then_inc(cf, 1)
                dve.wait_ge(cf, n + 4)
            dve.wait_ge(w_in, 80)
            for i in range(B * PC // 4):
                dve.wait_ge(h_mm, i + 1)
                nc.vector.tensor_tensor(hT[:, 4 * i:4 * i + 4], zps[i % 2][:].rearrange("p (r m) -> p r m", r=4),
                                        bhr[:].unsqueeze(1).to_broadcast([P, 4, MID]), ALU.add).then_inc(h_out, 1)

            def peak(n):
                dve.wait_ge(s_mm, n + 1)
                nc.vector.tensor_reduce(rs[:, n:n + 1], sps[n % 2][:], AX.X, ALU.max).then_inc(mxd, 1)
                dve.wait_ge(mxd, 2 * n + 1)
                nc.vector.tensor_scalar(nm[:, n:n + 1], rs[:, n:n + 1], -SC, None, ALU.mult).then_inc(mxd, 1)

            def norm(n):
                dve.wait_ge(exd, n + 1)
                nc.vector.reciprocal(rs[:, n:n + 1], sm[:, n:n + 1]).then_inc(sts, 1)
                dve.wait_ge(sts, 2 * n + 1)
                nc.vector.tensor_scalar(ex[n % 3], ex[n % 3], rs[:, n:n + 1], None, ALU.mult).then_inc(sts, 1)

            def project(b):
                for i in range(NT * CC):
                    t, o = divmod(i, CC)
                    x = K.X[:, o, b, t * BANK:(t + 1) * BANK]
                    dve.wait_ge(o_mm, b * NT * CC + i + 1)
                    nc.vector.scalar_tensor_tensor(x, zps[i % 2][:], K.v("bv2", o), x, ALU.add, ALU.add).then_inc(o_out, 1)

            for k in range(STEPS):
                if k < B * PC:
                    peak(k)
                if 1 <= k <= B * PC:
                    norm(k - 1)
                if k in TAIL:
                    project(TAIL[k])

        @block.scalar
        def _(act):
            act.wait_ge(K.eps_ready, 1)
            nc.scalar.activation(sc[:, 1:2], K.v("vg"), ACT.Sqrt, bias=K.eps[:])
            nc.scalar.activation(sc[:, 0:1], K.v("vf"), ACT.Sqrt, bias=K.eps[:]).then_inc(cs, 1)
            act.wait_ge(cf, 9)
            for i in range(NF):
                b, k = divmod(i, 2)
                act.wait_ge(fg_mm, i + 1)
                nc.scalar.activation(fg[k][:, b], sps[i % 2][:], ACT.Relu, bias=bi[:, k:k + 1], scale=sc[:, k:k + 1]).then_inc(fg_out, 1)

            def exps(n):
                act.wait_ge(mxd, 2 * n + 2)
                if n >= 3:
                    act.wait_ge(t_mm, n - 2)
                nc.scalar.activation(ex[n % 3], sps[n % 2][:], ACT.Exp, bias=nm[:, n:n + 1], scale=SC,
                                     accum_out=sm[:, n:n + 1]).then_inc(exd, 1)

            for k in range(STEPS):
                if k >= 2:
                    b, s = divmod(k - 2, PC)
                    act.wait_ge(t_mm, k - 1)
                    if b and s == 0:
                        act.wait_ge(z_mm, NT * b)
                    nc.scalar.activation(eT[:, :, s * P:(s + 1) * P], tps[:].rearrange("p (m n) -> p m n", m=PC), ACT.Copy).then_inc(t_out, 1)
                if k < B * PC:
                    exps(k)
                if k in TAIL:
                    b = TAIL[k]
                    for t in range(NT):
                        act.wait_ge(z_mm, b * NT + t + 1)
                        if b:
                            act.wait_ge(o_mm, b * NT * CC)
                        nc.scalar.activation(z[:, t * BANK:(t + 1) * BANK], zps[t][:], ACT.Copy).then_inc(z_out, 1)


def stage_rank_one(K, sb, ps):
    nc = K.nc
    d = K.dram
    se1, se2 = K.se1, K.se2
    rows = carver(K.Q)([3, B, HW])
    room = carver(K.WR)
    rep = room([P, 2, B, HW])
    th = sb("theta", [P, B, PC])
    av, mid, gate = sb("avg", [P, CC, B]), sb("se_mid", [SE, B]), sb("gate", [P, CC, B])
    inv, t1, ga, gd = sb("bn3_inv", [P, CC]), sb("bn3_t", [P, CC]), sb("ga", [P, CC, B]), sb("gd", [P, CC, B])
    pm = sb("phi_ext", [P, 2, B])
    m1, m2 = sb("m1", [P, B, PC]), sb("m2", [P, B, PC])
    e = [room([P, HW]) for _ in range(2)]
    den, num, y = sb("r1_den", [P, B * PC]), sb("r1_num", [P, B * PC]), sb("r1_y", [P, B * PC])
    ones, dg = sb("ones", [P, P]), [sb(f"dg{i}", [P, P]) for i in range(2)]
    out = [room([P, HW]) for _ in range(2)]
    gps = [ps(f"gtp_ps{i}", [3, BANK]) for i in range(2)]
    aps = ps("se_ps", [P, CC, B])
    mps = ps("se1_ps", [SE, B])
    yps = ps("yrep_ps", [P, B, HW])
    w_in, av_d, g_mm, g_out, gd_out, r_in = (K.se_in, K.sem("avg_done"), K.sem("gtp_mm"), K.sem("gtp_out"),
                                             K.sem("gtp_stored"), K.sem("rep_loaded"))
    se, sx, st, ex = K.sem("se_mm"), K.sem("se_act"), K.sem("r1_step"), K.sem("r1_exp")
    nd, ydg, y_mm, af, o_st, o_out = K.sem("r1_sum"), K.sem("r1_diag"), K.sem("r1_mm"), K.sem("r1_affine"), K.sem("out_stored"), K.sem("out_sum")
    dg_dram = nc.dram_tensor("gtp_scratch", (3, B, HW), F32).ap()
    with nc.Block() as block:
        @block.sync
        def _(sp):
            sp.wait_ge(g_out, B * NT)
            sp.dma_start(dg_dram, rows).then_inc(gd_out, 16)
            sp.wait_ge(gd_out, 16)
            sp.dma_start(rep[:, 1], dg_dram[2].partition_broadcast(P)).then_inc(r_in, 16)
            for b in range(B):
                sp.dma_start(th[:, b], dg_dram[1, b].rearrange("(p s) -> p s", p=P)).then_inc(r_in, 16)
            sp.dma_start(rep[:, 0], dg_dram[0].partition_broadcast(P)).then_inc(r_in, 16)
            for n in range(CC * B):
                c, b = divmod(n, B)
                sp.wait_ge(o_out, n + 1)
                sp.dma_start(d["out"][b, c * P:(c + 1) * P, :], out[n % 2]).then_inc(o_st, 16)
                sp.wait_ge(o_st, 16 * (n + 1))

        @block.gpsimd
        def _(pool):
            nc.gpsimd.memset(ones[:], 1.0).then_inc(ydg, 1)

        @block.tensor
        def _(pe):
            for n in range(B * NT):
                b, t = divmod(n, NT)
                if n >= 2:
                    pe.wait_ge(g_out, n - 1)
                for c in range(CC):
                    last = nc.tensor.matmul(gps[n % 2][:], K.v("gtp_w", 3 * c, 3), K.X[:, c, b, t * BANK:(t + 1) * BANK],
                                            start=(c == 0), stop=(c == CC - 1))
                last.then_inc(g_mm, 1)
            pe.wait_ge(w_in, 32)
            pe.wait_ge(av_d, 1)
            for c in range(CC):
                last = nc.tensor.matmul(mps[:], se1[:, c], av[:, c], start=(c == 0), stop=(c == CC - 1))
            last.then_inc(se, 1)
            pe.wait_ge(sx, 1)
            for c in range(CC):
                last = nc.tensor.matmul(aps[:, c], se2[:, c * P:(c + 1) * P], mid[:], start=True, stop=True)
            last.then_inc(se, 1)
            for n in range(B * PC):
                b, s = divmod(n, PC)
                pe.wait_ge(ydg, n + 2)
                nc.tensor.matmul(yps[:, b, s * P:(s + 1) * P], ones[:], dg[n % 2][:], start=True, stop=True).then_inc(y_mm, 1)

        @block.vector
        def _(dve):
            nc.vector.tensor_reduce(av[:], K.X[:], AX.X, ALU.add).then_inc(st, 1)
            dve.wait_ge(st, 1)
            nc.vector.tensor_scalar(av[:], av[:], 1.0 / HW, None, ALU.mult).then_inc(av_d, 1)
            dve.wait_ge(r_in, 64)
            nc.vector.tensor_reduce(pm[:, 0], rep[:, 1], AX.X, ALU.max).then_inc(st, 1)
            nc.vector.tensor_reduce(pm[:, 1], rep[:, 1], AX.X, ALU.min).then_inc(st, 1)
            dve.wait_ge(st, 3)
            nc.vector.tensor_tensor(m1[:], th[:], pm[:, 0].unsqueeze(2).to_broadcast([P, B, PC]), ALU.mult).then_inc(st, 1)
            nc.vector.tensor_tensor(m2[:], th[:], pm[:, 1].unsqueeze(2).to_broadcast([P, B, PC]), ALU.mult).then_inc(st, 1)
            dve.wait_ge(st, 5)
            nc.vector.tensor_tensor(m1[:], m1[:], m2[:], ALU.max).then_inc(st, 1)
            dve.wait_ge(st, 6)
            nc.vector.tensor_scalar(m2[:], m1[:], -1.0, None, ALU.mult).then_inc(st, 1)
            for n in range(B * PC):
                dve.wait_ge(ex, n + 1)
                nc.vector.tensor_tensor_reduce(e[n % 2], e[n % 2], rep[:, 0, n // PC], 1.0, 0.0, ALU.mult, ALU.add,
                                               num[:, n:n + 1]).then_inc(nd, 1)
            dve.wait_ge(nd, B * PC)
            nc.vector.reciprocal(y[:], den[:]).then_inc(st, 1)
            dve.wait_ge(st, 8)
            nc.vector.tensor_tensor(y[:], y[:], num[:], ALU.mult).then_inc(st, 1)
            dve.wait_ge(st, 9)
            dve.wait_ge(ydg, 1)
            for n in range(B * PC):
                if n >= 2:
                    dve.wait_ge(y_mm, n - 1)
                nc.vector.tensor_scalar(dg[n % 2][:], K.k("ident"), y[:, n:n + 1], None, ALU.mult).then_inc(ydg, 1)
            dve.wait_ge(sx, 3)
            nc.vector.reciprocal(t1[:], inv[:]).then_inc(st, 1)
            dve.wait_ge(st, 10)
            nc.vector.tensor_tensor(inv[:], t1[:], K.v("bn_gamma", 0, CC), ALU.mult).then_inc(st, 1)
            dve.wait_ge(st, 11)
            nc.vector.tensor_tensor(t1[:], K.v("W_b", 0, CC), K.v("bn_mean", 0, CC), ALU.subtract).then_inc(st, 1)
            dve.wait_ge(st, 12)
            nc.vector.tensor_tensor(t1[:], t1[:], inv[:], ALU.mult).then_inc(st, 1)
            dve.wait_ge(st, 13)
            nc.vector.tensor_tensor(t1[:], t1[:], K.v("bn_beta", 0, CC), ALU.add).then_inc(st, 1)
            nc.vector.tensor_tensor(inv[:], inv[:], K.v("W_w", 0, CC), ALU.mult).then_inc(st, 1)
            dve.wait_ge(st, 15)
            nc.vector.tensor_tensor(ga[:], gate[:], inv[:].unsqueeze(2).to_broadcast([P, CC, B]), ALU.mult).then_inc(st, 1)
            nc.vector.tensor_tensor(gd[:], gate[:], t1[:].unsqueeze(2).to_broadcast([P, CC, B]), ALU.mult).then_inc(st, 1)
            for n in range(CC * B):
                c, b = divmod(n, B)
                dve.wait_ge(af, n + 1)
                nc.vector.tensor_tensor(out[n % 2], out[n % 2], K.X[:, c, b], ALU.add).then_inc(o_out, 1)

        @block.scalar
        def _(act):
            for n in range(B * NT):
                b, t = divmod(n, NT)
                act.wait_ge(g_mm, n + 1)
                nc.scalar.activation(rows[:, b, t * BANK:(t + 1) * BANK], gps[n % 2][:], ACT.Identity,
                                     bias=K.v("gtp_b", p1=3)).then_inc(g_out, 1)
            act.wait_ge(se, 1)
            nc.scalar.activation(mid[:], mps[:], ACT.Relu, bias=K.v("se1_b", p1=SE)).then_inc(sx, 1)
            act.wait_ge(se, 2)
            for c in range(CC):
                last = nc.scalar.activation(gate[:, c], aps[:, c], ACT.Sigmoid, bias=K.v("se2_b", c))
            last.then_inc(sx, 1)
            nc.scalar.activation(inv[:], K.v("bn_var", 0, CC), ACT.Sqrt, bias=K.eps[:]).then_inc(sx, 1)
            act.wait_ge(st, 7)
            for n in range(B * PC):
                b, s = divmod(n, PC)
                if n >= 2:
                    act.wait_ge(nd, n - 1)
                nc.scalar.activation(e[n % 2], rep[:, 1, b], ACT.Exp, bias=m2[:, b, s:s + 1], scale=th[:, b, s:s + 1],
                                     accum_out=den[:, n:n + 1]).then_inc(ex, 1)
            act.wait_ge(y_mm, B * PC)
            act.wait_ge(st, 17)
            for n in range(CC * B):
                c, b = divmod(n, B)
                if n >= 2:
                    act.wait_ge(o_st, 16 * (n - 1))
                nc.scalar.activation(out[n % 2].rearrange("p (i s) -> p i s", i=P), yps[:, b].rearrange("p (s i) -> p i s", i=P),
                                     ACT.Identity, bias=gd[:, c, b:b + 1], scale=ga[:, c, b:b + 1]).then_inc(af, 1)


def build(nc, dram):
    with ExitStack() as ctx:
        K = Kit(nc, ctx, dram)
        sb, _ = tensors(nc, ctx)
        K.vecs, K.consts = sb("vecs", [P, VN]), sb("consts_sb", [P, KN])
        K.eps = sb("eps", [P, 1])
        K.X = sb("X", [P, CC, B, HW])
        K.W1R = sb("W1R", [32 + ROWS, BIASF], F32R)
        K.W2H, K.W2L = sb("W2H", [P, BIASF], F32R), sb("W2L", [P, BIASF], F32R)
        K.W3 = sb("W3", [P, 32])
        K.dx = nc.dram_tensor("x_table", (BG, 2, W, J), F32).ap()
        K.dy = nc.dram_tensor("y_table", (BG * H // 2, 2, 2, J), F32).ap()
        K.db = nc.dram_tensor("bias_scratch", (BG * H // 2, 2, 4, BANK), F32).ap()
        K.db_bg = K.db.rearrange("c q g n -> (c q g n)").rearrange("(g i j) -> g i j", g=BG, j=J)
        K.eps_ready = K.sem("eps_ready")
        with nc.Block() as block:
            @block.vector
            def _(dve):
                nc.vector.memset(K.eps[:], EPS).then_inc(K.eps_ready, 1)
        with ExitStack() as l0:
            sb0, _ = tensors(nc, l0)
            K.Q, K.w_hi2 = place(nc, sb0, "Q", [P, BLK, HW], [P, FC // 2, 2, C])
            K.KBD, hid0 = place(nc, sb0, "KBD", [P, BLK, P], [P, 2, BANK])
            K.VBD, hid1 = place(nc, sb0, "VBD", [P, BLK, P], [P, 2, BANK])
            with ExitStack() as front:
                with ExitStack() as s:
                    sbf, _ = tensors(nc, front)
                    stage_front(K, sbf, tensors(nc, s)[1])
                K.GXY, K.nt = sbf("GXY", [P, 2, HALF * BLK, J]), sbf("nt", [2 * BG, J])
                with ExitStack() as s:
                    sbo, pso = tensors(nc, s)
                    stage_offsets(K, sbo, pso)
                with ExitStack() as s:
                    stage_tables(K, *tensors(nc, s))
            with ExitStack() as s:
                sb1, _ = tensors(nc, s)
                K.WR, K.w_lo = place(nc, sb1, "mlp_w", [P, FC, 2, C])
                K.mlp_in = K.sem("mlp_w_loaded")
                with nc.Block() as block:
                    @block.scalar
                    def _(act):
                        act.dma_start(K.WR[:], dram["mlp_w"]).then_inc(K.mlp_in, 16)
                with ExitStack() as s2:
                    stage_bias(K, *tensors(nc, s2))
                K.HA, K.w_hi = place(nc, sb1, "mlp_w_hi", [P, FC // 2, 2, C])
                K.s2 = sb1("s2", [P, CC])
                K.XNA, xn2_a = place(nc, sb1, "xn2_a", [P, 2, CC, BANK])
                with ExitStack() as s2:
                    sb2, _ = tensors(nc, s2)
                    K.XNB, xn2_b = place(nc, sb2, "xn2_b", [P, 2, CC, BANK])
                    K.xn2 = [(t[:, 0], t[:, 1]) for t in (xn2_a, xn2_b)]
                    for stage in (stage_attention, stage_out_proj):
                        with ExitStack() as s3:
                            stage(K, *tensors(nc, s3))
                    K.hid = [hid0, hid1, sb2("hidden", [P, 2, BANK], F32R)]
                    with ExitStack() as s3:
                        stage_mlp(K, *tensors(nc, s3))
                room = carver(K.KBD, K.VBD)
                K.fgh_w = [room([P, CC, MID]) for _ in range(3)]
                K.nl_wv, K.bhr = room([P, C]), sb1("bh_rep", [P, MID])
                K.se1, K.se2 = sb1("se1", [P, CC, SE]), sb1("se2", [SE, C])
                K.nl_in, K.se_in = K.sem("l2_w_loaded"), K.sem("l3_w_loaded")
                for stage in (stage_linear, stage_nonlocal, stage_rank_one):
                    with ExitStack() as s2:
                        stage(K, *tensors(nc, s2))


def constants():
    j, p = np.arange(J), np.arange(P)
    k = np.zeros((P, KN), np.float32)

    def put(name, a):
        o, w = KCOL[name]
        k[:, o:o + w] = a

    put("grid_x", (j % WD)[None])
    put("grid_y", (j // WD)[None])
    put("neg_ix", -(p % W)[:, None])
    put("neg_iy", -(np.arange(PC)[None] * (P // W) + (p // W)[:, None]))
    put("grid_q", (np.float32(2.0) * np.arange(W, dtype=np.float32) / np.float32(W - 1) - np.float32(1.0))[None])
    put("mask_hi", np.isin(p, (0, 1, 4, 5, 8)).astype(np.float32)[:, None])
    put("mask_lo", np.isin(p, (2, 3, 6, 7, 9)).astype(np.float32)[:, None])
    put("ident", np.eye(P, dtype=np.float32))
    return k


def lay_out(a):
    def chunks(v):
        return v.reshape(-1, P).T

    def pad(v):
        return np.concatenate([v, np.zeros(P - v.shape[0], v.dtype)])[:, None]

    def in_rows(w):
        return np.ascontiguousarray(w.T.reshape(-1, P, w.shape[0]).transpose(1, 0, 2))

    def rep(v, n=P):
        return np.broadcast_to(v.reshape(1, 1), (n, 1))

    L0, L1, L2, L3 = ({k[8:]: v for k, v in a.items() if k.startswith(f"L{i}_conv_")} for i in range(4))
    vec = {
        "bn1_g": chunks(L0["bn1_g"]), "bn1_b": chunks(L0["bn1_b"]), "bn2_g": chunks(L0["bn2_g"]), "bn2_b": chunks(L0["bn2_b"]),
        "out_b": chunks(L0["out_b"]), "dw_w": np.concatenate([L0["off_dw_w"].reshape(DH, -1)] * HALF),
        "dw_b": np.concatenate([L0["off_dw_b"]] * HALF)[:, None], "pw": np.concatenate([L0["off_pw_w"].T] * HALF),
        "cpb_b2": L0["cpb_b2"][:, None], "cpb_b3": rep(L0["cpb_b3"]), "cpb_w3": L0["cpb_w3"],
        "mlp_b1": chunks(L0["mlp_b1"]), "mlp_b2": chunks(L0["mlp_b2"]),
        "bk": chunks(L1["bk"]), "bo": chunks(L1["bo"]), "gamma": chunks(L1["gamma"]), "beta": chunks(L1["beta"]),
        "bv2": chunks(L2["bv"]),
        "gtp_w": np.stack([L3["g_w"][0], L3["theta_w"][0], L3["phi_w"][0]], 1).reshape(CC, P, 3).transpose(1, 0, 2).reshape(P, 3 * CC),
        "gtp_b": pad(np.concatenate([L3["g_b"], L3["theta_b"], L3["phi_b"]])),
        "W_w": chunks(L3["W_w"].reshape(-1)), "W_b": chunks(L3["W_b"]),
        "bn_gamma": chunks(L3["bn_gamma"]), "bn_beta": chunks(L3["bn_beta"]), "bn_mean": chunks(L3["bn_mean"]),
        "bn_var": chunks(L3["bn_var"]), "se1_b": pad(L3["se1_b"]), "se2_b": chunks(L3["se2_b"]),
    }
    for n in ("bf", "gf", "betaf", "mf", "vf", "bg", "gg", "betag", "mg", "vg"):
        vec[n] = L2[n][:, None]

    def per_group(w):
        return np.ascontiguousarray(w.reshape(CC, HALF, DH, DH).transpose(1, 3, 0, 2).reshape(P, CC, DH))

    w1, b1 = L0["cpb_w1"], L0["cpb_b1"]
    return {
        "x": a["x"].reshape(B, C, HW),
        "vecs": np.concatenate([vec[n] for n, _ in _WIDTHS], 1), "consts": constants(),
        "qwT": per_group(L0["qw"]), "kwT": per_group(L0["kw"]), "vwT": per_group(L0["vw"]),
        "cpb_w1r": np.stack([w1[0]] * 4 + [w1[1]] * 4 + [b1] * 2), "cpb_w2": L0["cpb_w2"],
        "out_wT": in_rows(L0["out_w"]),
        "mlp_w": np.stack([in_rows(L0["mlp_w1"]).reshape(P, CC, FC, P).transpose(0, 2, 1, 3).reshape(P, FC, C), in_rows(L0["mlp_w2"])], 2),
        "WqT": in_rows(L1["Wq"]), "WvT": in_rows(L1["Wv"]), "Wk": in_rows(L1["Wk"].T), "WoT": in_rows(L1["Wo"]),
        "bq": L1["bq"], "bv": L1["bv"],
        "wfT": in_rows(L2["wf"]), "wgT": in_rows(L2["wg"]), "whT": in_rows(L2["wh"]), "wvT": np.ascontiguousarray(L2["wv"].T),
        "bh": L2["bh"], "se1_wT": in_rows(L3["se1_w"]), "se2_wT": np.ascontiguousarray(L3["se2_w"].T),
    }


def kernel(**inputs):
    import concourse.bacc as bacc
    from concourse.bass_utils import run_bass_kernel_spmd

    arrays = {n: np.ascontiguousarray(v) for n, v in lay_out({k: np.asarray(v) for k, v in inputs.items()}).items()}
    nc = bacc.Bacc("TRN2", target_bir_lowering=False, num_devices=1)
    dram = {n: nc.dram_tensor(f"in_{n}", v.shape, mybir.dt.from_np(v.dtype), kind="ExternalInput").ap() for n, v in arrays.items()}
    dram["out"] = nc.dram_tensor("out", (B, C, HW), F32, kind="ExternalOutput").ap()
    build(nc, dram)
    result = run_bass_kernel_spmd(nc, [{f"in_{n}": v for n, v in arrays.items()}], core_ids=[0])
    return result.results[0]["out"].reshape(B, C, H, W)
```

```python
from contextlib import ExitStack

import numpy as np

import concourse.bass as bass
from concourse import mybir

F32 = mybir.dt.float32
F32R = mybir.dt.float32r
ACT = mybir.ActivationFunctionType
ALU = mybir.AluOpType
AX = mybir.AxisListType

P = 128
B, C, H, W = 2, 512, 32, 32
HW = H * W
CC = C // P
BLK = CC * B
BANK = 512
NT = HW // BANK
PC = HW // P
HEADS, DH = 8, 64
HALF = P // DH
HD = WD = 8
J = HD * WD
KS, DF = 6, 4
TAPS = sorted(range(KS * KS), key=lambda tap: tap != KS + 1)
V_TAPS = [KS * ky + kx for ky in (2, 3, 4) for kx in (1, 2, 3, 4, 0)]
TAPS = [tap for tap in TAPS if tap not in V_TAPS]


def reach(tap):
    (y0, y1), (x0, x1) = ((int(k == 0), HD - int(k == KS - 1)) for k in divmod(tap, KS))
    ky, kx = divmod(tap, KS)
    return (y0, y1), (x0, x1), DF * y0 + ky - 1, DF * x0 + kx - 1


OFF_SCALE = 4.0
EPS = 1e-5
BG = B * HEADS
FH = 4 * C
FC = FH // P
MID = C // 4
SE = C // 16
BIASF = 128

_WIDTHS = [
    ("bn1_g", CC), ("bn1_b", CC), ("bn2_g", CC), ("bn2_b", CC), ("out_b", CC),
    ("dw_w", KS * KS), ("dw_b", 1), ("pw", 2), ("cpb_b2", 1), ("cpb_b3", 1), ("cpb_w3", 1),
    ("mlp_b1", FC), ("mlp_b2", CC),
    ("bk", CC), ("bo", CC), ("gamma", CC), ("beta", CC),
    ("bf", 1), ("gf", 1), ("betaf", 1), ("mf", 1), ("vf", 1),
    ("bg", 1), ("gg", 1), ("betag", 1), ("mg", 1), ("vg", 1), ("bv2", CC),
    ("gtp_w", CC * 3), ("gtp_b", 1), ("W_w", CC), ("W_b", CC),
    ("bn_gamma", CC), ("bn_beta", CC), ("bn_mean", CC), ("bn_var", CC), ("se1_b", 1), ("se2_b", CC),
]
VCOL, VN = {}, 0
for _n, _w in _WIDTHS:
    VCOL[_n] = (VN, _w)
    VN += _w
ROWQ = W * 2 * BG // P
BEFORE = 4
_CWIDTHS = [("pixel_x", J), ("pixel_y", J), ("grid_nt", J), ("neg_ix", 1), ("neg_iy", PC), ("grid_q", ROWQ),
            ("mask_hi", 1), ("mask_lo", 1), ("ident", P)]
KCOL, KN = {}, 0
for _n, _w in _CWIDTHS:
    KCOL[_n] = (KN, _w)
    KN += _w

W_FIRST = 6

ROWS = 10


def flat(ap):
    n = ap.ndim - 1
    names = " ".join("abcdef"[:n])
    return ap.rearrange(f"p {names} -> p ({names})") if n > 1 else ap


def carver(*tensors):
    free = [[flat(t[:]), 0] for t in tensors]

    def room(shape):
        n = int(np.prod(shape[1:]))
        area = next(a for a in free if a[1] + n <= a[0].shape[-1])
        ap = area[0][0:shape[0], area[1]:area[1] + n]
        area[1] += n
        names = "abcdef"[:len(shape) - 1]
        if len(names) > 1:
            ap = ap.rearrange(f"p ({' '.join(names)}) -> p {' '.join(names)}", **dict(zip(names, shape[1:])))
        return ap

    return room


def place(nc, sb, name, shape, rounded_shape=None):
    at = -(-nc.sbuf_base // 32) * 32
    t = sb(name, shape)
    return t, nc.alloc_sbuf_tensor_at(f"{name}_r", rounded_shape or shape, F32R, offset=at)


def split_norm(K, n, tmp, hi_done, lo_done):
    nc, (b, t) = K.nc, divmod(n, NT)

    def high(c):
        nc.scalar.activation(K.xn2[n % 2][0][:, c], K.X[:, c, b, t * BANK:(t + 1) * BANK],
                             ACT.Identity, bias=K.v("bn2_b", c), scale=K.s2[:, c:c + 1]).then_inc(hi_done, 1)

    def low(c, dve, step):
        if n or c:
            dve.wait_ge(lo_done, n * CC + c)
        nc.vector.tensor_scalar(tmp[:], K.X[:, c, b, t * BANK:(t + 1) * BANK], K.s2[:, c:c + 1], K.v("bn2_b", c),
                                ALU.mult, ALU.add).then_inc(step, 1)
        dve.wait_ge(step, n * CC + c + 1)
        dve.wait_ge(hi_done, n * CC + c + 1)
        nc.vector.tensor_tensor(K.xn2[n % 2][1][:, c], tmp[:], K.xn2[n % 2][0][:, c].bitcast(F32), ALU.subtract).then_inc(lo_done, 1)

    return high, low


class Kit:

    def __init__(self, nc, ctx, dram):
        self.nc, self.ctx, self.dram = nc, ctx, dram

    def sem(self, name):
        return self.ctx.enter_context(self.nc.semaphore(name))

    def v(self, name, i=0, n=1, p0=0, p1=P):
        o, _ = VCOL[name]
        return self.vecs[p0:p1, o + i:o + i + n]

    def k(self, name, i=0, n=None, p0=0, p1=P):
        o, w = KCOL[name]
        return self.consts[p0:p1, o + i:o + i + (w if n is None else n)]


def tensors(nc, ctx):
    def sb(name, shape, dt=F32):
        return ctx.enter_context(nc.sbuf_tensor(name, shape, dt))

    def ps(name, shape):
        return ctx.enter_context(nc.psum_tensor(name, shape, F32))

    return sb, ps


def stage_front(K, sb, ps):
    nc = K.nc
    K.XN = sb("XN", [P, CC, B, HW])
    K.XT = sb("XT", [P, B * PC, C])
    s1 = sb("s1", [P, CC])
    K.QW = QW = sb("QW", [P, CC, P])
    K.KW = KW = sb("KW", [P, CC, P])
    K.VW = VW = sb("VW", [P, CC, DH])
    R = BANK // P
    qps = [ps(f"qps{i}", [P, BANK]) for i in range(3)]
    tps = [ps(f"tps{i}", [P, R, P]) for i in range(3)]
    small, x_in, zero = K.sem("small_loaded"), [K.sem(f"x_loaded{i}") for i in range(BLK)], K.sem("front_zeroed")
    w_in, kw_in, s1_ready = K.sem("q_weights"), K.sem("kv_weights"), K.sem("s1_ready")
    xn_act, xn_dve = K.sem("xn_even_ready"), K.sem("xn_odd_ready")
    q_mm, q_out, t_mm, t_out = K.sem("q_mm"), K.sem("q_out"), K.sem("xt_mm"), K.sem("xt_out")
    d = K.dram
    with nc.Block() as block:
        @block.sync
        def _(sp):
            sp.dma_start(K.vecs[:], d["vecs"]).then_inc(small, 16)
            for i in range(BLK):
                c, b = divmod(i, B)
                sp.dma_start(K.X[:, c, b], d["x"][b, c * P:(c + 1) * P, :]).then_inc(x_in[i], 16)
                if i == 1:
                    sp.dma_start(K.consts[:], d["consts"]).then_inc(small, 16)
            sp.wait_ge(zero, 2)
            for h in range(HALF):
                half = slice(h * DH, (h + 1) * DH)
                sp.dma_start(KW[half, :, half], d["kwT"][half]).then_inc(kw_in, 16)
            sp.dma_start(VW[:], d["vwT"]).then_inc(kw_in, 16)
            sp.wait_ge(kw_in, 48)

        @block.gpsimd
        def _(pool):
            nc.gpsimd.memset(QW[:], 0.0).then_inc(zero, 1)
            pool.wait_ge(zero, 1)
            for h in range(HALF):
                half = slice(h * DH, (h + 1) * DH)
                pool.dma_start(QW[half, :, half], d["qwT"][half]).then_inc(w_in, 16)
            nc.gpsimd.memset(KW[:], 0.0).then_inc(zero, 1)
            nc.gpsimd.memset(K.KBD, 0.0).then_inc(zero, 1)
            nc.gpsimd.memset(K.VBD, 0.0).then_inc(zero, 1)
            pool.wait_ge(zero, 4)

        @block.scalar
        def _(act):
            def norm(c):
                act.wait_ge(x_in[B * c], 16)
                nc.scalar.activation(K.XN[:, c, 0], K.X[:, c, 0], ACT.Identity,
                                     bias=K.v("bn1_b", c), scale=s1[:, c:c + 1]).then_inc(xn_act, 1)

            act.wait_ge(s1_ready, 1)
            norm(0)
            for c in range(CC):
                if c + 1 < CC:
                    norm(c + 1)
                for r in range(B * NT):
                    i = c * B * NT + r
                    act.wait_ge(q_mm, i + 1)
                    nc.scalar.activation(K.Q[:, B * c + r // NT, (r % NT) * BANK:(r % NT + 1) * BANK], qps[i % 3][:],
                                         ACT.Copy).then_inc(q_out, 1)

        @block.tensor
        def _(pe):
            pe.wait_ge(w_in, 32)
            pe.wait_ge(small, 32)
            for i in range(BLK * NT):
                blk, t = divmod(i, NT)
                c, b = divmod(blk, B)
                pe.wait_ge((xn_act, xn_dve)[b], c + 1)
                if i >= 3:
                    pe.wait_ge(q_out, i - 2)
                nc.tensor.matmul(qps[i % 3][:], QW[:, c], K.XN[:, c, b, t * BANK:(t + 1) * BANK],
                                 start=True, stop=True).then_inc(q_mm, 1)
                if i >= 3:
                    pe.wait_ge(t_out, i - 2)
                for r in range(R):
                    at = (t * R + r) * P
                    last = nc.tensor.transpose(tps[i % 3][:, r], K.XN[:, c, b, at:at + P], K.k("ident"))
                last.then_inc(t_mm, 1)

        @block.vector
        def _(dve):
            def norm(c):
                dve.wait_ge(x_in[B * c + 1], 16)
                nc.vector.tensor_scalar(K.XN[:, c, 1], K.X[:, c, 1], s1[:, c:c + 1], K.v("bn1_b", c),
                                        ALU.mult, ALU.add).then_inc(xn_dve, 1)

            dve.wait_ge(small, 16)
            dve.wait_ge(small, 32)
            nc.vector.tensor_scalar(s1[:], K.v("bn1_g", 0, CC), float(1.0 / np.sqrt(1.0 + EPS)), None,
                                    ALU.mult).then_inc(s1_ready, 1)
            dve.wait_ge(s1_ready, 1)
            norm(0)
            for c in range(CC):
                if c + 1 < CC:
                    norm(c + 1)
                for r in range(B * NT):
                    i = c * B * NT + r
                    b, t = divmod(r, NT)
                    at = b * PC + t * R
                    dve.wait_ge(t_mm, i + 1)
                    nc.vector.tensor_copy(K.XT[:, at:at + R, c * P:(c + 1) * P], tps[i % 3][:]).then_inc(t_out, 1)


def stage_samples(K, sb, ps):
    nc = K.nc
    SAMP = HALF * BLK * J
    n_ax, QT = 2 * BG, W // ROWQ
    diag = [sb(f"dw_diag{i}", [P, P]) for i in range(4)]
    pwr = sb("pw_rep", [P, 2, P])
    gel = sb("dw_gelu", [P, BLK * J])
    off, GXY = sb("offset", [P, 2, HALF * BLK, J]), sb("pixel", [P, 2, HALF * BLK, J])
    nt, nt2 = sb("nt", [P, J]), sb("nt_tmp", [P, J])
    acc2 = sb("dw_part", [P, BLK, HD, WD])
    tabs = sb("tables", [P, 2, ROWQ, J], F32R)
    pos, lg, sg = (sb(n, [P, ROWQ, J]) for n in ("pos", "log_pos", "sign_pos"))
    wt = K.XN[:].rearrange("p c b n -> p (c b n)").rearrange("p (s n) -> p s n", s=PC)
    tx = sb("tent_x", [P, SAMP])
    ty = [sb(f"tent_y{i}", [P, SAMP]) for i in range(4)]
    kv = sb("kv", [P, BLK, J])
    w1raw, w1h, w1l, w1t = (sb("w1raw", [ROWS, BIASF]), sb("w1h", [ROWS, BIASF], F32R),
                            sb("w1l", [ROWS, BIASF], F32R), sb("w1t", [ROWS, BIASF]))
    w2raw = K.QW[:, 0]
    ops, acc = ps("off_ps", [P, 2, HALF, BANK]), ps("dw_ps", [P, BLK, HD, WD])
    kvps, vps = ps("kv_ps", [P, BLK, HALF, J]), ps("v_ps", [P, BLK, J])
    kps = acc[:].rearrange("p k y x -> p k (y x)")
    taps, conv, gelu_done, pw_mm, tanh_done, crd = (K.sem("conv_taps"), K.sem("conv_step"), K.sem("gelu_done"),
                                                    K.sem("pw_mm"), K.sem("tanh_done"), K.sem("coord_step"))
    nx_dram, nt_in, ntd, part = K.sem("nx_stored"), K.sem("nt_loaded"), K.sem("nt_step"), K.sem("conv_part")
    tab, axd, absd, tyd, wtd = (K.sem("tab_step"), K.sem("act_pos"), K.sem("act_dist"), K.sem("act_tent"), K.sem("w_tent"))
    kv_mm, kv_out, k_mm, v_mm, kb_out = (K.sem("kv_mm"), K.sem("kv_out"), K.sem("k_mm"), K.sem("v_mm"), K.sem("kvbd_out"))
    cw_in, cw, tab_out = K.sem("cpb_w_loaded"), K.sem("cpb_w_step"), K.sem("tab_stored")
    dn = nc.dram_tensor("nx_scratch", (2, BLK, HALF, J), F32).ap()
    d = K.dram
    TB = len(ty)
    with nc.Block() as block:
        @block.sync
        def _(sp):
            sp.dma_start(w1raw[:], d["cpb_w1r"]).then_inc(cw_in, 16)
            sp.dma_start(w2raw, d["cpb_w2"]).then_inc(cw_in, 16)
            sp.wait_ge(tanh_done, 1)
            for axis in range(2):
                for h in range(HALF):
                    sp.dma_start(dn[axis, :, h].unsqueeze(0), off[0:1, axis, h * BLK:(h + 1) * BLK]).then_inc(nx_dram, 16)
            sp.wait_ge(nx_dram, 16 * 2 * HALF)
            for r in range(QT):
                sp.dma_start(nt[r * n_ax:(r + 1) * n_ax, :], dn.rearrange("a k h j -> (a k h) j")).then_inc(nt_in, 16)
            sp.wait_ge(tab, 5)
            for r in range(QT):
                at = r * n_ax
                sp.dma_start(K.dx[:, :, r * ROWQ:(r + 1) * ROWQ].rearrange("g a y j -> g a (y j)"),
                             tabs[at:at + BG].bitcast(F32).rearrange("g a y j -> g a (y j)")).then_inc(tab_out, 16)
                for part in range(2):
                    sp.dma_start(K.dy[:, part].rearrange("(g c) y j -> g c (y j)", g=BG)[:, r * ROWQ // 2:(r + 1) * ROWQ // 2],
                                 tabs[at + BG:at + n_ax, part].bitcast(F32).rearrange("g (c y) j -> g c (y j)", y=2)).then_inc(tab_out, 16)
            sp.wait_ge(tab_out, 16 * 3 * QT)

        @block.vector
        def _(dve):
            nc.vector.tensor_copy(pwr[:], K.v("pw", 0, 2).unsqueeze(2).to_broadcast([P, 2, P])).then_inc(conv, 1)
            qr = K.Q[:].rearrange("p k (y x) -> p (k y) x", x=W)
            a2 = acc2[:].rearrange("p k y x -> p (k y) x")

            def tap_here(m):
                _, (x0, x1), iy, ix = reach(V_TAPS[m])
                src = qr[:, iy::DF, ix:ix + DF * (x1 - x0 - 1) + 1:DF]
                if m == 0:
                    nc.vector.tensor_scalar(a2, src, K.v("dw_w", V_TAPS[m]), None, ALU.mult).then_inc(part, 1)
                else:
                    dve.wait_ge(part, m)
                    nc.vector.scalar_tensor_tensor(a2[:, :, x0:x1], src, K.v("dw_w", V_TAPS[m]), a2[:, :, x0:x1],
                                                   ALU.mult, ALU.add).then_inc(part, 1)

            for n in range(len(TAPS)):
                if n >= 4:
                    dve.wait_ge(taps, n - 3)
                nc.vector.tensor_scalar(diag[n % 4][:], K.k("ident"), K.v("dw_w", TAPS[n]), None, ALU.mult).then_inc(conv, 1)
                if n >= 3 and n - 3 < len(V_TAPS):
                    tap_here(n - 3)
            dve.wait_ge(taps, len(TAPS))
            dve.wait_ge(part, len(V_TAPS))
            nc.vector.tensor_tensor(acc2[:], acc2[:], acc[:], ALU.add).then_inc(part, 1)
            dve.wait_ge(cw_in, 32)
            nc.vector.tensor_copy(w1h[:], w1raw[:]).then_inc(cw, 1)
            nc.vector.tensor_copy(K.W2H[:], w2raw).then_inc(cw, 1)
            nc.vector.tensor_copy(K.W3[:], K.v("cpb_w3").to_broadcast([P, 32])).then_inc(cw, 1)
            dve.wait_ge(cw, 3)
            nc.vector.tensor_tensor(w1l[:], w1raw[:], w1h[:].bitcast(F32), ALU.subtract).then_inc(cw, 1)
            nc.vector.tensor_tensor(K.W2L[:], w2raw, K.W2H[:].bitcast(F32), ALU.subtract).then_inc(cw, 1)
            dve.wait_ge(cw, 5)
            nc.vector.tensor_scalar(w1t[:], w1l[:].bitcast(F32), K.k("mask_lo", p1=ROWS), None, ALU.mult).then_inc(cw, 1)
            dve.wait_ge(cw, 6)
            for par in range(2):
                nc.vector.scalar_tensor_tensor(K.W1R[32 * par:32 * par + ROWS], w1h[:].bitcast(F32), K.k("mask_hi", p1=ROWS), w1t[:],
                                               ALU.mult, ALU.add).then_inc(cw, 1)
            dve.wait_ge(tanh_done, 1)
            for axis, grid in enumerate(("pixel_x", "pixel_y")):
                nc.vector.scalar_tensor_tensor(GXY[:, axis], off[:, axis], OFF_SCALE * W / (HD - 1),
                                               K.k(grid).unsqueeze(1).to_broadcast([P, HALF * BLK, J]),
                                               ALU.mult, ALU.add).then_inc(crd, 1)

            def tents(chunks):
                for s in chunks:
                    dve.wait_ge(tyd, s + 2)
                    nc.vector.tensor_tensor(wt[:, s], ty[s % TB][:], tx[:], ALU.mult).then_inc(wtd, 1)

            tents(range(0, BEFORE))
            dve.wait_ge(nt_in, 16 * QT)
            nc.vector.scalar_tensor_tensor(nt2[:], nt[:], OFF_SCALE, K.k("grid_nt"), ALU.mult, ALU.add).then_inc(ntd, 1)
            dve.wait_ge(ntd, 1)
            nc.vector.tensor_scalar(nt[:], nt2[:], 2.0, 1.0 / (HD - 1), ALU.mult, ALU.mult).then_inc(ntd, 1)
            dve.wait_ge(ntd, 2)
            nc.vector.tensor_scalar(nt2[:], nt[:], -1.0, None, ALU.add).then_inc(ntd, 1)
            dve.wait_ge(ntd, 3)
            nc.vector.tensor_tensor(pos[:], K.k("grid_q").unsqueeze(2).to_broadcast([P, ROWQ, J]),
                                    nt2[:].unsqueeze(1).to_broadcast([P, ROWQ, J]), ALU.subtract).then_inc(tab, 1)
            dve.wait_ge(tab, 1)
            nc.vector.tensor_scalar(sg[:], pos[:], 0.0, 2.0, ALU.is_ge, ALU.mult).then_inc(tab, 1)
            dve.wait_ge(axd, 2)
            dve.wait_ge(tab, 2)
            nc.vector.scalar_tensor_tensor(flat(pos[:]), flat(sg[:]), -1.0, flat(lg[:]), ALU.add, ALU.mult).then_inc(tab, 1)
            dve.wait_ge(tab, 3)
            nc.vector.tensor_copy(tabs[:, 0], pos[:]).then_inc(tab, 1)
            dve.wait_ge(tab, 4)
            nc.vector.tensor_tensor(tabs[:, 1], pos[:], tabs[:, 0].bitcast(F32), ALU.subtract).then_inc(tab, 1)
            tents(range(BEFORE, PC))
            dve.wait_ge(kv_mm, 1)
            for h in range(HALF):
                half = slice(h * DH, (h + 1) * DH)
                nc.vector.tensor_copy(kv[half], kvps[half, :, h]).then_inc(kv_out, 1)
            dve.wait_ge(k_mm, 1)
            for h in range(HALF):
                half = slice(h * DH, (h + 1) * DH)
                nc.vector.tensor_scalar(K.KBD[half, :, half], kps[half], float(DH) ** -0.5, None, ALU.mult).then_inc(kb_out, 1)
            dve.wait_ge(kb_out, 2)
            dve.wait_ge(cw, 8)

        @block.scalar
        def _(act):
            act.wait_ge(part, len(V_TAPS) + 1)
            nc.scalar.activation(gel[:], flat(acc2[:]), ACT.Gelu, bias=K.v("dw_b")).then_inc(gelu_done, 1)
            act.wait_ge(pw_mm, 1)
            nc.scalar.activation(off[:].rearrange("p a (h k) j -> p a h (k j)", h=HALF), ops[:], ACT.Tanh).then_inc(tanh_done, 1)
            act.wait_ge(crd, 2)
            gx, gy = (GXY[:, a].rearrange("p k j -> p (k j)") for a in range(2))

            def tent(s):
                to = tx[:] if s < 0 else ty[s % TB][:]
                if s >= TB:
                    act.wait_ge(wtd, s - TB + 1)
                nc.scalar.activation(to, gx if s < 0 else gy, ACT.Abs,
                                     bias=K.k("neg_ix") if s < 0 else K.k("neg_iy", s, 1)).then_inc(absd, 1)
                act.wait_ge(absd, s + 2)
                nc.scalar.activation(to, to, ACT.Relu, bias=1.0, scale=-1.0).then_inc(tyd, 1)

            for s in range(-1, BEFORE):
                tent(s)
            act.wait_ge(tab, 1)
            nc.scalar.activation(lg[:], pos[:], ACT.Abs).then_inc(axd, 1)
            act.wait_ge(axd, 1)
            nc.scalar.activation(lg[:], lg[:], ACT.Ln, bias=1.0).then_inc(axd, 1)
            for s in range(BEFORE, PC):
                tent(s)
            act.wait_ge(v_mm, 1)
            for h in range(HALF):
                half = slice(h * DH, (h + 1) * DH)
                nc.scalar.activation(K.VBD[half, :, half], vps[half], ACT.Copy)

        @block.tensor
        def _(pe):
            q = K.Q[:].rearrange("p k (y x) -> p k y x", x=W)
            for n, tap in enumerate(TAPS):
                (y0, y1), (x0, x1), iy, ix = reach(tap)
                pe.wait_ge(conv, n + 2)
                last = nc.tensor.matmul(acc[:, :, y0:y1, x0:x1], diag[n % 4][:],
                                        q[:, :, iy:iy + DF * (y1 - y0 - 1) + 1:DF, ix:ix + DF * (x1 - x0 - 1) + 1:DF],
                                        start=(n == 0), stop=(n == len(TAPS) - 1))
                last.then_inc(taps, 1)
            pe.wait_ge(gelu_done, 1)
            for axis in range(2):
                for h in range(HALF):
                    half = slice(h * DH, (h + 1) * DH)
                    last = nc.tensor.matmul(ops[:, axis, h], pwr[half, axis], gel[half, :], start=True, stop=True)
            last.then_inc(pw_mm, 1)
            PER_BANK = BANK // (HALF * J)
            for s in range(PC):
                pe.wait_ge(wtd, s + 1)
                for blk in range(BLK):
                    c, b = divmod(blk, B)
                    last = nc.tensor.matmul(kvps[:, blk], K.XT[:, b * PC + s, c * P:(c + 1) * P],
                                            wt[:, s].rearrange("p (h k j) -> p h k j", h=HALF, k=BLK)[:, :, blk],
                                            start=(s == 0 and blk % PER_BANK == 0),
                                            stop=(s == PC - 1 and blk % PER_BANK == PER_BANK - 1))
            last.then_inc(kv_mm, 1)
            pe.wait_ge(kv_out, 2)
            for c in range(CC):
                last = nc.tensor.matmul(flat(kps[:, B * c:B * c + B]), K.KW[:, c], flat(kv[:, B * c:B * c + B]), start=True, stop=True)
            last.then_inc(k_mm, 1)
            for blk in range(BLK):
                for h in range(HALF):
                    half = slice(h * DH, (h + 1) * DH)
                    last = nc.tensor.matmul(vps[half, blk], kv[half, blk], K.VW[half, blk // B], start=True, stop=True)
            last.then_inc(v_mm, 1)


def stage_bias(K, sb, ps):
    nc = K.nc
    TILE = 1024
    QROW = W * J
    CHUNK = 2 * QROW
    N = K.mlp_pieces = BG * HW * J // (2 * CHUNK)
    S_all = sb("S", [32 + ROWS, 2, W, J], F32R)
    S = [S_all[32 * i:32 * i + ROWS] for i in range(2)]
    hh = [sb(f"h1_hi{i}", [P, TILE], F32R) for i in range(2)]
    hl = [sb(f"h1_lo{i}", [P, TILE], F32R) for i in range(2)]
    h2 = [sb(f"h2_{i}", [P, QROW]) for i in range(2)]
    br = [sb(f"bias_rows{i}", [P, 2, BANK]) for i in range(2)]
    p1 = [ps(f"l1_ps{i}", [P, TILE]) for i in range(2)]
    p2 = [ps(f"l2_ps{i}", [P, BANK]) for i in range(3)]
    p3 = ps("l3_ps", [P, BANK])
    ones, ones_odd = K.sem("s_ones"), K.sem("s_ones_odd")
    s_in, rows_out = [K.sem(f"s_loaded{i}") for i in range(2)], [K.sem(f"rows_stored{i}") for i in range(2)]
    l1, hi_done, lo_done, l2 = K.sem("l1_mm"), K.sem("hi_done"), K.sem("lo_done"), K.sem("l2_mm")
    relu_a, relu_b, l3, copied = K.sem("relu_a"), K.sem("relu_b"), K.sem("l3_mm"), K.sem("rows_copied")
    with nc.Block() as block:
        @block.vector
        def _(dve):
            nc.vector.memset(S_all[:, 0].bitcast(F32), 1.0).then_inc(ones, 1)
            dve.wait_ge(ones, 1)

        @block.gpsimd
        def _(pool):
            nc.gpsimd.memset(S_all[:, 1].bitcast(F32), 1.0).then_inc(ones_odd, 1)
            pool.wait_ge(ones_odd, 1)
    LOADS = 6 * 16
    with nc.Block() as block:
        @block.sync
        def _(sp):
            def load(it, bg, k):
                for dup in range(2):
                    sp.dma_start(S[k][2 * dup:2 * dup + 2].bitcast(F32).rearrange("r q a j -> r q (a j)"),
                                 K.dx[bass.ds(bg, 1)].squeeze(0).rearrange("r a j -> r (a j)").unsqueeze(1)
                                 .to_broadcast([2, 2, QROW])).then_inc(s_in[k], 16)
                    for q in range(2):
                        sp.dma_start(S[k][4 + 2 * dup:6 + 2 * dup, q].bitcast(F32),
                                     K.dy[bass.ds(it * 2 + k, 1), :, q].squeeze(0).unsqueeze(1)
                                     .to_broadcast([2, W, J])).then_inc(s_in[k], 16)
            load(0, 0, 0)
            load(0, 0, 1)
            to, fr = K.WR[:].rearrange("p f a o -> p (f a o)"), K.dram["mlp_w"].rearrange("p f a o -> p (f a o)")
            piece = to.shape[-1] // N
            sp.dma_start(to[:, 0:piece], fr[:, 0:piece]).then_inc(K.mlp_in, 16)
            with sp.Fori(1, N) as it:
                for k in range(2):
                    sp.wait_ge(l1, it * 8 + 4 * k - 4)
                    load(it, it // 8, k)
                sp.dma_start(to[:, bass.ds(it * piece, piece)], fr[:, bass.ds(it * piece, piece)]).then_inc(K.mlp_in, 16)

        @block.tensor
        def _(pe):
            def layer_one(u):
                k, q, part = (u // 4) % 2, (u // 2) % 2, u % 2
                row = S[k][:, q].rearrange("r a j -> r (a j)")
                for a in range(2):
                    at = TILE * part + BANK * a
                    last = nc.tensor.matmul(p1[u % 2][:, BANK * a:BANK * (a + 1)], K.W1R[32 * k:32 * k + ROWS], row[:, at:at + BANK],
                                            start=True, stop=True)
                last.then_inc(l1, 1)

            def layer_three(par):
                for g in range(4):
                    last = nc.tensor.matmul(p3[32 * g:32 * g + 32, :], K.W3[:], h2[par][:, BANK * g:BANK * (g + 1)],
                                            start=True, stop=True, tile_position=(0, 32 * g))
                last.then_inc(l3, 1)

            pe.wait_ge(s_in[0], LOADS)
            layer_one(0)
            layer_one(1)

            def body(it, first, last):
                for u in range(8):
                    t = it * 8 + u
                    pe.wait_ge(hi_done, t + 1)
                    out = (p2[u % 2], p2[2])
                    for a in range(2):
                        if a == 0 and not (first and u < 2):
                            pe.wait_ge(relu_a, t - 1)
                        if a == 1 and not (first and u == 0):
                            pe.wait_ge(relu_b, t)
                        h = hh[u % 2][:, BANK * a:BANK * (a + 1)]
                        nc.tensor.matmul(out[a][:], K.W2H[:], h, start=True, stop=False)
                        nc.tensor.matmul(out[a][:], K.W2L[:], h, start=False, stop=False)
                        if a == 0:
                            pe.wait_ge(lo_done, t + 1)
                        nc.tensor.matmul(out[a][:], K.W2H[:], hl[u % 2][:, BANK * a:BANK * (a + 1)],
                                         start=False, stop=True).then_inc(l2, 1)
                    if not (last and u >= 6):
                        if u == 2:
                            pe.wait_ge(s_in[1], (it + 1) * LOADS)
                        if u == 6:
                            pe.wait_ge(s_in[0], (it + 2) * LOADS)
                        layer_one((u + 2) % 8)
                    if u % 2 == 0 and not (first and u == 0):
                        pe.wait_ge(relu_a, t)
                        pe.wait_ge(relu_b, t)
                        if not (first and u == 2):
                            pe.wait_ge(copied, it * 4 + u // 2 - 1)
                        layer_three((u // 2 - 1) % 2)

            body(0, True, False)
            with pe.Fori(1, N - 1) as it:
                body(it, False, False)
            body(N - 1, False, True)
            pe.wait_ge(relu_a, N * 8)
            pe.wait_ge(relu_b, N * 8)
            pe.wait_ge(copied, N * 4 - 1)
            layer_three(1)

        @block.scalar
        def _(act):
            def high(it, u):
                act.wait_ge(l1, it * 8 + u + 1)
                nc.scalar.activation(hh[u % 2][:], p1[u % 2][:], ACT.Relu).then_inc(hi_done, 1)

            def copy_rows(it, row, first):
                act.wait_ge(l3, it * 4 + row + 1)
                k = row // 2
                if row % 2 == 0 and not first:
                    act.wait_ge(rows_out[k], it * 16)
                nc.scalar.activation(br[k][:, row % 2, :], p3[:], ACT.Identity, bias=K.v("cpb_b3")).then_inc(copied, 1)

            high(0, 0)
            high(0, 1)

            def body(it, first, last):
                for u in range(8):
                    t = it * 8 + u
                    act.wait_ge(l2, t * 2 + 2)
                    if not first or u >= 4:
                        act.wait_ge(l3, it * 4 + u // 2 - 1)
                    at = (u % 2) * TILE + BANK
                    nc.scalar.activation(h2[(u // 2) % 2][:, at:at + BANK], p2[2][:], ACT.Relu,
                                         bias=K.v("cpb_b2")).then_inc(relu_b, 1)
                    if not (last and u >= 6):
                        high(it if u < 6 else it + 1, (u + 2) % 8)
                    if u % 2 == 0 and not (first and u == 0):
                        if u == 0:
                            copy_rows(it - 1, 3, False)
                        else:
                            copy_rows(it, u // 2 - 1, first)

            body(0, True, False)
            with act.Fori(1, N - 1) as it:
                body(it, False, False)
            body(N - 1, False, True)
            copy_rows(N - 1, 3, False)

        @block.vector
        def _(dve):
            def low(it, u):
                dve.wait_ge(hi_done, it * 8 + u + 1)
                nc.vector.scalar_tensor_tensor(hl[u % 2][:], p1[u % 2][:], 0.0, hh[u % 2][:].bitcast(F32),
                                               ALU.max, ALU.subtract).then_inc(lo_done, 1)

            low(0, 0)
            low(0, 1)

            def body(it, first, last):
                for u in range(8):
                    t = it * 8 + u
                    dve.wait_ge(l2, t * 2 + 1)
                    if not first or u >= 4:
                        dve.wait_ge(l3, it * 4 + u // 2 - 1)
                    at = (u % 2) * TILE
                    nc.vector.tensor_scalar(h2[(u // 2) % 2][:, at:at + BANK], p2[u % 2][:], K.v("cpb_b2"), 0.0,
                                            ALU.add, ALU.max).then_inc(relu_a, 1)
                    if not (last and u >= 6):
                        low(it if u < 6 else it + 1, (u + 2) % 8)

            body(0, True, False)
            with dve.Fori(1, N - 1) as it:
                body(it, False, False)
            body(N - 1, False, True)

        @block.gpsimd
        def _(pool):
            with pool.Fori(0, N) as it:
                for k in range(2):
                    pool.wait_ge(copied, it * 4 + 2 * k + 2)
                    pool.dma_start(K.db[bass.ds(it * 2 + k, 1)].squeeze(0).rearrange("q g n -> g q n"),
                                   br[k][0:P:32]).then_inc(rows_out[k], 16)
            for k in range(2):
                pool.wait_ge(rows_out[k], 16 * N)


def stage_attention(K, sb, ps):
    nc = K.nc
    room = carver(K.HA[:, 0:W_FIRST], K.XNA)
    bi = [room([P, HALF, PC, J]) for _ in range(2)]
    sc = [room([P, PC, HALF, J]) for _ in range(4)]
    at = [room([P, HW]) for _ in range(2)]
    pr = [room([P, PC, HALF, J]) for _ in range(2)]
    OW = carver(K.XNB)([P, CC, C])
    mx, sm = sb("smax", [P, PC * HALF]), sb("ssum", [P, PC * HALF])
    rs = [sb(f"srec{i}", [P, PC * HALF]) for i in range(2)]
    sps = [ps(f"score_ps{i}", [P, PC, P]) for i in range(2)]
    tps, ops = ps("probsT_ps", [P, HW]), ps("att_ps", [P, HW])
    b_in, s_mm, ex = [K.sem(f"bias_in{i}") for i in range(2)], K.sem("score_mm"), K.sem("soft_exp")
    added, peaked, shifted, summed, recip, scaled = (K.sem("bias_added"), K.sem("soft_max"), K.sem("soft_shift"),
                                                     K.sem("soft_sum"), K.sem("soft_recip"), K.sem("soft_scaled"))
    t_mm, t_out, o_mm, o_out = K.sem("probsT_mm"), K.sem("probsT_out"), K.sem("att_mm"), K.sem("att_out")
    ow_in = K.sem("out_w_loaded")

    def rows(t):
        return t[:].rearrange("p s h j -> p (s h) j")

    def wide(t):
        return t[:].unsqueeze(2).to_broadcast([P, PC * HALF, J])

    with nc.Block() as block:
        @block.sync
        def _(sp):
            for g in range(BLK):
                if g >= 2:
                    sp.wait_ge(added, g - 1)
                for h in range(HALF):
                    sp.dma_start(bi[g % 2][:, h], K.db_bg[HALF * g + h].rearrange("(s p) j -> p s j", p=P)).then_inc(b_in[g % 2], 16)
                if g == 1:
                    sp.dma_start(OW, K.dram["out_wT"]).then_inc(ow_in, 16)

        @block.tensor
        def _(pe):
            for k in range(BLK + 4):
                if k < BLK:
                    if k >= 2:
                        pe.wait_ge(added, k - 1)
                    for s in range(PC):
                        last = nc.tensor.matmul(sps[k % 2][:, s], K.Q[:, k, s * P:(s + 1) * P], K.KBD[:, k], start=True, stop=True)
                    last.then_inc(s_mm, 1)
                if k >= 4:
                    g = k - 4
                    pe.wait_ge(t_out, g + 1)
                    if g >= 1:
                        pe.wait_ge(o_out, g)
                    for t in range(NT):
                        last = nc.tensor.matmul(ops[:, t * BANK:(t + 1) * BANK], K.VBD[:, g], at[g % 2][:, t * BANK:(t + 1) * BANK],
                                                start=True, stop=True)
                    last.then_inc(o_mm, 1)
                if 3 <= k < BLK + 3:
                    g = k - 3
                    pe.wait_ge(scaled, g + 1)
                    if g >= 1:
                        pe.wait_ge(t_out, g)
                    for s in range(PC):
                        last = nc.tensor.transpose(tps[:, s * P:(s + 1) * P], pr[g % 2][:, s].rearrange("p h j -> p (h j)"), K.k("ident"))
                    last.then_inc(t_mm, 1)

        @block.vector
        def _(dve):
            for k in range(BLK + 1):
                if k < BLK:
                    dve.wait_ge(s_mm, k + 1)
                    dve.wait_ge(b_in[k % 2], 16 * HALF * (k // 2 + 1))
                    if k >= 4:
                        dve.wait_ge(scaled, k - 3)
                    nc.vector.tensor_tensor(sc[k % 4], sps[k % 2][:].rearrange("p s (h j) -> p s h j", h=HALF),
                                            bi[k % 2].rearrange("p h s j -> p s h j"), ALU.add).then_inc(added, 1)
                    dve.wait_ge(added, k + 1)
                    if k:
                        dve.wait_ge(shifted, k)
                    nc.vector.tensor_reduce(mx[:], rows(sc[k % 4]), AX.X, ALU.max).then_inc(peaked, 1)
                if k:
                    g = k - 1
                    dve.wait_ge(ex, g + 1)
                    if g:
                        dve.wait_ge(recip, g)
                    nc.vector.tensor_reduce(sm[:], rows(sc[g % 4]), AX.X, ALU.add).then_inc(summed, 1)
                    dve.wait_ge(summed, g + 1)
                    if g >= 2:
                        dve.wait_ge(scaled, g - 1)
                    nc.vector.reciprocal(rs[g % 2][:], sm[:]).then_inc(recip, 1)
            dve.wait_ge(K.ow_split, 1)
            nc.vector.tensor_tensor(K.ow_lo, OW, K.ow_hi.bitcast(F32), ALU.subtract).then_inc(K.ow_split, 1)
            dve.wait_ge(K.ao_high, 1)
            nc.vector.tensor_tensor(K.ao_lo(0), K.ao(0), K.ao_hi(0).bitcast(F32), ALU.subtract).then_inc(K.ao_low, 1)

        @block.gpsimd
        def _(pool):
            for k in range(BLK + 1):
                if k < BLK:
                    pool.wait_ge(peaked, k + 1)
                    nc.gpsimd.tensor_tensor(rows(sc[k % 4]), rows(sc[k % 4]), wide(mx), ALU.subtract).then_inc(shifted, 1)
                if k:
                    g = k - 1
                    pool.wait_ge(recip, g + 1)
                    if g >= 2:
                        pool.wait_ge(t_mm, g - 1)
                    nc.gpsimd.tensor_tensor(rows(pr[g % 2]), rows(sc[g % 4]), wide(rs[g % 2]), ALU.mult).then_inc(scaled, 1)

        @block.scalar
        def _(act):
            for k in range(BLK + 5):
                if k >= 5:
                    act.wait_ge(o_mm, k - 4)
                    nc.scalar.activation(K.Q[:, k - 5], ops[:], ACT.Copy).then_inc(o_out, 1)
                if 4 <= k < BLK + 4:
                    g = k - 4
                    act.wait_ge(t_mm, g + 1)
                    if g >= 2:
                        act.wait_ge(o_mm, g - 1)
                    nc.scalar.activation(at[g % 2], tps[:], ACT.Copy).then_inc(t_out, 1)
                if 1 <= k <= BLK:
                    act.wait_ge(shifted, k)
                    e = flat(sc[(k - 1) % 4][:])
                    nc.scalar.activation(e, e, ACT.Exp).then_inc(ex, 1)
                if k == 3:
                    act.wait_ge(ow_in, 16)
                    nc.scalar.activation(K.ow_hi, OW, ACT.Copy).then_inc(K.ow_split, 1)
                if k == BLK + 3:
                    act.wait_ge(o_out, BLK - 1)
                    nc.scalar.activation(K.ao_hi(0), K.ao(0), ACT.Copy).then_inc(K.ao_high, 1)


def stage_out_proj(K, sb, ps):
    nc = K.nc
    pp = [ps(f"proj_ps{i}", [P, BANK]) for i in range(4)]
    mm, out, s2d, wh_done, wl_done = K.sem("proj_mm"), K.sem("proj_out"), K.sem("s2_ready"), K.sem("w_hi_done"), K.sem("w_lo_done")
    K.xh_done, K.xl_done, K.x_step = K.sem("xn2_hi_done"), K.sem("xn2_lo_done"), K.sem("xn2_step")
    x_high, x_low = split_norm(K, 0, ps("norm_ps", [P, BANK]), K.xh_done, K.xl_done)
    TILES = B * NT
    with nc.Block() as block:
        @block.tensor
        def _(pe):
            for i in range(TILES * CC):
                n, o = divmod(i, CC)
                pe.wait_ge(K.ao_low, n + 1)
                if i >= 4:
                    pe.wait_ge(out, i - 3)
                part = slice(o * P, (o + 1) * P)
                for c in range(CC):
                    pairs = ((K.ow_hi, K.ao_hi(n)), (K.ow_lo, K.ao_hi(n)), (K.ow_hi, K.ao_lo(n)))
                    for k, (w, x) in enumerate(pairs):
                        last = nc.tensor.matmul(pp[i % 4][:], w[:, c, part], x[:, c],
                                                start=(c == 0 and k == 0), stop=(c == CC - 1 and k == 2))
                last.then_inc(mm, 1)

        @block.vector
        def _(dve):
            nc.vector.tensor_scalar(K.s2[:], K.v("bn2_g", 0, CC), float(1.0 / np.sqrt(1.0 + EPS)), None,
                                    ALU.mult).then_inc(s2d, 1)
            dve.wait_ge(s2d, 1)
            for i in range(TILES * CC):
                n, o = divmod(i, CC)
                b, t = divmod(n, NT)
                if o == 0 and n + 1 < TILES:
                    dve.wait_ge(K.ao_high, n + 2)
                    nc.vector.tensor_tensor(K.ao_lo(n + 1), K.ao(n + 1), K.ao_hi(n + 1).bitcast(F32), ALU.subtract).then_inc(K.ao_low, 1)
                x = K.X[:, o, b, t * BANK:(t + 1) * BANK]
                dve.wait_ge(mm, i + 1)
                nc.vector.scalar_tensor_tensor(x, pp[i % 4][:], K.v("out_b", o), x, ALU.add, ALU.add).then_inc(out, 1)
                if n == 1:
                    x_low(o, dve, K.x_step)
                if i % 2 and i // 2 < W_FIRST:
                    f = i // 2
                    dve.wait_ge(wh_done, f + 1)
                    nc.vector.tensor_tensor(flat(K.w_lo[:, f]), flat(K.WR[:, f]), flat(K.w_hi[:, f]).bitcast(F32),
                                            ALU.subtract).then_inc(wl_done, 1)

        @block.scalar
        def _(act):
            def high(n):
                if n >= 2:
                    act.wait_ge(mm, CC * (n - 1))
                nc.scalar.activation(K.ao_hi(n), K.ao(n), ACT.Copy).then_inc(K.ao_high, 1)

            high(1)
            act.wait_ge(K.mlp_in, 16 * K.mlp_pieces)
            for f in range(W_FIRST):
                nc.scalar.activation(flat(K.w_hi[:, f]), flat(K.WR[:, f]), ACT.Copy).then_inc(wh_done, 1)
            act.wait_ge(s2d, 1)
            high(2)
            for c in range(CC):
                act.wait_ge(out, c + 1)
                x_high(c)
            high(3)


def stage_mlp(K, sb, ps):
    nc = K.nc
    parts = [(K.w_hi[:, f] if f < FC // 2 else K.w_hi2[:, f - FC // 2], K.w_lo[:, f]) for f in range(FC)]
    hid = [(s[:, 0], s[:, 1]) for s in K.hid]
    SLOTS = len(hid)
    pa = [ps(f"mlp_ps{i}", [P, BANK]) for i in range(3)]
    pb = [ps(f"mlp_out_ps{i}", [P, BANK]) for i in range(CC)]
    tmp = ps("norm_ps2", [P, BANK])
    m1, ge, lo_done, m2, out, w_step = (K.sem("mlp1_mm"), K.sem("mlp_gelu"), K.sem("hidden_lo"), K.sem("mlp2_mm"),
                                        K.sem("mlp_out"), K.sem("w_split"))
    PAIRS = ((0, 0), (1, 0), (0, 1))
    N = B * NT * FC
    NORM = range(4, 4 + CC)
    room = carver(K.HA)
    K.lin_w = [room([P, CC, C]) for _ in range(4)]
    K.lin_b = [flat(K.XNA[:])[:, i * C:(i + 1) * C] for i in range(2)]
    K.lin_in = K.sem("l1_w_loaded")
    with nc.Block() as block:
        @block.sync
        def _(sp):
            sp.wait_ge(m2, N - FC // 2)
            for t, n in zip(K.lin_w, ("WqT", "WvT", "Wk", "WoT")):
                sp.dma_start(t, K.dram[n]).then_inc(K.lin_in, 16)
            for t, n in zip(K.lin_b, ("bq", "bv")):
                sp.dma_start(t, K.dram[n].partition_broadcast(P)).then_inc(K.lin_in, 16)

        @block.gpsimd
        def _(pool):
            for f in range(W_FIRST, FC):
                hi, lo = (flat(w) for w in parts[f])
                nc.gpsimd.tensor_copy(hi, flat(K.WR[:, f])).then_inc(w_step, 1)
                pool.wait_ge(w_step, 2 * (f - W_FIRST) + 1)
                nc.gpsimd.tensor_tensor(lo, flat(K.WR[:, f]), hi.bitcast(F32), ALU.subtract).then_inc(w_step, 1)

        @block.tensor
        def _(pe):
            def hidden(n):
                bt, f = divmod(n, FC)
                if f == 0 and bt:
                    pe.wait_ge(K.xl_done, CC * (bt + 1))
                if bt == 0 and f >= W_FIRST:
                    pe.wait_ge(w_step, 2 * (f - W_FIRST) + 2)
                if n >= 3:
                    pe.wait_ge(lo_done, n - 2)
                for c in range(CC):
                    for i, (w, x) in enumerate(PAIRS):
                        last = nc.tensor.matmul(pa[n % 3][:], parts[f][w][:, 0, c * P:(c + 1) * P],
                                                K.xn2[bt % 2][x][:, c],
                                                start=(c == 0 and i == 0), stop=(c == CC - 1 and i == 2))
                last.then_inc(m1, 1)

            def gather(n):
                bt, f = divmod(n, FC)
                pe.wait_ge(lo_done, n + 1)
                for o in range(CC):
                    if f == 0 and bt:
                        pe.wait_ge(out, (bt - 1) * CC + o + 1)
                    for i, (w, x) in enumerate(PAIRS):
                        last = nc.tensor.matmul(pb[o][:], parts[f][w][:, 1, o * P:(o + 1) * P],
                                                hid[n % SLOTS][x],
                                                start=(f == 0 and i == 0), stop=(f == FC - 1 and i == 2))
                last.then_inc(m2, 1)

            hidden(0)
            for n in range(N):
                if n + 1 < N:
                    hidden(n + 1)
                gather(n)

        @block.scalar
        def _(act):
            for n in range(N):
                bt, f = divmod(n, FC)
                act.wait_ge(m1, n + 1)
                if n >= SLOTS:
                    act.wait_ge(m2, n - SLOTS + 1)
                nc.scalar.activation(hid[n % SLOTS][0], pa[n % 3][:], ACT.Gelu, bias=K.v("mlp_b1", f))
                nc.scalar.activation(pa[n % 3][:], pa[n % 3][:], ACT.Gelu, bias=K.v("mlp_b1", f)).then_inc(ge, 1)
                if f in NORM and bt + 1 < B * NT:
                    split_norm(K, bt + 1, tmp, K.xh_done, K.xl_done)[0](f - NORM[0])

        @block.vector
        def _(dve):
            def add(bt):
                b, t = divmod(bt, NT)
                dve.wait_ge(m2, (bt + 1) * FC)
                for o in range(CC):
                    x = K.X[:, o, b, t * BANK:(t + 1) * BANK]
                    nc.vector.scalar_tensor_tensor(x, pb[o][:], K.v("mlp_b2", o), x, ALU.add, ALU.add).then_inc(out, 1)

            for n in range(N):
                bt, f = divmod(n, FC)
                hi, lo = hid[n % SLOTS]
                dve.wait_ge(ge, n + 1)
                nc.vector.tensor_tensor(lo, pa[n % 3][:], hi.bitcast(F32), ALU.subtract).then_inc(lo_done, 1)
                if f == 0 and bt:
                    add(bt - 1)
                if f in NORM and bt + 1 < B * NT:
                    split_norm(K, bt + 1, tmp, K.xh_done, K.xl_done)[1](f - NORM[0], dve, K.x_step)
            add(B * NT - 1)


def stage_linear(K, sb, ps):
    nc = K.nc
    d = K.dram
    wq, wv, wk, wo = K.lin_w
    bqr, bvr = K.lin_b
    room = carver(K.WR)
    xt, gram = [room([P, PC, C]) for _ in range(B)], [room([P, CC, C]) for _ in range(B)]
    gq = room([P, CC, C])
    room([P, CC, C])
    mt = sb("mt", [P, CC, P])
    low = carver(K.w_lo)
    xp = [[low([P, CC, BANK]) for _ in range(2)] for _ in range(2)]
    tt = [low([P, CC, C]) for _ in range(2)]
    low([P, CC, C])
    aT = [sb("aT_hi", [P, CC, C], F32R), low([P, CC, C])]
    wkp = [K.xn2[0][1], K.w_hi[:, 4:6].rearrange("p f a o -> p (f a) o")]
    xs, wrow, brow = sb("x_sums", [P, B, CC]), sb("wq_s", [1, C]), sb("bias_row", [1, C])
    bkp = [sb(f"bk_part{i}", [P, CC], F32R) for i in range(2)]
    bb = sb("lin_bias", [P, CC])
    Y = carver(K.Q)([P, CC, B, HW])
    st = sb("bn_st", [P, CC, B * NT, 6])
    mv, inv, sh = sb("bn_mv", [P, CC, 2]), sb("bn_inv", [P, CC]), sb("bn_sh", [P, CC])
    bank = [ps(f"lin_ps{i}", [P, BANK]) for i in range(8)]
    w_in, zero = K.lin_in, K.sem("mt_zeroed")
    mm, by_act, by_dve, summed = K.sem("lin_mm"), K.sem("lin_act"), K.sem("lin_dve"), K.sem("x_summed")
    high, x_high, x_low, wk_split = K.sem("lin_high"), K.sem("x_high"), K.sem("x_low"), K.sem("wk_split")
    s_step, sq, nrm = K.sem("bn_step"), K.sem("bn_sqrt"), K.sem("bn_done")

    def tasks(kind, b, *index):
        return [(kind, b, i) for i in index]

    ORDER = (tasks("turn", 0, *range(PC)) + tasks("turn", 1, *range(PC)) + tasks("gram", 0, *range(CC)) + tasks("row", 0, 0)
             + tasks("gram", 1, 0) + tasks("mirror", 0, *range(1, CC)) + tasks("gram", 1, 1) + tasks("times_q", 0, *range(CC))
             + tasks("gram", 1, 2, 3) + tasks("m", 0, 0) + tasks("row", 1, 0) + tasks("mirror", 1, *range(1, CC))
             + tasks("times_q", 1, 0, 1) + tasks("times_o", 0, *range(CC)) + tasks("times_q", 1, 2, 3)
             + tasks("times_k", 0, *range(CC)) + tasks("bias_row", 0, 0) + tasks("m", 1, 0) + tasks("bias", 0, 0) + tasks("y", 0, 0, 1, 2, 3)
             + tasks("times_o", 1, *range(CC)) + tasks("y", 0, 4, 5, 6, 7) + tasks("bias_row", 1, 0) + tasks("times_k", 1, *range(CC))
             + tasks("bias", 1, 0) + tasks("y", 1, *range(NT * CC)))
    AT = {task: n for n, task in enumerate(ORDER)}
    PAIRS = ((0, 0), (1, 0), (0, 1))
    SPLIT = ("times_o", "times_k")
    on_act = [k == "gram" or (k == "turn" and i % 2 == 1) for k, _, i in ORDER]

    def emptied(engine, n):
        engine.wait_ge(by_act if on_act[n] else by_dve, sum(on_act[m] == on_act[n] for m in range(n + 1)))

    TILE_AT = {("times_o", 0, 0): 0, ("times_q", 1, 2): 1, ("y", 0, 4): 2, ("y", 1, 0): 3}

    def x_tile(tile):
        b, t = divmod(tile, NT)
        return K.X[:, :, b, t * BANK:(t + 1) * BANK]

    with nc.Block() as block:
        @block.sync
        def _(sp):
            for t, n in zip(K.fgh_w, ("wfT", "wgT", "whT")):
                sp.dma_start(t, d[n]).then_inc(K.nl_in, 16)
            sp.dma_start(K.nl_wv, d["wvT"]).then_inc(K.nl_in, 16)
            sp.dma_start(K.bhr[:], d["bh"].partition_broadcast(P)).then_inc(K.nl_in, 16)
            sp.dma_start(K.se1[:], d["se1_wT"]).then_inc(K.se_in, 16)
            sp.dma_start(K.se2[:], d["se2_wT"]).then_inc(K.se_in, 16)

        @block.gpsimd
        def _(pool):
            nc.gpsimd.memset(mt[:], 0.0).then_inc(zero, 1)

        @block.tensor
        def _(pe):
            pe.wait_ge(w_in, 96)
            for n, (kind, b, i) in enumerate(ORDER):
                out = bank[n % 8]

                def need(kind, *index):
                    for k in index:
                        emptied(pe, AT[(kind, b, k)])

                if n >= 8:
                    emptied(pe, n - 8)
                if kind == "turn":
                    for c in range(CC):
                        last = nc.tensor.transpose(out[:, c * P:(c + 1) * P], K.X[:, c, b, i * P:(i + 1) * P], K.k("ident"))
                elif kind == "gram":
                    need("turn", PC - 2, PC - 1)
                    for s in range(PC):
                        last = nc.tensor.matmul(out[:, i * P:], xt[b][:, s, i * P:(i + 1) * P], xt[b][:, s, i * P:],
                                                start=(s == 0), stop=(s == PC - 1))
                elif kind == "mirror":
                    need("gram", i - 1)
                    for c in range(i):
                        last = nc.tensor.transpose(out[:, c * P:(c + 1) * P], gram[b][:, c, i * P:(i + 1) * P], K.k("ident"))
                elif kind == "row":
                    pe.wait_ge(summed, b + 1)
                    for c in range(CC):
                        last = nc.tensor.matmul(out[0:1, :], xs[:, b, c:c + 1], wq[:, c], start=(c == 0), stop=(c == CC - 1))
                elif kind == "times_q":
                    need("gram", CC - 1)
                    need("mirror", CC - 1)
                    for c in range(CC):
                        last = nc.tensor.matmul(out[:], gram[b][:, c, i * P:(i + 1) * P], wq[:, c], start=(c == 0), stop=(c == CC - 1))
                elif kind == "m":
                    need("times_q", CC - 1)
                    need("row", 0)
                    for o in range(CC):
                        part = slice(o * P, (o + 1) * P)
                        for c in range(CC):
                            nc.tensor.matmul(out[:, part], wv[:, c, part], gq[:, c, part], start=(c == 0), stop=False)
                        last = nc.tensor.matmul(out[:, part], bvr[0:1, part], wrow[:, part], start=False, stop=True)
                elif kind == "times_o":
                    need("m", 0)
                    last = nc.tensor.matmul(out[:], mt[:, i], wo[:, i], start=True, stop=True)
                elif kind == "times_k":
                    need("times_o", CC - 1)
                    pe.wait_ge(wk_split, 2)
                    for c in range(CC):
                        for k, (w, x) in enumerate(PAIRS):
                            last = nc.tensor.matmul(out[:], wkp[w][:, c, i * P:(i + 1) * P], aT[x][:, c],
                                                    start=(c == 0 and k == 0), stop=(c == CC - 1 and k == 2))
                elif kind == "bias_row":
                    need("times_o", CC - 1)
                    for c in range(CC):
                        for k, (w, x) in enumerate(PAIRS):
                            last = nc.tensor.matmul(out[0:1, :], bkp[w][:, c:c + 1], aT[x][:, c],
                                                    start=(c == 0 and k == 0), stop=(c == CC - 1 and k == 2))
                elif kind == "bias":
                    need("bias_row", 0)
                    for o in range(CC):
                        last = nc.tensor.matmul(out[:, o:o + 1], brow[:, o * P:(o + 1) * P], K.k("ident", 0, 1, p1=1),
                                                start=True, stop=True)
                elif kind == "y":
                    need("times_k", CC - 1)
                    t, o = divmod(i, CC)
                    tile = b * NT + t
                    pe.wait_ge(x_low, tile + 1)
                    for c in range(CC):
                        for k, (w, x) in enumerate(PAIRS):
                            last = nc.tensor.matmul(out[:], tt[w][:, c, o * P:(o + 1) * P], xp[tile % 2][x][:, c],
                                                    start=(c == 0 and k == 0), stop=(c == CC - 1 and k == 2))
                last.then_inc(mm, 1)

        @block.vector
        def _(dve):
            dve.wait_ge(zero, 1)
            stats = 0
            for n, (kind, b, i) in enumerate(ORDER):
                src = bank[n % 8]
                if kind == "gram" and i == 0:
                    nc.vector.tensor_reduce(xs[:, b], K.X[:, :, b], AX.X, ALU.add).then_inc(summed, 1)
                if (kind, b, i) in TILE_AT:
                    tile = TILE_AT[(kind, b, i)]
                    dve.wait_ge(x_high, tile + 1)
                    nc.vector.tensor_tensor(xp[tile % 2][1], x_tile(tile), xp[tile % 2][0].bitcast(F32), ALU.subtract).then_inc(x_low, 1)
                if (kind, b, i) == ("gram", 0, 1):
                    dve.wait_ge(wk_split, 1)
                    nc.vector.tensor_tensor(bkp[1][:], K.v("bk", 0, CC), bkp[0][:].bitcast(F32), ALU.subtract)
                    nc.vector.tensor_tensor(wkp[1], wk, wkp[0].bitcast(F32), ALU.subtract).then_inc(wk_split, 1)
                if on_act[n]:
                    continue
                dve.wait_ge(mm, n + 1)
                if kind == "turn":
                    nc.vector.tensor_copy(xt[b][:, i], src[:]).then_inc(by_dve, 1)
                elif kind == "mirror":
                    nc.vector.tensor_copy(gram[b][:, i, 0:i * P], src[:, 0:i * P]).then_inc(by_dve, 1)
                elif kind == "row":
                    nc.vector.scalar_tensor_tensor(wrow[:], bqr[0:1], float(HW), src[0:1, :], ALU.mult, ALU.add).then_inc(by_dve, 1)
                elif kind == "times_q":
                    dve.wait_ge(summed, b + 1)
                    nc.vector.scalar_tensor_tensor(gq[:, i], bqr, xs[:, b, i:i + 1], src[:], ALU.mult, ALU.add).then_inc(by_dve, 1)
                elif kind == "m":
                    m = src[:].rearrange("p (c m) -> p c m", c=CC)
                    nc.vector.tensor_copy(mt[0:DH, :, 0:DH], m[0:DH, :, 0:DH])
                    nc.vector.tensor_copy(mt[DH:P, :, DH:P], m[DH:P, :, DH:P]).then_inc(by_dve, 1)
                elif kind in SPLIT:
                    part = {"times_o": aT, "times_k": tt}[kind]
                    dve.wait_ge(high, sum(k in SPLIT for k, _, _ in ORDER[:n + 1]))
                    nc.vector.tensor_tensor(part[1][:, i], src[:], part[0][:, i].bitcast(F32), ALU.subtract).then_inc(by_dve, 1)
                elif kind == "bias_row":
                    nc.vector.tensor_copy(brow[:], src[0:1, :]).then_inc(by_dve, 1)
                elif kind == "bias":
                    nc.vector.tensor_tensor(bb[:], src[:, 0:CC], K.v("bo", 0, CC), ALU.add).then_inc(by_dve, 1)
                elif kind == "y":
                    t, o = divmod(i, CC)
                    emptied(dve, AT[("bias", b, 0)])
                    part = Y[:, o, b, t * BANK:(t + 1) * BANK]
                    nc.vector.scalar_tensor_tensor(part, src[:], bb[:, o:o + 1],
                                                   K.X[:, o, b, t * BANK:(t + 1) * BANK], ALU.add, ALU.add).then_inc(by_dve, 1)
                    emptied(dve, n)
                    nc.vector.bn_stats(st[:, o, b * NT + t], part).then_inc(s_step, 1)
            n = CC * B * NT
            dve.wait_ge(s_step, n)
            for o in range(CC):
                nc.vector.bn_aggr(mv[:, o], flat(st[:, o])).then_inc(s_step, 1)
                n += 1
            dve.wait_ge(sq, 1)
            nc.vector.reciprocal(sh[:], inv[:]).then_inc(s_step, 1)
            dve.wait_ge(s_step, n + 1)
            nc.vector.tensor_tensor(inv[:], sh[:], K.v("gamma", 0, CC), ALU.mult).then_inc(s_step, 1)
            dve.wait_ge(s_step, n + 2)
            nc.vector.tensor_tensor(sh[:], mv[:, :, 0], inv[:], ALU.mult).then_inc(s_step, 1)
            dve.wait_ge(s_step, n + 3)
            nc.vector.tensor_tensor(sh[:], K.v("beta", 0, CC), sh[:], ALU.subtract).then_inc(s_step, 1)
            dve.wait_ge(s_step, n + 4)
            for o, b in [(o, b) for o in range(2) for b in range(B)] + [(2, 0)]:
                nc.vector.tensor_scalar(K.X[:, o, b], Y[:, o, b], inv[:, o:o + 1], sh[:, o:o + 1], ALU.mult, ALU.add).then_inc(nrm, 1)

        @block.scalar
        def _(act):
            for n, (kind, b, i) in enumerate(ORDER):
                if (kind, b, i) in TILE_AT:
                    tile = TILE_AT[(kind, b, i)]
                    act.wait_ge(mm, AT[("gram", 1, CC - 1)] + 1 if tile < 2 else AT[("y", (tile - 2) // NT, CC * ((tile - 2) % NT) + CC - 1)] + 1)
                    nc.scalar.activation(xp[tile % 2][0], x_tile(tile), ACT.Copy).then_inc(x_high, 1)
                if (kind, b, i) == ("gram", 0, 0):
                    nc.scalar.activation(bkp[0][:], K.v("bk", 0, CC), ACT.Copy)
                    nc.scalar.activation(wkp[0], wk, ACT.Copy).then_inc(wk_split, 1)
                src = bank[n % 8][:]
                if on_act[n]:
                    act.wait_ge(mm, n + 1)
                    if kind == "gram":
                        nc.scalar.activation(gram[b][:, i, i * P:], src[:, i * P:], ACT.Copy).then_inc(by_act, 1)
                    else:
                        nc.scalar.activation(xt[b][:, i], src, ACT.Copy).then_inc(by_act, 1)
                elif kind in SPLIT:
                    act.wait_ge(mm, n + 1)
                    nc.scalar.activation({"times_o": aT, "times_k": tt}[kind][0][:, i], src, ACT.Copy).then_inc(high, 1)
            N_ST = CC * B * NT + CC
            act.wait_ge(s_step, N_ST)
            act.wait_ge(K.eps_ready, 1)
            nc.scalar.activation(inv[:], mv[:, :, 1], ACT.Sqrt, bias=K.eps[:]).then_inc(sq, 1)
            act.wait_ge(s_step, N_ST + 4)
            for o, b in ((2, 1), (3, 0), (3, 1)):
                nc.scalar.activation(K.X[:, o, b], Y[:, o, b], ACT.Identity, bias=sh[:, o:o + 1], scale=inv[:, o:o + 1])


def stage_nonlocal(K, sb, ps):
    nc = K.nc
    wf, wg, wh = K.fgh_w
    wv, bhr = K.nl_wv, K.bhr
    room = carver(K.WR)
    room([P, 4 * B * HW])
    low = carver(K.w_lo)
    fg = [[low([P, B, HW]) for _ in range(2)] for _ in range(2)]
    PAIRS = ((0, 0), (1, 0), (0, 1))
    hT = room([P, B * PC, MID])
    ex = [room([P, HW]) for _ in range(3)]
    z = room([P, HW])
    eT = carver(K.Q)([P, PC, HW])
    sc, bi = sb("fg_sc", [P, 2]), sb("fg_bi", [P, 2])
    nm, sm, rs = sb("nmax", [P, B * PC]), sb("esum", [P, B * PC]), sb("erec", [P, B * PC])
    sps = [ps(f"fg_ps{i}", [P, HW]) for i in range(2)]
    tps = ps("eT_ps", [P, HW])
    zps = [ps(f"z_ps{i}", [P, BANK]) for i in range(2)]
    SC = float(MID) ** -0.5
    w_in, cf, cs = K.nl_in, K.sem("fg_coef"), K.sem("fg_sqrt")
    fg_mm, fg_out, fg_low, h_mm, h_out = K.sem("fg_mm"), K.sem("fg_out"), K.sem("fg_low"), K.sem("h_mm"), K.sem("h_out")
    s_mm, mxd, exd, sts, t_mm, t_out = K.sem("nl_score"), K.sem("nl_max"), K.sem("nl_exp"), K.sem("nl_step"), K.sem("nl_tr"), K.sem("nl_tr_out")
    z_mm, z_out, o_mm, o_out = K.sem("z_mm"), K.sem("z_out"), K.sem("nlo_mm"), K.sem("nlo_out")
    NF = 2 * B
    TAIL = {PC * (b + 1) + 1: b for b in range(B)}
    STEPS = B * PC + 2
    with nc.Block() as block:
        @block.tensor
        def _(pe):
            pe.wait_ge(w_in, 80)
            for i in range(NF):
                b, k = divmod(i, 2)
                if i >= 2:
                    pe.wait_ge(fg_low, i - 1)
                for t in range(NT):
                    for c in range(CC):
                        last = nc.tensor.matmul(sps[i % 2][:, t * BANK:(t + 1) * BANK], (wf, wg)[k][:, c],
                                                K.X[:, c, b, t * BANK:(t + 1) * BANK], start=(c == 0), stop=(c == CC - 1))
                last.then_inc(fg_mm, 1)
            for i in range(B * PC // 4):
                if i >= 2:
                    pe.wait_ge(h_out, i - 1)
                for r in range(4):
                    b, s = divmod(4 * i + r, PC)
                    for c in range(CC):
                        last = nc.tensor.matmul(zps[i % 2][:, r * MID:(r + 1) * MID], K.X[:, c, b, s * P:(s + 1) * P], wh[:, c],
                                                start=(c == 0), stop=(c == CC - 1))
                last.then_inc(h_mm, 1)
            pe.wait_ge(fg_low, NF)
            pe.wait_ge(h_out, B * PC // 4)

            def scores(n):
                b, s = divmod(n, PC)
                if n >= 2:
                    pe.wait_ge(exd, n - 1)
                for t in range(NT):
                    for k, (x, y) in enumerate(PAIRS):
                        last = nc.tensor.matmul(sps[n % 2][:, t * BANK:(t + 1) * BANK], fg[0][x][:, b, s * P:(s + 1) * P],
                                                fg[1][y][:, b, t * BANK:(t + 1) * BANK], start=(k == 0), stop=(k == 2))
                last.then_inc(s_mm, 1)

            def turn(n):
                pe.wait_ge(sts, 2 * n + 2)
                if n >= 1:
                    pe.wait_ge(t_out, n)
                for m in range(PC):
                    last = nc.tensor.transpose(tps[:, m * P:(m + 1) * P], ex[n % 3][:, m * P:(m + 1) * P], K.k("ident"))
                last.then_inc(t_mm, 1)

            def weigh(b):
                pe.wait_ge(t_out, PC * (b + 1))
                for t in range(NT):
                    if b:
                        pe.wait_ge(o_out, b * NT * CC - NT + t + 1)
                    for m in range(PC):
                        last = nc.tensor.matmul(zps[t][:], hT[:, b * PC + m], eT[:, m, t * BANK:(t + 1) * BANK],
                                                start=(m == 0), stop=(m == PC - 1))
                    last.then_inc(z_mm, 1)
                for i in range(NT * CC):
                    t, o = divmod(i, CC)
                    k = b * NT * CC + i
                    pe.wait_ge(z_out, b * NT + max(t, i % 2) + 1)
                    if i >= 2:
                        pe.wait_ge(o_out, k - 1)
                    nc.tensor.matmul(zps[i % 2][:], wv[:, o * P:(o + 1) * P], z[:, t * BANK:(t + 1) * BANK],
                                     start=True, stop=True).then_inc(o_mm, 1)

            for k in range(STEPS):
                if k < B * PC:
                    scores(k)
                if k >= 2:
                    turn(k - 2)
                if k in TAIL:
                    weigh(TAIL[k])

        @block.vector
        def _(dve):
            dve.wait_ge(cs, 1)
            n = 0
            nc.vector.reciprocal(bi[:], sc[:]).then_inc(cf, 1)
            dve.wait_ge(cf, 1)
            for k, (g, cb, be, me) in enumerate((("gf", "bf", "betaf", "mf"), ("gg", "bg", "betag", "mg"))):
                n = 1 + 4 * k
                col = slice(k, k + 1)
                nc.vector.tensor_tensor(sc[:, col], bi[:, col], K.v(g), ALU.mult).then_inc(cf, 1)
                dve.wait_ge(cf, n + 1)
                nc.vector.tensor_tensor(bi[:, col], K.v(cb), K.v(me), ALU.subtract).then_inc(cf, 1)
                dve.wait_ge(cf, n + 2)
                nc.vector.tensor_tensor(bi[:, col], bi[:, col], sc[:, col], ALU.mult).then_inc(cf, 1)
                dve.wait_ge(cf, n + 3)
                nc.vector.tensor_tensor(bi[:, col], bi[:, col], K.v(be), ALU.add).then_inc(cf, 1)
                dve.wait_ge(cf, n + 4)
            for i in range(NF):
                b, k = divmod(i, 2)
                dve.wait_ge(fg_out, i + 1)
                nc.vector.tensor_tensor(fg[k][1][:, b], sps[i % 2][:], fg[k][0][:, b].bitcast(F32), ALU.subtract).then_inc(fg_low, 1)
            dve.wait_ge(w_in, 80)
            for i in range(B * PC // 4):
                dve.wait_ge(h_mm, i + 1)
                nc.vector.tensor_tensor(hT[:, 4 * i:4 * i + 4], zps[i % 2][:].rearrange("p (r m) -> p r m", r=4),
                                        bhr[:].unsqueeze(1).to_broadcast([P, 4, MID]), ALU.add).then_inc(h_out, 1)

            def peak(n):
                dve.wait_ge(s_mm, n + 1)
                nc.vector.tensor_reduce(rs[:, n:n + 1], sps[n % 2][:], AX.X, ALU.max).then_inc(mxd, 1)
                dve.wait_ge(mxd, 2 * n + 1)
                nc.vector.tensor_scalar(nm[:, n:n + 1], rs[:, n:n + 1], -SC, None, ALU.mult).then_inc(mxd, 1)

            def norm(n):
                dve.wait_ge(exd, n + 1)
                nc.vector.reciprocal(rs[:, n:n + 1], sm[:, n:n + 1]).then_inc(sts, 1)
                dve.wait_ge(sts, 2 * n + 1)
                nc.vector.tensor_scalar(ex[n % 3], ex[n % 3], rs[:, n:n + 1], None, ALU.mult).then_inc(sts, 1)

            def project(b):
                for i in range(NT * CC):
                    t, o = divmod(i, CC)
                    x = K.X[:, o, b, t * BANK:(t + 1) * BANK]
                    dve.wait_ge(o_mm, b * NT * CC + i + 1)
                    nc.vector.scalar_tensor_tensor(x, zps[i % 2][:], K.v("bv2", o), x, ALU.add, ALU.add).then_inc(o_out, 1)

            for k in range(STEPS):
                if k < B * PC:
                    peak(k)
                if 1 <= k <= B * PC:
                    norm(k - 1)
                if k in TAIL:
                    project(TAIL[k])

        @block.scalar
        def _(act):
            act.wait_ge(K.eps_ready, 1)
            nc.scalar.activation(sc[:, 1:2], K.v("vg"), ACT.Sqrt, bias=K.eps[:])
            nc.scalar.activation(sc[:, 0:1], K.v("vf"), ACT.Sqrt, bias=K.eps[:]).then_inc(cs, 1)
            act.wait_ge(cf, 9)
            for i in range(NF):
                b, k = divmod(i, 2)
                act.wait_ge(fg_mm, i + 1)
                nc.scalar.activation(fg[k][0][:, b], sps[i % 2][:], ACT.Relu, bias=bi[:, k:k + 1], scale=sc[:, k:k + 1])
                nc.scalar.activation(sps[i % 2][:], sps[i % 2][:], ACT.Relu, bias=bi[:, k:k + 1], scale=sc[:, k:k + 1]).then_inc(fg_out, 1)

            def exps(n):
                act.wait_ge(mxd, 2 * n + 2)
                if n >= 3:
                    act.wait_ge(t_mm, n - 2)
                nc.scalar.activation(ex[n % 3], sps[n % 2][:], ACT.Exp, bias=nm[:, n:n + 1], scale=SC,
                                     accum_out=sm[:, n:n + 1]).then_inc(exd, 1)

            for k in range(STEPS):
                if k >= 2:
                    b, s = divmod(k - 2, PC)
                    act.wait_ge(t_mm, k - 1)
                    if b and s == 0:
                        act.wait_ge(z_mm, NT * b)
                    nc.scalar.activation(eT[:, :, s * P:(s + 1) * P], tps[:].rearrange("p (m n) -> p m n", m=PC), ACT.Copy).then_inc(t_out, 1)
                if k < B * PC:
                    exps(k)
                if k in TAIL:
                    b = TAIL[k]
                    for t in range(NT):
                        act.wait_ge(z_mm, b * NT + t + 1)
                        if b:
                            act.wait_ge(o_mm, b * NT * CC)
                        nc.scalar.activation(z[:, t * BANK:(t + 1) * BANK], zps[t][:], ACT.Copy).then_inc(z_out, 1)


def stage_rank_one(K, sb, ps):
    nc = K.nc
    d = K.dram
    se1, se2 = K.se1, K.se2
    room = carver(K.WR)
    EB = 8
    rep = room([P, 2, B, HW])
    e = [room([P, HW]) for _ in range(EB)]
    rows = room([P, BANK])
    out = [carver(K.Q)([P, CC * B, HW])[:, i] for i in range(CC * B)]
    gw = sb("gtp_w32", [P, CC, 32])
    sel = sb("row_select", [P, 2, B * NT, P])
    th = sb("theta", [P, B * PC])
    av, mid, gate = sb("avg", [P, CC, B]), sb("se_mid", [SE, B]), sb("gate", [P, CC, B])
    inv, t1, ga, gd = sb("bn3_inv", [P, CC]), sb("bn3_t", [P, CC]), sb("ga", [P, CC, B]), sb("gd", [P, CC, B])
    pm = sb("phi_ext", [P, B, 2])
    m1, m2 = sb("m1", [P, B, PC]), sb("m2", [P, B, PC])
    den, num, y = sb("r1_den", [P, B * PC]), sb("r1_num", [P, B * PC]), sb("r1_y", [P, B * PC])
    ones, dg = sb("ones", [P, P]), [room([P, P]) for _ in range(PC)]
    gps = ps("gtp_ps", [P, BANK])
    small = ps("small_ps", [P, BANK])
    aps, mps = small[:, 0:BLK].rearrange("p (c b) -> p c b", b=B), small[0:SE, P:P + B]
    rps = [ps(f"rep_ps{i}", [P, BANK]) for i in range(2)]
    yps = ps("yrep_ps", [P, B, HW])
    padded, w_pad, avd, av_act, g_mm, g_out, th_mm, th_out = (
        K.sem("pad_zeroed"), K.sem("gtp_w_padded"), K.sem("avg_dve"), K.sem("avg_act"), K.sem("gtp_mm"), K.sem("gtp_out"),
        K.sem("theta_mm"), K.sem("theta_out"))
    av_d, sel_done, rep_mm, rep_out = K.sem("avg_done"), K.sem("select_done"), K.sem("rep_mm"), K.sem("rep_out")
    se, sx, sq, st, ex = K.sem("se_mm"), K.sem("se_act"), K.sem("bn3_sqrt"), K.sem("r1_step"), K.sem("r1_exp")
    bound, coef, xg, nd, yd = K.sem("r1_bound"), K.sem("r1_coef"), K.sem("x_shifted"), K.sem("r1_sum"), K.sem("r1_quotient")
    ydg, y_mm, o_st, o_out = K.sem("r1_diag"), K.sem("r1_mm"), K.sem("out_stored"), K.sem("out_sum")
    af, o_first = K.sem("r1_affine"), K.sem("out_sum_first")
    ones_done = K.sem("ones_done")
    TILES = [(c, b) for b in range(B) for c in range(CC)]
    AV_DVE = CC * B // 2
    with nc.Block() as block:
        @block.sync
        def _(sp):
            for n, (c, b) in enumerate(TILES):
                sp.wait_ge(o_out if b else o_first, c + 1)
                sp.dma_start(d["out"][b, c * P:(c + 1) * P, :], out[n]).then_inc(o_st, 16)
            sp.wait_ge(o_st, 16 * CC * B)

        @block.gpsimd
        def _(pool):
            nc.gpsimd.memset(gw[:], 0.0).then_inc(padded, 1)
            for k, row in enumerate((2, 0)):
                for n in range(B * NT):
                    nc.gpsimd.tensor_copy(sel[:, k, n], K.k("ident", 32 * n + row, 1).to_broadcast([P, P])).then_inc(sel_done, 1)
            nc.gpsimd.memset(ones[:], 1.0).then_inc(ones_done, 1)
            pool.wait_ge(coef, 8)
            for c in range(CC):
                nc.gpsimd.tensor_scalar(K.X[:, c, 1], K.X[:, c, 1], gd[:, c, 1:2], None, ALU.add).then_inc(xg, 1)
            for c in range(CC):
                pool.wait_ge(af, c + 1)
                nc.gpsimd.tensor_tensor(out[c], out[c], K.X[:, c, 0], ALU.add).then_inc(o_first, 1)

        @block.tensor
        def _(pe):
            pe.wait_ge(w_pad, 1)
            for c in range(CC):
                for n in range(B * NT):
                    b, t = divmod(n, NT)
                    last = nc.tensor.matmul(gps[32 * n:32 * n + 32, :], gw[:, c], K.X[:, c, b, t * BANK:(t + 1) * BANK],
                                            start=(c == 0), stop=(c == CC - 1), tile_position=(0, 32 * n))
            last.then_inc(g_mm, 1)
            pe.wait_ge(g_out, 1)
            for r in range(BANK // P):
                last = nc.tensor.transpose(gps[:, r * P:(r + 1) * P], rows[:, r * P:(r + 1) * P], K.k("ident"))
            last.then_inc(th_mm, 1)
            pe.wait_ge(sel_done, 2 * B * NT)
            for i in range(2 * B * NT):
                b, r = divmod(i, 2 * NT)
                k, t = divmod(r, NT)
                if i >= 2:
                    pe.wait_ge(rep_out, i - 1)
                nc.tensor.matmul(rps[i % 2][:], sel[:, k, b * NT + t], rows, start=True, stop=True).then_inc(rep_mm, 1)
                if i == 2 * NT - 1:
                    pe.wait_ge(K.se_in, 32)
                    pe.wait_ge(av_d, 1)
                    for c in range(CC):
                        last = nc.tensor.matmul(mps, se1[:, c], av[:, c], start=(c == 0), stop=(c == CC - 1))
                    last.then_inc(se, 1)
            pe.wait_ge(sx, 1)
            for c in range(CC):
                last = nc.tensor.matmul(aps[:, c], se2[:, c * P:(c + 1) * P], mid[:], start=True, stop=True)
            last.then_inc(se, 1)
            pe.wait_ge(ones_done, 1)
            for n in range(B * PC):
                b, s = divmod(n, PC)
                pe.wait_ge(ydg, n + 1)
                nc.tensor.matmul(yps[:, b, s * P:(s + 1) * P], ones[:], dg[n % PC], start=True, stop=True).then_inc(y_mm, 1)

        @block.vector
        def _(dve):
            dve.wait_ge(padded, 1)
            nc.vector.tensor_copy(gw[:, :, 0:3], K.v("gtp_w", 0, 3 * CC).rearrange("p (c k) -> p c k", k=3)).then_inc(w_pad, 1)
            nc.vector.tensor_reduce(av[:, 0:CC // 2], K.X[:, 0:CC // 2], AX.X, ALU.add).then_inc(avd, 1)
            dve.wait_ge(avd, 1)
            dve.wait_ge(av_act, 1)
            nc.vector.tensor_scalar(av[:], av[:], 1.0 / HW, None, ALU.mult).then_inc(av_d, 1)
            dve.wait_ge(th_mm, 1)
            nc.vector.tensor_copy(th[:].rearrange("p (n r) -> p r n", n=B * NT),
                                  gps[:].rearrange("p (r n k) -> p r n k", r=BANK // P, k=32)[:, :, :, 1]).then_inc(th_out, 1)
            dve.wait_ge(th_out, 1)

            def limits(b):
                phi, t, k = rep[:, 0, b], th[:, b * PC:(b + 1) * PC], 6 * b
                dve.wait_ge(rep_out, 2 * NT * b + NT)
                nc.vector.tensor_reduce(pm[:, b, 0:1], phi, AX.X, ALU.max).then_inc(bound, 1)
                nc.vector.tensor_reduce(pm[:, b, 1:2], phi, AX.X, ALU.min).then_inc(bound, 1)
                dve.wait_ge(bound, k + 2)
                nc.vector.tensor_scalar(m1[:, b], t, pm[:, b, 0:1], None, ALU.mult).then_inc(bound, 1)
                nc.vector.tensor_scalar(m2[:, b], t, pm[:, b, 1:2], None, ALU.mult).then_inc(bound, 1)
                dve.wait_ge(bound, k + 4)
                nc.vector.tensor_tensor(m1[:, b], m1[:, b], m2[:, b], ALU.max).then_inc(bound, 1)
                dve.wait_ge(bound, k + 5)
                nc.vector.tensor_scalar(m2[:, b], m1[:, b], -1.0, None, ALU.mult).then_inc(bound, 1)

            def gate_coefficients():
                dve.wait_ge(sq, 1)
                dve.wait_ge(sx, 2)
                nc.vector.reciprocal(t1[:], inv[:]).then_inc(coef, 1)
                dve.wait_ge(coef, 1)
                nc.vector.tensor_tensor(inv[:], t1[:], K.v("bn_gamma", 0, CC), ALU.mult).then_inc(coef, 1)
                dve.wait_ge(coef, 2)
                nc.vector.tensor_tensor(t1[:], K.v("W_b", 0, CC), K.v("bn_mean", 0, CC), ALU.subtract).then_inc(coef, 1)
                dve.wait_ge(coef, 3)
                nc.vector.tensor_tensor(t1[:], t1[:], inv[:], ALU.mult).then_inc(coef, 1)
                dve.wait_ge(coef, 4)
                nc.vector.tensor_tensor(t1[:], t1[:], K.v("bn_beta", 0, CC), ALU.add).then_inc(coef, 1)
                nc.vector.tensor_tensor(inv[:], inv[:], K.v("W_w", 0, CC), ALU.mult).then_inc(coef, 1)
                dve.wait_ge(coef, 6)
                nc.vector.tensor_tensor(ga[:], gate[:], inv[:].unsqueeze(2).to_broadcast([P, CC, B]), ALU.mult).then_inc(coef, 1)
                nc.vector.tensor_tensor(gd[:], gate[:], t1[:].unsqueeze(2).to_broadcast([P, CC, B]), ALU.mult).then_inc(coef, 1)

            def sums(b):
                for n in range(b * PC, (b + 1) * PC):
                    dve.wait_ge(ex, n + 1)
                    nc.vector.tensor_tensor_reduce(e[n % EB], e[n % EB], rep[:, 1, b], 1.0, 0.0, ALU.mult, ALU.add,
                                                   num[:, n:n + 1]).then_inc(nd, 1)

            def finish(b):
                part = slice(b * PC, (b + 1) * PC)
                dve.wait_ge(nd, (b + 1) * PC)
                nc.vector.reciprocal(y[:, part], den[:, part]).then_inc(yd, 1)
                dve.wait_ge(yd, 2 * b + 1)
                nc.vector.tensor_tensor(y[:, part], y[:, part], num[:, part], ALU.mult).then_inc(yd, 1)
                dve.wait_ge(yd, 2 * b + 2)
                for n in range(b * PC, (b + 1) * PC):
                    if n >= PC:
                        dve.wait_ge(y_mm, n - PC + 1)
                    nc.vector.tensor_scalar(dg[n % PC], K.k("ident"), y[:, n:n + 1], None, ALU.mult).then_inc(ydg, 1)

            limits(0)
            limits(1)
            gate_coefficients()
            sums(0)
            finish(0)
            sums(1)
            finish(1)
            dve.wait_ge(y_mm, B * PC)
            for c in range(CC):
                dve.wait_ge(xg, c + 1)
                nc.vector.scalar_tensor_tensor(out[CC + c], yps[:, 1], ga[:, c, 1:2], K.X[:, c, 1],
                                               ALU.mult, ALU.add).then_inc(o_out, 1)

        @block.scalar
        def _(act):
            nc.scalar.activation(inv[:], K.v("bn_var", 0, CC), ACT.Sqrt, bias=K.eps[:]).then_inc(sq, 1)
            for i in range(CC * B // 2, CC * B):
                c, b = divmod(i, B)
                last = nc.scalar.activation(out[i], K.X[:, c, b], ACT.Copy, accum_out=av[:, c, b:b + 1])
            last.then_inc(av_act, 1)
            act.wait_ge(g_mm, 1)
            nc.scalar.activation(rows, gps[:], ACT.Identity, bias=K.v("gtp_b")).then_inc(g_out, 1)
            for i in range(2 * B * NT):
                b, r = divmod(i, 2 * NT)
                k, t = divmod(r, NT)
                act.wait_ge(rep_mm, i + 1)
                nc.scalar.activation(rep[:, k, b, t * BANK:(t + 1) * BANK], rps[i % 2][:], ACT.Copy).then_inc(rep_out, 1)
            act.wait_ge(se, 1)
            nc.scalar.activation(mid[:], mps, ACT.Relu, bias=K.v("se1_b", p1=SE)).then_inc(sx, 1)
            act.wait_ge(se, 2)
            for c in range(CC):
                last = nc.scalar.activation(gate[:, c], aps[:, c], ACT.Sigmoid, bias=K.v("se2_b", c))
            last.then_inc(sx, 1)
            for n in range(B * PC):
                b, s = divmod(n, PC)
                act.wait_ge(bound, 6 * (b + 1))
                if n >= EB:
                    act.wait_ge(nd, n - EB + 1)
                nc.scalar.activation(e[n % EB], rep[:, 0, b], ACT.Exp, bias=m2[:, b, s:s + 1], scale=th[:, n:n + 1],
                                     accum_out=den[:, n:n + 1]).then_inc(ex, 1)
                if n >= B * PC - CC:
                    c = n - (B * PC - CC)
                    act.wait_ge(y_mm, PC)
                    nc.scalar.activation(out[c], yps[:, 0], ACT.Identity, bias=gd[:, c, 0:1], scale=ga[:, c, 0:1]).then_inc(af, 1)


def build(nc, dram):
    with ExitStack() as ctx:
        K = Kit(nc, ctx, dram)
        sb, _ = tensors(nc, ctx)
        K.vecs, K.consts = sb("vecs", [P, VN]), sb("consts_sb", [P, KN])
        K.eps = sb("eps", [P, 1])
        K.X = sb("X", [P, CC, B, HW])
        K.W1R = sb("W1R", [32 + ROWS, BIASF], F32R)
        K.W2H, K.W2L = sb("W2H", [P, BIASF], F32R), sb("W2L", [P, BIASF], F32R)
        K.W3 = sb("W3", [P, 32])
        K.dx = nc.dram_tensor("x_table", (BG, 2, W, J), F32).ap()
        K.dy = nc.dram_tensor("y_table", (BG * H // 2, 2, 2, J), F32).ap()
        K.db = nc.dram_tensor("bias_scratch", (BG * H // 2, 2, 4, BANK), F32).ap()
        K.db_bg = K.db.rearrange("c q g n -> (c q g n)").rearrange("(g i j) -> g i j", g=BG, j=J)
        K.eps_ready = K.sem("eps_ready")
        with nc.Block() as block:
            @block.vector
            def _(dve):
                nc.vector.memset(K.eps[:], EPS).then_inc(K.eps_ready, 1)
        with ExitStack() as l0:
            sb0, _ = tensors(nc, l0)
            K.Q, K.w_hi2 = place(nc, sb0, "Q", [P, BLK, HW], [P, FC // 2, 2, C])
            K.KVBD, hid01 = place(nc, sb0, "KV_diag", [P, 2, BLK, P], [P, CC, BANK])
            K.KBD, K.VBD = K.KVBD[:, 0], K.KVBD[:, 1]
            with ExitStack() as front:
                with ExitStack() as s:
                    sbf, _ = tensors(nc, front)
                    stage_front(K, sbf, tensors(nc, s)[1])
                with ExitStack() as s:
                    stage_samples(K, *tensors(nc, s))
            with ExitStack() as s:
                sb1, _ = tensors(nc, s)
                K.WR, K.w_lo = place(nc, sb1, "mlp_w", [P, FC, 2, C])
                K.mlp_in = K.sem("mlp_w_loaded")
                with ExitStack() as s2:
                    stage_bias(K, *tensors(nc, s2))
                K.HA, K.w_hi = place(nc, sb1, "mlp_w_hi", [P, FC // 2, 2, C])
                K.s2 = sb1("s2", [P, CC])
                K.XNA, xn2_a = place(nc, sb1, "xn2_a", [P, 2, CC, BANK])
                with ExitStack() as s2:
                    sb2, _ = tensors(nc, s2)
                    K.XNB, xn2_b = place(nc, sb2, "xn2_b", [P, 2, CC, BANK])
                    K.xn2 = [(t[:, 0], t[:, 1]) for t in (xn2_a, xn2_b)]
                    K.ow_hi, K.ow_lo = K.w_hi[:, W_FIRST:W_FIRST + 2].rearrange("p f a o -> p (f a) o"), xn2_b[:, 0]
                    ao, ao_lo = K.Q[:].rearrange("p (c b) n -> p c b n", b=B), K.w_hi2[:].rearrange("p (c b) h o -> p c b (h o)", b=B)
                    ao_hi = (xn2_b[:, 1], hid01[:])
                    K.ao = lambda n: ao[:, :, n // NT, n % NT * BANK:(n % NT + 1) * BANK]
                    K.ao_lo = lambda n: ao_lo[:, :, n // NT, n % NT * BANK:(n % NT + 1) * BANK]
                    K.ao_hi = lambda n: ao_hi[n % 2]
                    K.ow_split, K.ao_high, K.ao_low = K.sem("out_w_split"), K.sem("att_high"), K.sem("att_low")
                    for stage in (stage_attention, stage_out_proj):
                        with ExitStack() as s3:
                            stage(K, *tensors(nc, s3))
                    K.hid = [hid01[:, 0:2], hid01[:, 2:4], sb2("hidden", [P, 2, BANK], F32R)]
                    with ExitStack() as s3:
                        stage_mlp(K, *tensors(nc, s3))
                room = carver(K.KVBD)
                K.fgh_w = [room([P, CC, MID]) for _ in range(3)]
                K.nl_wv, K.bhr = room([P, C]), sb1("bh_rep", [P, MID])
                K.se1, K.se2 = sb1("se1", [P, CC, SE]), sb1("se2", [SE, C])
                K.nl_in, K.se_in = K.sem("l2_w_loaded"), K.sem("l3_w_loaded")
                for stage in (stage_linear, stage_nonlocal, stage_rank_one):
                    with ExitStack() as s2:
                        stage(K, *tensors(nc, s2))


def constants():
    j, p = np.arange(J), np.arange(P)
    k = np.zeros((P, KN), np.float32)

    def put(name, a):
        o, w = KCOL[name]
        k[:, o:o + w] = a

    put("pixel_x", ((j % WD) * (W / (WD - 1)) - 0.5)[None])
    put("pixel_y", ((j // WD) * (H / (HD - 1)) - 0.5)[None])
    put("grid_nt", np.where((p // BG % 2 == 0)[:, None], (j % WD)[None], (j // WD)[None]))
    put("neg_ix", -(p % W)[:, None])
    put("neg_iy", -(np.arange(PC)[None] * (P // W) + (p // W)[:, None]))
    gq = np.float32(2.0) * np.arange(W, dtype=np.float32) / np.float32(W - 1) - np.float32(1.0)
    put("grid_q", gq.reshape(-1, ROWQ)[p // (2 * BG)])
    put("mask_hi", np.isin(p, (0, 1, 4, 5, 8)).astype(np.float32)[:, None])
    put("mask_lo", np.isin(p, (2, 3, 6, 7, 9)).astype(np.float32)[:, None])
    put("ident", np.eye(P, dtype=np.float32))
    return k


def lay_out(a):
    def chunks(v):
        return v.reshape(-1, P).T

    def pad(v):
        return np.concatenate([v, np.zeros(P - v.shape[0], v.dtype)])[:, None]

    def in_rows(w):
        return np.ascontiguousarray(w.T.reshape(-1, P, w.shape[0]).transpose(1, 0, 2))

    def rep(v, n=P):
        return np.broadcast_to(v.reshape(1, 1), (n, 1))

    L0, L1, L2, L3 = ({k[8:]: v for k, v in a.items() if k.startswith(f"L{i}_conv_")} for i in range(4))
    vec = {
        "bn1_g": chunks(L0["bn1_g"]), "bn1_b": chunks(L0["bn1_b"]), "bn2_g": chunks(L0["bn2_g"]), "bn2_b": chunks(L0["bn2_b"]),
        "out_b": chunks(L0["out_b"]), "dw_w": np.concatenate([L0["off_dw_w"].reshape(DH, -1)] * HALF),
        "dw_b": np.concatenate([L0["off_dw_b"]] * HALF)[:, None], "pw": np.concatenate([L0["off_pw_w"].T] * HALF),
        "cpb_b2": L0["cpb_b2"][:, None], "cpb_b3": rep(L0["cpb_b3"]), "cpb_w3": L0["cpb_w3"],
        "mlp_b1": chunks(L0["mlp_b1"]), "mlp_b2": chunks(L0["mlp_b2"]),
        "bk": chunks(L1["bk"]), "bo": chunks(L1["bo"]), "gamma": chunks(L1["gamma"]), "beta": chunks(L1["beta"]),
        "bv2": chunks(L2["bv"]),
        "gtp_w": np.stack([L3["g_w"][0], L3["theta_w"][0], L3["phi_w"][0]], 1).reshape(CC, P, 3).transpose(1, 0, 2).reshape(P, 3 * CC),
        "gtp_b": np.concatenate([np.pad(np.concatenate([L3["g_b"], L3["theta_b"], L3["phi_b"]]), (0, 29))] * (B * NT))[:, None],
        "W_w": chunks(L3["W_w"].reshape(-1)), "W_b": chunks(L3["W_b"]),
        "bn_gamma": chunks(L3["bn_gamma"]), "bn_beta": chunks(L3["bn_beta"]), "bn_mean": chunks(L3["bn_mean"]),
        "bn_var": chunks(L3["bn_var"]), "se1_b": pad(L3["se1_b"]), "se2_b": chunks(L3["se2_b"]),
    }
    for n in ("bf", "gf", "betaf", "mf", "vf", "bg", "gg", "betag", "mg", "vg"):
        vec[n] = L2[n][:, None]

    def per_group(w):
        return np.ascontiguousarray(w.reshape(CC, HALF, DH, DH).transpose(1, 3, 0, 2).reshape(P, CC, DH))

    w1, b1 = L0["cpb_w1"], L0["cpb_b1"]
    return {
        "x": a["x"].reshape(B, C, HW),
        "vecs": np.concatenate([vec[n] for n, _ in _WIDTHS], 1), "consts": constants(),
        "qwT": per_group(L0["qw"]), "kwT": per_group(L0["kw"]), "vwT": per_group(L0["vw"]),
        "cpb_w1r": np.stack([w1[0]] * 4 + [w1[1]] * 4 + [b1] * 2), "cpb_w2": L0["cpb_w2"],
        "out_wT": in_rows(L0["out_w"]),
        "mlp_w": np.stack([in_rows(L0["mlp_w1"]).reshape(P, CC, FC, P).transpose(0, 2, 1, 3).reshape(P, FC, C), in_rows(L0["mlp_w2"])], 2),
        "WqT": in_rows(L1["Wq"]), "WvT": in_rows(L1["Wv"]), "Wk": in_rows(L1["Wk"].T), "WoT": in_rows(L1["Wo"]),
        "bq": L1["bq"], "bv": L1["bv"],
        "wfT": in_rows(L2["wf"]), "wgT": in_rows(L2["wg"]), "whT": in_rows(L2["wh"]), "wvT": np.ascontiguousarray(L2["wv"].T),
        "bh": L2["bh"], "se1_wT": in_rows(L3["se1_w"]), "se2_wT": np.ascontiguousarray(L3["se2_w"].T),
    }


def kernel(**inputs):
    import concourse.bacc as bacc
    from concourse.bass_utils import run_bass_kernel_spmd

    arrays = {n: np.ascontiguousarray(v) for n, v in lay_out({k: np.asarray(v) for k, v in inputs.items()}).items()}
    nc = bacc.Bacc("TRN2", target_bir_lowering=False, num_devices=1)
    dram = {n: nc.dram_tensor(f"in_{n}", v.shape, mybir.dt.from_np(v.dtype), kind="ExternalInput").ap() for n, v in arrays.items()}
    dram["out"] = nc.dram_tensor("out", (B, C, HW), F32, kind="ExternalOutput").ap()
    build(nc, dram)
    result = run_bass_kernel_spmd(nc, [{f"in_{n}": v for n, v in arrays.items()}], core_ids=[0])
    return result.results[0]["out"].reshape(B, C, H, W)
```
